# Optimizing a Trainium2 kernel written in Bass

```python
import numpy as np
import jax
import jax.numpy as jnp

def _softmax(x, axis=-1):
    return jax.nn.softmax(x, axis=axis)

def _gelu(x):
    return jax.nn.gelu(x, approximate=True)

def _silu(x):
    return jax.nn.silu(x)

def _sigmoid(x):
    return jax.nn.sigmoid(x)

def _layernorm(x, axis=-1, eps=1e-05):
    m = jnp.mean(x, axis=axis, keepdims=True)
    v = jnp.var(x, axis=axis, keepdims=True)
    return (x - m) / jnp.sqrt(v + eps)

def _scatter_add(tgt, idx, src, axis=0):
    return tgt.at[idx].add(src)

def _segment_sum(src, seg, n):
    return jax.ops.segment_sum(src, seg, n)
kernel_name = 'mk_seq_postln_d1_jaxref_r4_5e0984'

def setup_inputs(seed: int=0):
    np.random.seed(seed)
    _w = jnp.asarray

    def _L0_attn_setup():
        import jax, jax.numpy as jnp
        import numpy as np
        B, S, D_IN = (2, 512, 256)
        H, D_HEAD = (16, 64)
        key = jax.random.key(seed)
        k1, k2, k3 = jax.random.split(key, 3)
        x = jax.random.normal(k1, (B, S, D_IN), dtype=jnp.float32)
        kernel = jax.random.normal(k2, (3, H, D_IN, D_HEAD), dtype=jnp.float32) * np.float32(np.sqrt(2.0 / D_IN))
        WO = jax.random.normal(k3, (1, H * D_HEAD, D_IN), dtype=jnp.float32) * np.float32(np.sqrt(2.0 / (H * D_HEAD)))
        return {'x': x, 'kernel': kernel, 'WO': WO}
    _L0_attn_in = _L0_attn_setup()

    def _L0_ffn_setup():
        import jax, jax.numpy as jnp
        import numpy as np
        B, S, D, E, H, DO = (4, 512, 256, 8, 1024, 256)
        TOP_K = 2
        LN_EPS = 1e-05
        key = jax.random.key(seed)
        ks = jax.random.split(key, 9)
        s = 0.02
        return {'x': jax.random.normal(ks[0], (B, S, D), dtype=jnp.float32), 'W1': jax.random.normal(ks[1], (E, D, H), dtype=jnp.float32) * s, 'b1': jnp.zeros((E, H), dtype=jnp.float32), 'W2': jax.random.normal(ks[2], (E, H, DO), dtype=jnp.float32) * s, 'b2': jnp.zeros((E, DO), dtype=jnp.float32), 'gate_W': jax.random.normal(ks[3], (D, E), dtype=jnp.float32) * s, 'shared_W': jax.random.normal(ks[4], (D, DO), dtype=jnp.float32) * s, 'shared_b': jnp.zeros((DO,), dtype=jnp.float32), 'gamma': jnp.ones((DO,), dtype=jnp.float32), 'beta': jnp.zeros((DO,), dtype=jnp.float32)}
    _L0_ffn_in = _L0_ffn_setup()
    _d = {'L0_attn_x': _L0_attn_in['x'], 'L0_attn_kernel': _L0_attn_in['kernel'], 'L0_attn_WO': _L0_attn_in['WO'], 'L0_ffn_W1': _L0_ffn_in['W1'], 'L0_ffn_b1': _L0_ffn_in['b1'], 'L0_ffn_W2': _L0_ffn_in['W2'], 'L0_ffn_b2': _L0_ffn_in['b2'], 'L0_ffn_gate_W': _L0_ffn_in['gate_W'], 'L0_ffn_shared_W': _L0_ffn_in['shared_W'], 'L0_ffn_shared_b': _L0_ffn_in['shared_b'], 'L0_ffn_gamma': _L0_ffn_in['gamma'], 'L0_ffn_beta': _L0_ffn_in['beta']}
    _x0 = _d['L0_attn_x']
    _d['L0_attn_x'] = jax.random.normal(jax.random.fold_in(jax.random.key(seed), 1), (4, 1024, 256), dtype=_x0.dtype)
    del _x0
    return _d

def reference(L0_attn_x, L0_attn_kernel, L0_attn_WO, L0_ffn_W1, L0_ffn_b1, L0_ffn_W2, L0_ffn_b2, L0_ffn_gate_W, L0_ffn_shared_W, L0_ffn_shared_b, L0_ffn_gamma, L0_ffn_beta):

    def _L0_attn_ref(x, kernel, WO):
        import jax, jax.numpy as jnp
        import numpy as np
        B, S, D_IN = (2, 512, 256)
        H, D_HEAD = (16, 64)
        b, s, _ = x.shape
        h, d = (kernel.shape[1], kernel.shape[3])
        q = jnp.einsum('bsm,hmd->bhsd', x, kernel[0])
        k = jnp.einsum('bsm,hmd->bhsd', x, kernel[1])
        v = jnp.einsum('bsm,hmd->bhsd', x, kernel[2])
        scale = jnp.float32(1.0 / (d * d * h))
        scores = jnp.einsum('bhsd,bhtd->bhst', q, k) * scale
        attn = jax.nn.softmax(scores, axis=-1)
        out = jnp.einsum('bhst,bhtd->bhsd', attn, v)
        out = jnp.transpose(out, (0, 2, 3, 1)).reshape(b, s, d * h)
        out = jnp.einsum('bsf,fm->bsm', out, WO[0])
        return out

    def _L0_ffn_ref(x, W1, b1, W2, b2, gate_W, shared_W, shared_b, gamma, beta):
        import jax, jax.numpy as jnp
        import numpy as np
        B, S, D, E, H, DO = (4, 512, 256, 8, 1024, 256)
        TOP_K = 2
        LN_EPS = 1e-05
        d = x.shape[-1]
        flat = x.reshape(-1, d)
        n_exp = gate_W.shape[-1]
        probs = jax.nn.softmax(flat @ gate_W, axis=-1)
        topk_w, topk_idx = jax.lax.top_k(probs, TOP_K)
        topk_w = topk_w / topk_w.sum(axis=-1, keepdims=True)
        combine = (jax.nn.one_hot(topk_idx, n_exp, dtype=flat.dtype) * topk_w[..., None]).sum(axis=1)
        out = 0.5 * jax.nn.gelu(flat @ shared_W + shared_b, approximate=False)
        for e in range(n_exp):
            h = jax.nn.gelu(flat @ W1[e] + b1[e], approximate=False)
            out = out + combine[:, e:e + 1] * (h @ W2[e] + b2[e])
        mean = out.mean(axis=-1, keepdims=True)
        var = ((out - mean) ** 2).mean(axis=-1, keepdims=True)
        out = (out - mean) * jax.lax.rsqrt(var + LN_EPS) * gamma + beta
        return out.reshape(*x.shape[:-1], out.shape[-1])
    x = L0_attn_x
    x = _layernorm(x + _L0_attn_ref(x, L0_attn_kernel, L0_attn_WO), axis=-1)
    x = _layernorm(x + _L0_ffn_ref(x, L0_ffn_W1, L0_ffn_b1, L0_ffn_W2, L0_ffn_b2, L0_ffn_gate_W, L0_ffn_shared_W, L0_ffn_shared_b, L0_ffn_gamma, L0_ffn_beta), axis=-1)
    return x

_drawn_inputs = setup_inputs


def setup_inputs(seed=0):
    import zlib

    import numpy as np

    out = dict(_drawn_inputs(seed))
    spreads = {'L0_ffn_b1': (0.0, 0.1),
     'L0_ffn_b2': (0.0, 0.1),
     'L0_ffn_shared_b': (0.0, 0.1),
     'L0_ffn_gamma': (1.0, 0.2),
     'L0_ffn_beta': (0.0, 0.1)}
    factors = {}
    for name, (base, spread) in spreads.items():
        noise = np.random.default_rng([zlib.crc32(name.encode()), seed]).standard_normal(out[name].shape)
        drawn = base * np.exp(spread * noise) if base else spread * noise
        out[name] = jnp.asarray(drawn.astype(out[name].dtype))
    for name, factor in factors.items():
        out[name] = (out[name] * factor).astype(out[name].dtype)
    return out
```

```python
from contextlib import ExitStack

import concourse.bass as bass
from concourse import mybir

F32 = mybir.dt.float32
I32 = mybir.dt.int32
U32 = mybir.dt.uint32
ALU = mybir.AluOpType
ACT = mybir.ActivationFunctionType
AX = mybir.AxisListType

P = 128
B, S, D = 4, 1024, 256
H, DH = 16, 64
E, HID, TOPK = 8, 1024, 2
T = B * S
KD = D // P
PAIRS = H // 2
ST = S // P
TT = T // P
BANK = 512
NB = S // BANK
HB = HID // P
SCALE = 1.0 / (DH * DH * H)
EPS = 1e-5
CHUNK = 256
CT = CHUNK // P
NCHUNK = (TOPK * T + E * (CHUNK - 1)) // CHUNK
NCHUNK += NCHUNK % 2
SLOTS = NCHUNK * CHUNK
WX = KD * HID + HB * D + HB
NEVER = -3.0e38


def prime(engine, *semaphores):
    for semaphore in semaphores:
        engine.nop().then_inc(semaphore, 1)


def make_identity(gpsimd, tile, done):
    gpsimd.memset(tile[:, :], 0.0).then_inc(done, 1)
    gpsimd.wait_ge(done, 1)
    gpsimd.affine_select(out=tile[:, :], in_=tile[:, :], compare_op=ALU.not_equal, fill=1.0, base=0,
                         pattern=[[-1, P]], channel_multiplier=1).then_inc(done, 1)


def attention(nc, banks, x_t, w_qkv, attn_out):
    UNITS = 2 * ST
    with ExitStack() as ctx:
        def sb(name, shape, dt=F32):
            return ctx.enter_context(nc.sbuf_tensor(name, shape, dt))

        def sem(name):
            return ctx.enter_context(nc.semaphore(name))

        xt = sb("a_xt", [P, KD, T])
        w = sb("a_w", [P, KD, 3, P])
        q = sb("a_q", [DH, 2, S])
        k = sb("a_k", [DH, 2, S])
        vt = sb("a_vt", [P, S])
        v = sb("a_v", [P, ST, P])
        e = sb("a_e", [P, S])
        et = sb("a_et", [P, ST, P])
        ot = sb("a_ot", [P, S])
        top = sb("a_top", [P, 1])
        shift = sb("a_shift", [P, 1])
        total = sb("a_total", [P, 1])
        inv = sb("a_inv", [P, 1])
        ident = sb("a_ident", [P, P])
        scores, turned, misc, o_ps = banks[0:2], banks[2:4], banks[4:6], banks[6]

        x_in, w_in = sem("a_x_in"), sem("a_w_in")
        ident_ok = sem("a_ident_ok")
        qkv_done, qkv_evac = sem("a_qkv_done"), sem("a_qkv_evac")
        vt_turned, v_ready = sem("a_vt_turned"), sem("a_v_ready")
        s_done, top_ok, shift_ok, e_done = sem("a_s_done"), sem("a_top_ok"), sem("a_shift_ok"), sem("a_e_done")
        inv_ok, e_norm = sem("a_inv_ok"), sem("a_e_norm")
        et_done, et_evac = sem("a_et_done"), sem("a_et_evac")
        pv_done, o_evac, ot_out = sem("a_pv_done"), sem("a_o_evac"), sem("a_ot_out")
        stored = sem("a_stored")
        block = ctx.enter_context(nc.Block())

        @block.sync
        def _(sp):
            prime(sp, stored)
            sp.dma_start(xt[:, :, :], x_t).then_inc(x_in, 16)
            with sp.Fori(0, B) as b:
                with sp.Fori(0, PAIRS) as p:
                    i = b * PAIRS + p
                    sp.wait_ge(qkv_done, i * 6 + 1)
                    sp.dma_start(w[:, :, :, :], w_qkv[p]).then_inc(w_in, 16)
                    sp.wait_ge(o_evac, i * UNITS + UNITS + 1)
                    sp.dma_start(attn_out[i], ot[:, :]).then_inc(ot_out, 16)
                    sp.wait_ge(ot_out, 16 * i + 16)
                    sp.nop().then_inc(stored, 1)

        @block.gpsimd
        def _(gp):
            make_identity(gp, ident, ident_ok)

        @block.tensor
        def _(pe):
            prime(pe, qkv_done, vt_turned, s_done, et_done, pv_done)
            pe.wait_ge(ident_ok, 2)
            pe.wait_ge(x_in, 16)
            with pe.Fori(0, B) as b:
                with pe.Fori(0, PAIRS) as p:
                    i = b * PAIRS + p
                    pe.wait_ge(w_in, 16 * i + 16)
                    for c in range(6):
                        blk, n = c // NB, c % NB
                        pe.wait_ge(qkv_evac, i * 6 + max(c - 1, 0) + 1)
                        for kk in range(KD):
                            mm = pe.matmul(misc[c % 2][:, :], w[:, kk, blk, :],
                                           xt[:, kk, bass.ds(b * S + n * BANK, BANK)],
                                           start=kk == 0, stop=kk == KD - 1)
                        mm.then_inc(qkv_done, 1)
                    pe.wait_ge(qkv_evac, i * 6 + 6 + 1)
                    pe.wait_ge(et_evac, i * UNITS + 1)
                    for t in range(ST):
                        mm = pe.transpose(turned[t // 4][:, (t % 4) * P:(t % 4 + 1) * P],
                                          vt[:, t * P:(t + 1) * P], ident[:, :])
                    mm.then_inc(vt_turned, 1)
                    for h in range(2):
                        for st in range(ST):
                            g = i * UNITS + h * ST + st
                            pe.wait_ge(e_done, g + 1)
                            for n in range(NB):
                                mm = pe.matmul(scores[n][:, :], q[:, h, st * P:(st + 1) * P],
                                               k[:, h, n * BANK:(n + 1) * BANK], start=True, stop=True)
                            mm.then_inc(s_done, 1)
                            pe.wait_ge(e_norm, g + 1)
                            pe.wait_ge(v_ready, i + 1)
                            pe.wait_ge(et_evac, g + 1)
                            for t in range(ST):
                                mm = pe.transpose(turned[t // 4][:, (t % 4) * P:(t % 4 + 1) * P],
                                                  e[:, t * P:(t + 1) * P], ident[:, :])
                            mm.then_inc(et_done, 1)
                            pe.wait_ge(et_evac, g + 2)
                            pe.wait_ge(o_evac, g + 1)
                            for t in range(ST):
                                mm = pe.matmul(o_ps[h * DH:(h + 1) * DH, 0:P], v[:, t, h * DH:(h + 1) * DH],
                                               et[:, t, :], start=t == 0, stop=t == ST - 1)
                            mm.then_inc(pv_done, 1)

        @block.scalar
        def _(act):
            prime(act, qkv_evac, e_done, et_evac)
            with act.Fori(0, B) as b:
                with act.Fori(0, PAIRS) as p:
                    i = b * PAIRS + p
                    act.wait_ge(s_done, i * UNITS + 1)
                    for c in range(6):
                        blk, n = c // NB, c % NB
                        cols = slice(n * BANK, (n + 1) * BANK)
                        act.wait_ge(qkv_done, i * 6 + c + 2)
                        if blk < 2:
                            act.copy(q[:, blk, cols], misc[c % 2][0:DH, :])
                            act.copy(k[:, blk, cols], misc[c % 2][DH:P, :]).then_inc(qkv_evac, 1)
                        else:
                            act.wait_ge(vt_turned, i + 1)
                            act.copy(vt[:, cols], misc[c % 2][:, :]).then_inc(qkv_evac, 1)
                    for u in range(UNITS):
                        g = i * UNITS + u
                        act.wait_ge(shift_ok, g + 1)
                        act.wait_ge(et_done, g + 1)
                        act.activation(e[:, :], scores_all(banks), ACT.Exp, bias=shift[:, :], scale=SCALE,
                                       accum_out=total[:, :]).then_inc(e_done, 1)
                        act.wait_ge(et_done, g + 2)
                        act.wait_ge(pv_done, g + 1)
                        act.copy(et[:, :, :].rearrange("p a b -> p (a b)"), turned_all(banks)).then_inc(et_evac, 1)

        @block.vector
        def _(dve):
            prime(dve, o_evac)
            with dve.Fori(0, B) as b:
                with dve.Fori(0, PAIRS) as p:
                    i = b * PAIRS + p
                    dve.wait_ge(vt_turned, i + 2)
                    dve.wait_ge(pv_done, i * UNITS + 1)
                    dve.tensor_copy(v[:, :, :].rearrange("p a b -> p (a b)"), turned_all(banks)).then_inc(v_ready, 1)
                    for h in range(2):
                        for st in range(ST):
                            g = i * UNITS + h * ST + st
                            dve.wait_ge(s_done, g + 2)
                            dve.tensor_reduce(top[:, :], scores_all(banks), AX.X, ALU.max, negate=True)\
                               .then_inc(top_ok, 1)
                            dve.wait_ge(top_ok, g + 1)
                            dve.tensor_scalar(shift[:, :], top[:, :], SCALE, None, ALU.mult).then_inc(shift_ok, 1)
                            dve.wait_ge(e_done, g + 2)
                            dve.reciprocal(inv[:, :], total[:, :]).then_inc(inv_ok, 1)
                            dve.wait_ge(inv_ok, g + 1)
                            dve.tensor_scalar(e[:, :], e[:, :], inv[:, :], None, ALU.mult).then_inc(e_norm, 1)
                            dve.wait_ge(pv_done, g + 2)
                            dve.wait_ge(stored, i + 1)
                            dve.tensor_copy(ot[h * DH:(h + 1) * DH, st * P:(st + 1) * P],
                                            o_ps[h * DH:(h + 1) * DH, 0:P]).then_inc(o_evac, 1)


def tokens(nc, banks, keep, x_rows, attn_out, w_o, w_gs, shared_b):
    x2, shared, logits = keep["x2"], keep["shared"], keep["logits"]
    GS = D + E
    with ExitStack() as ctx:
        def sb(name, shape, dt=F32):
            return ctx.enter_context(nc.sbuf_tensor(name, shape, dt))

        def sem(name):
            return ctx.enter_context(nc.semaphore(name))

        ot = sb("t_ot", [P, 2, PAIRS, P])
        xr = sb("t_xr", [P, 2, D])
        wo = sb("t_wo", [P, PAIRS, D])
        wgs = sb("t_wgs", [P, KD, GS])
        sbias = sb("t_sbias", [P, D])
        stats = sb("t_stats", [P, TT, 6])
        mv = sb("t_mv", [P, TT, 2])
        var = sb("t_var", [P, TT])
        std = sb("t_std", [P, TT])
        rstd = sb("t_rstd", [P, TT])
        mean8 = sb("t_mean8", [P, ST])
        rstd8 = sb("t_rstd8", [P, ST])
        xn = sb("t_xn", [P, 2, D])
        x2t = sb("t_x2t", [P, 2, KD, P])
        pre = sb("t_pre", [P, 2, D])
        ident = sb("t_ident", [P, P])

        c_in, ident_ok = sem("t_c_in"), sem("t_ident_ok")
        ot_in = [sem(f"t_ot_in{u}") for u in range(2)]
        y_done, r_done = sem("t_y_done"), sem("t_r_done")
        stats_ok, mv_ok, var_ok = sem("t_stats_ok"), sem("t_mv_ok"), sem("t_var_ok")
        std_ok, rstd_ok = sem("t_std_ok"), sem("t_rstd_ok")
        m8_ok = sem("t_m8_ok")
        xn_ok, x2_ok, turned, x2t_ok, gs_done, pre_ok, sh_ok = (
            sem("t_" + n) for n in ("xn_ok", "x2_ok", "turned", "x2t_ok", "gs_done", "pre_ok", "sh_ok"))
        log_ok = sem("t_log_ok")
        block = ctx.enter_context(nc.Block())

        @block.sync
        def _(sp):
            sp.dma_start(wo[:, :, :], w_o).then_inc(c_in, 16)
            sp.dma_start(wgs[:, :, :], w_gs).then_inc(c_in, 16)
            sp.dma_start(sbias[:, :], shared_b.partition_broadcast(P)).then_inc(c_in, 16)
            with sp.Fori(0, B) as b:
                for st in range(ST):
                    u = st % 2
                    g = b * ST + st
                    if st >= 2:
                        sp.wait_ge(r_done, g + 0)
                    else:
                        sp.wait_ge(r_done, b * ST + 1)
                    sp.dma_start(ot[:, u, :, :], attn_out[bass.ds(b * PAIRS, PAIRS), :, st * P:(st + 1) * P]
                                 .rearrange("a p s -> p a s")).then_inc(ot_in[u], 16)
                    sp.dma_start(xr[:, u, :], x_rows[bass.ds(b * S + st * P, P), :]).then_inc(ot_in[u], 16)

        @block.gpsimd
        def _(gp):
            make_identity(gp, ident, ident_ok)

        @block.tensor
        def _(pe):
            prime(pe, turned)
            pe.wait_ge(c_in, 48)
            with pe.Fori(0, B) as b:
                for st in range(ST):
                    u = st % 2
                    g = b * ST + st
                    pe.wait_ge(ot_in[u], (b * (ST // 2) + st // 2 + 1) * 32)
                    if st >= 2:
                        pe.wait_ge(r_done, g + 0)
                    for a in range(PAIRS):
                        mm = pe.matmul(banks[u][:, 0:D], ot[:, u, a, :], wo[:, a, :], start=a == 0, stop=a == PAIRS - 1)
                    mm.then_inc(y_done, 1)
            pe.wait_ge(ident_ok, 2)
            with pe.Fori(0, B) as b:
                for st in range(ST):
                    u = st % 2
                    g = b * ST + st
                    pe.wait_ge(xn_ok, g + 2)
                    pe.wait_ge(x2t_ok, g + 1)
                    for kk in range(KD):
                        mm = pe.transpose(banks[2][:, kk * P:(kk + 1) * P], xn[:, u, kk * P:(kk + 1) * P], ident[:, :])
                    mm.then_inc(turned, 1)
                    pe.wait_ge(x2t_ok, g + 2)
                    pe.wait_ge(log_ok, g + 1)
                    for kk in range(KD):
                        mm = pe.matmul(banks[3][:, 0:GS], x2t[:, u, kk, :], wgs[:, kk, :], start=kk == 0, stop=kk == KD - 1)
                    mm.then_inc(gs_done, 1)

        @block.scalar
        def _(act):
            prime(act, x2_ok, x2t_ok, sh_ok)
            act.wait_ge(var_ok, 1)
            act.activation(std[:, :], var[:, :], ACT.Sqrt).then_inc(std_ok, 1)
            with act.Fori(0, B) as b:
                for st in range(ST):
                    u = st % 2
                    g = b * ST + st
                    act.wait_ge(xn_ok, g + 2)
                    act.copy(x2[:, bass.ds(g, 1), :].rearrange("p a d -> p (a d)"), xn[:, u, :]).then_inc(x2_ok, 1)
                    act.wait_ge(turned, g + 2)
                    act.copy(x2t[:, u, :, :].rearrange("p a b -> p (a b)"), banks[2][:, 0:D]).then_inc(x2t_ok, 1)
                    act.wait_ge(pre_ok, g + 1)
                    act.activation(shared[:, bass.ds(g, 1), :].rearrange("p a d -> p (a d)"), pre[:, u, :],
                                   ACT.Gelu).then_inc(sh_ok, 1)

        @block.vector
        def _(dve):
            prime(dve, r_done, log_ok, xn_ok)
            with dve.Fori(0, B) as b:
                for st in range(ST):
                    u = st % 2
                    g = b * ST + st
                    dve.wait_ge(y_done, g + 1)
                    dve.wait_ge(ot_in[u], (b * (ST // 2) + st // 2 + 1) * 32)
                    row = x2[:, bass.ds(g, 1), :].rearrange("p a d -> p (a d)")
                    dve.tensor_tensor(row, banks[u][:, 0:D], xr[:, u, :], ALU.add).then_inc(r_done, 1)
            dve.wait_ge(r_done, TT + 1)
            for t in range(TT):
                ins = dve.bn_stats(stats[:, t, :], x2[:, t, :])
            ins.then_inc(stats_ok, 1)
            dve.wait_ge(stats_ok, 1)
            for t in range(TT):
                ins = dve.bn_aggr(mv[:, t, :], stats[:, t, :])
            ins.then_inc(mv_ok, 1)
            dve.wait_ge(mv_ok, 1)
            dve.tensor_scalar(var[:, :], mv[:, :, 1], EPS, None, ALU.add).then_inc(var_ok, 1)
            dve.wait_ge(std_ok, 1)
            dve.reciprocal(rstd[:, :], std[:, :]).then_inc(rstd_ok, 1)
            dve.wait_ge(rstd_ok, 1)
            with dve.Fori(0, B) as b:
                dve.wait_ge(xn_ok, b * ST + 1)
                dve.tensor_copy(mean8[:, :], mv[:, bass.ds(b * ST, ST), 0]).then_inc(m8_ok, 1)
                dve.tensor_copy(rstd8[:, :], rstd[:, bass.ds(b * ST, ST)]).then_inc(m8_ok, 1)
                dve.wait_ge(m8_ok, b * 2 + 2)
                for st in range(ST):
                    u = st % 2
                    g = b * ST + st
                    if st >= 2:
                        dve.wait_ge(x2_ok, g + 0)
                        dve.wait_ge(turned, g + 0)
                    else:
                        dve.wait_ge(x2_ok, b * ST + 1)
                        dve.wait_ge(turned, b * ST + 1)
                    dve.tensor_scalar(xn[:, u, :], x2[:, bass.ds(g, 1), :].rearrange("p a d -> p (a d)"),
                                      mean8[:, st:st + 1], rstd8[:, st:st + 1], ALU.subtract, ALU.mult).then_inc(xn_ok, 1)
                    dve.wait_ge(gs_done, g + 1)
                    if st >= 2:
                        dve.wait_ge(sh_ok, g + 0)
                    else:
                        dve.wait_ge(sh_ok, b * ST + 1)
                    dve.tensor_tensor(pre[:, u, :], banks[3][:, 0:D], sbias[:, :], ALU.add).then_inc(pre_ok, 1)
                    dve.tensor_copy(logits[:, bass.ds(g, 1), :].rearrange("p a d -> p (a d)"),
                                    banks[3][:, D:GS]).then_inc(log_ok, 1)


def routing(nc, banks, keep):
    logits, w1, w2, slots, chunk_expert = (keep[n] for n in ("logits", "w1", "w2", "slots", "chunk_expert"))
    with ExitStack() as ctx:
        def sb(name, shape, dt=F32):
            return ctx.enter_context(nc.sbuf_tensor(name, shape, dt))

        def sem(name):
            return ctx.enter_context(nc.semaphore(name))

        first = sb("r_first", [P, E])
        best = [sb(f"r_best{j}", [P, TT]) for j in range(2)]
        eq = sb("r_eq", [P, TT, E])
        pref = sb("r_pref", [P, TT, E])
        ptop = sb("r_ptop", [P, TT])
        hot = [sb(f"r_hot{j}", [P, TT, E]) for j in range(2)]
        rest = sb("r_rest", [P, TT, E])
        gap = sb("r_gap", [P, TT])
        e2 = sb("r_e2", [P, TT])
        den = sb("r_den", [P, TT])
        chosen = sb("r_chosen", [P, TT, E])
        before = sb("r_before", [P, P])
        ones = sb("r_ones", [P, P])
        cnt = sb("r_cnt", [P, TT, E])
        run = [sb(f"r_run{j}", [P, TT, E]) for j in range(2)]
        nch = sb("r_nch", [P, E])
        ends = [sb(f"r_ends{j}", [P, E]) for j in range(2)]
        base = sb("r_base", [P, E])
        slot = sb("r_slot", [P, TT, E])
        pick = sb("r_pick", [P, TT, E])
        slotf = sb("r_slotf", [P, TT])
        cidx = sb("r_cidx", [1, NCHUNK, E])
        past = sb("r_past", [1, NCHUNK, E])
        cexp = sb("r_cexp", [1, NCHUNK])
        consts_ok, chain, m_ok, counted, gap_ok, e2_ok = (
            sem("r_" + n) for n in ("consts_ok", "chain", "m_ok", "counted", "gap_ok", "e2_ok"))
        block = ctx.enter_context(nc.Block())

        def over_experts(a):
            return a[:, :].unsqueeze(2).to_broadcast([P, TT, E])

        def over_tiles(a):
            return a[:, :].unsqueeze(1).to_broadcast([P, TT, E])

        @block.gpsimd
        def _(gp):
            gp.memset(ones[:, :], 1.0).then_inc(consts_ok, 1)
            gp.wait_ge(consts_ok, 1)
            gp.affine_select(out=before[:, :], in_=ones[:, :], compare_op=ALU.is_ge, fill=0.0, base=-1,
                             pattern=[[1, P]], channel_multiplier=-1).then_inc(consts_ok, 1)
            for e in range(E):
                gp.memset(first[:, e:e + 1], float(E - e)).then_inc(consts_ok, 1)
            for c in range(NCHUNK):
                gp.memset(cidx[:, c, :], float(c)).then_inc(consts_ok, 1)

        @block.tensor
        def _(pe):
            pe.wait_ge(m_ok, 1)
            flat = chosen[:, :, :].rearrange("p a b -> p (a b)")
            pe.matmul(banks[0][:, 0:TT * E], before[:, :], flat, start=True, stop=True)
            pe.matmul(banks[1][:, 0:TT * E], ones[:, :], flat, start=True, stop=True).then_inc(counted, 1)

        @block.scalar
        def _(act):
            act.wait_ge(gap_ok, 1)
            act.activation(e2[:, :], gap[:, :], ACT.Exp).then_inc(e2_ok, 1)

        @block.vector
        def _(dve):
            steps = [0]

            def link(ins):
                steps[0] += 1
                ins.then_inc(chain, 1)
                dve.wait_ge(chain, steps[0])

            dve.wait_ge(consts_ok, 2 + E + NCHUNK)
            left = logits
            for j in range(2):
                link(dve.tensor_reduce(best[j][:, :], left[:, :, :], AX.X, ALU.max))
                link(dve.tensor_tensor(eq[:, :, :], left[:, :, :], over_experts(best[j]), ALU.is_equal))
                link(dve.tensor_tensor(pref[:, :, :], eq[:, :, :], over_tiles(first), ALU.mult))
                link(dve.tensor_reduce(ptop[:, :], pref[:, :, :], AX.X, ALU.max))
                link(dve.tensor_tensor(hot[j][:, :, :], pref[:, :, :], over_experts(ptop), ALU.is_equal))
                if j == 0:
                    link(dve.scalar_tensor_tensor(rest[:, :, :], hot[0][:, :, :], NEVER, logits[:, :, :],
                                                  ALU.mult, ALU.add))
                    left = rest
            dve.tensor_tensor(gap[:, :], best[1][:, :], best[0][:, :], ALU.subtract).then_inc(gap_ok, 1)
            dve.tensor_tensor(chosen[:, :, :], hot[0][:, :, :], hot[1][:, :, :], ALU.add).then_inc(m_ok, 1)
            dve.wait_ge(e2_ok, 1)
            link(dve.tensor_scalar(den[:, :], e2[:, :], 1.0, None, ALU.add))
            link(dve.reciprocal(w1[:, :], den[:, :]))
            link(dve.tensor_tensor(w2[:, :], e2[:, :], w1[:, :], ALU.mult))
            dve.wait_ge(counted, 1)
            link(dve.tensor_copy(cnt[:, :, :].rearrange("p a b -> p (a b)"), banks[1][:, 0:TT * E]))
            src, n, step = cnt, 0, 1
            while step < TT:
                dst = run[n % 2]
                link(dve.tensor_tensor(dst[:, step:TT, :], src[:, step:TT, :], src[:, 0:TT - step, :], ALU.add))
                link(dve.tensor_copy(dst[:, 0:step, :], src[:, 0:step, :]))
                src, n, step = dst, n + 1, 2 * step
            total = src[:, TT - 1, :]
            link(dve.tensor_scalar(nch[:, :], total, 1.0 / CHUNK, 0.5 - 0.5 / CHUNK, ALU.mult, ALU.add))
            link(dve.tensor_scalar(nch[:, :], nch[:, :], 1.5 * 2.0 ** 23, None, ALU.add))
            link(dve.tensor_scalar(nch[:, :], nch[:, :], -1.5 * 2.0 ** 23, None, ALU.add))
            esrc, n, step = nch, 0, 1
            while step < E:
                dst = ends[n % 2]
                link(dve.tensor_tensor(dst[:, step:E], esrc[:, step:E], esrc[:, 0:E - step], ALU.add))
                link(dve.tensor_copy(dst[:, 0:step], esrc[:, 0:step]))
                esrc, n, step = dst, n + 1, 2 * step
            link(dve.tensor_tensor(base[:, :], esrc[:, :], nch[:, :], ALU.subtract))
            link(dve.tensor_scalar(base[:, :], base[:, :], float(CHUNK), None, ALU.mult))
            link(dve.tensor_tensor(slot[:, :, :], src[:, :, :], cnt[:, :, :], ALU.subtract))
            link(dve.tensor_tensor(slot[:, :, :], slot[:, :, :], over_tiles(base), ALU.add))
            link(dve.tensor_tensor(slot[:, :, :], slot[:, :, :],
                                   banks[0][:, 0:TT * E].rearrange("p (a b) -> p a b", b=E), ALU.add))
            for j in range(2):
                link(dve.tensor_tensor(pick[:, :, :], slot[:, :, :], hot[j][:, :, :], ALU.mult))
                link(dve.tensor_reduce(slotf[:, :], pick[:, :, :], AX.X, ALU.add))
                link(dve.tensor_copy(slots[:, j, :], slotf[:, :]))
            link(dve.tensor_tensor(past[:, :, :], cidx[:, :, :],
                                   esrc[0:1, :].unsqueeze(1).to_broadcast([1, NCHUNK, E]), ALU.is_ge))
            link(dve.tensor_reduce(cexp[:, :], past[:, :, :], AX.X, ALU.add))
            link(dve.tensor_scalar(cexp[:, :], cexp[:, :], float(E - 1), None, ALU.min))
            link(dve.tensor_copy(chunk_expert[:, :], cexp[:, :]))


def experts(nc, banks, keep, w_exp, b2, rows_in, rows_out):
    x2, slots, chunk_expert = keep["x2"], keep["slots"], keep["chunk_expert"]
    with ExitStack() as ctx:
        def sb(name, shape, dt=F32):
            return ctx.enter_context(nc.sbuf_tensor(name, shape, dt))

        def sem(name):
            return ctx.enter_context(nc.semaphore(name))

        w = sb("e_w", [P, 2, WX])
        b2r = sb("e_b2r", [P, 2, D])
        xg = sb("e_xg", [P, 2, CT, D])
        xgt = sb("e_xgt", [P, 2, KD, CHUNK])
        ht = sb("e_ht", [P, 2, HB, CHUNK])
        y = sb("e_y", [P, 2, CT, D])
        ident = sb("e_ident", [P, P])
        zero = sb("e_zero", [P, 2048])
        ident_ok, zero_ok, cleared, placed = (sem("e_" + n) for n in ("ident_ok", "zero_ok", "cleared", "placed"))
        scattered = sem("e_scattered")
        chunk_in = [sem(f"e_chunk_in{u}") for u in range(2)]
        turned, xgt_ok, h_done, h_ok, y_done, y_ok = (
            sem("e_" + n) for n in ("turned", "xgt_ok", "h_done", "h_ok", "y_done", "y_ok"))
        y_out, y_stored = sem("e_y_out"), sem("e_y_stored")
        block = ctx.enter_context(nc.Block())
        W1 = [[w[:, u, kk * HID:(kk + 1) * HID] for kk in range(KD)] for u in range(2)]
        W2 = [[w[:, u, KD * HID + hb * D:KD * HID + (hb + 1) * D] for hb in range(HB)] for u in range(2)]
        B1 = [w[:, u, KD * HID + HB * D:WX] for u in range(2)]

        @block.gpsimd
        def _(gp):
            prime(gp, y_stored)
            make_identity(gp, ident, ident_ok)
            gp.memset(zero[:, :], 0.0).then_inc(zero_ok, 1)
            gp.wait_ge(cleared, 16)
            for t in range(TT):
                for j in range(2):
                    gp.indirect_dma_start(
                        out=rows_in, out_offset=bass.IndirectOffsetOnAxis(ap=slots[:, j, t:t + 1], axis=0),
                        in_=x2[:, t, :], in_offset=None).then_inc(placed, 16)
            gp.wait_ge(placed, 16 * 2 * TT)
            gp.nop().then_inc(scattered, 1)

        @block.sync
        def _(sp):
            sp.wait_ge(zero_ok, 1)
            per = SLOTS * D // P
            z = rows_in.rearrange("(p a) d -> p (a d)", p=P)
            n = 0
            sp.dma_start(z.rearrange("p (a c) -> p a c", c=2048),
                         zero[:, :].unsqueeze(1).to_broadcast([P, per // 2048, 2048])).then_inc(cleared, 16)
            sp.wait_ge(scattered, 1)
            with sp.Fori(0, NCHUNK // 2) as c2:
                for u in range(2):
                    c = c2 * 2 + u
                    sp.wait_ge(y_ok, c2 * 2 * CT + 1)
                    ex = sp.value_load(chunk_expert[0:1, bass.ds(c, 1)], min_val=0, max_val=E - 1)
                    sp.dma_start(xg[:, u, :, :], rows_in[bass.ds(c * CHUNK, CHUNK), :]
                                 .rearrange("(a p) d -> p a d", p=P)).then_inc(chunk_in[u], 16)
                    sp.dma_start(w[:, u, :], w_exp[bass.ds(ex, 1)].rearrange("a p n -> p (a n)")).then_inc(chunk_in[u], 16)
                    sp.dma_start(b2r[:, u, :], b2[bass.ds(ex, 1), :].rearrange("a n -> (a n)").partition_broadcast(P))\
                      .then_inc(chunk_in[u], 16)

        @block.tensor
        def _(pe):
            pe.wait_ge(ident_ok, 2)
            with pe.Fori(0, NCHUNK // 2) as c2:
                for u in range(2):
                    c = c2 * 2 + u
                    pe.wait_ge(chunk_in[u], (c2 + 1) * 48)
                    pe.wait_ge(xgt_ok, c + 1)
                    for kk in range(KD):
                        for a in range(CT):
                            mm = pe.transpose(banks[0][:, kk * CHUNK + a * P:kk * CHUNK + (a + 1) * P],
                                              xg[:, u, a, kk * P:(kk + 1) * P], ident[:, :])
                    mm.then_inc(turned, 1)
                    pe.wait_ge(xgt_ok, c + 2)
                    for hb in range(HB):
                        pe.wait_ge(h_ok, c * HB + max(hb - 1, 0) + 1)
                        for kk in range(KD):
                            mm = pe.matmul(banks[1 + hb % 2][:, 0:CHUNK], W1[u][kk][:, hb * P:(hb + 1) * P],
                                           xgt[:, u, kk, :], start=kk == 0, stop=kk == KD - 1)
                        mm.then_inc(h_done, 1)
                    pe.wait_ge(h_ok, c * HB + HB + 1)
                    for a in range(CT):
                        pe.wait_ge(y_ok, c * CT + max(a - 1, 0) + 1)
                        for hb in range(HB):
                            mm = pe.matmul(banks[3 + a % 2][:, 0:D], ht[:, u, hb, a * P:(a + 1) * P], W2[u][hb],
                                           start=hb == 0, stop=hb == HB - 1)
                        mm.then_inc(y_done, 1)

        @block.scalar
        def _(act):
            prime(act, xgt_ok, h_ok)
            with act.Fori(0, NCHUNK // 2) as c2:
                for u in range(2):
                    c = c2 * 2 + u
                    act.wait_ge(turned, c + 1)
                    act.copy(xgt[:, u, :, :].rearrange("p a b -> p (a b)"), banks[0][:, 0:KD * CHUNK]).then_inc(xgt_ok, 1)
                    act.wait_ge(chunk_in[u], (c2 + 1) * 48)
                    for hb in range(HB):
                        act.wait_ge(h_done, c * HB + hb + 1)
                        act.activation(ht[:, u, hb, :], banks[1 + hb % 2][:, 0:CHUNK], ACT.Gelu,
                                       bias=B1[u][:, hb:hb + 1]).then_inc(h_ok, 1)

        @block.vector
        def _(dve):
            prime(dve, y_ok)
            with dve.Fori(0, NCHUNK // 2) as c2:
                for u in range(2):
                    c = c2 * 2 + u
                    dve.wait_ge(chunk_in[u], (c2 + 1) * 48)
                    dve.wait_ge(y_stored, c + 1)
                    for a in range(CT):
                        dve.wait_ge(y_done, c * CT + a + 1)
                        dve.tensor_tensor(y[:, u, a, :], banks[3 + a % 2][:, 0:D], b2r[:, u, :], ALU.add).then_inc(y_ok, 1)

        @block.gpsimd
        def _(gp):
            with gp.Fori(0, NCHUNK // 2) as c2:
                for u in range(2):
                    c = c2 * 2 + u
                    gp.wait_ge(y_ok, c * CT + CT + 1)
                    gp.dma_start(rows_out[bass.ds(c * CHUNK, CHUNK), :].rearrange("(a p) d -> p a d", p=P),
                                 y[:, u, :, :]).then_inc(y_out, 16)
                    gp.wait_ge(y_out, 16 * c + 16)
                    gp.nop().then_inc(y_stored, 1)


def outputs(nc, banks, keep, gamma, beta, rows_out, out):
    x2, shared, w1, w2, slots = (keep[n] for n in ("x2", "shared", "w1", "w2", "slots"))
    with ExitStack() as ctx:
        def sb(name, shape, dt=F32):
            return ctx.enter_context(nc.sbuf_tensor(name, shape, dt))

        def sem(name):
            return ctx.enter_context(nc.semaphore(name))

        g = sb("o_g", [P, D])
        bt = sb("o_b", [P, D])
        y1 = sb("o_y1", [P, TT, D])
        y2 = sb("o_y2", [P, 8, D])
        stats = sb("o_stats", [P, TT, 6])
        mv = sb("o_mv", [P, TT, 2])
        std = sb("o_std", [P, 2, TT])
        c_in = sem("o_c_in")
        in1 = [sem(f"o_in1_{i}") for i in range(8)]
        in2 = [sem(f"o_in2_{i}") for i in range(8)]
        used, chain, var_ok, std_ok, done = (sem("o_" + n) for n in ("used", "chain", "var_ok", "std_ok", "done"))
        out_sem = sem("o_out")
        block = ctx.enter_context(nc.Block())

        @block.gpsimd
        def _(gp):
            for t in range(TT):
                if t >= 8:
                    gp.wait_ge(used, t - 7)
                gp.indirect_dma_start(out=y1[:, t, :], out_offset=None, in_=rows_out,
                                      in_offset=bass.IndirectOffsetOnAxis(ap=slots[:, 0, t:t + 1], axis=0))\
                  .then_inc(in1[t % 8], 16)
                gp.indirect_dma_start(out=y2[:, t % 8, :], out_offset=None, in_=rows_out,
                                      in_offset=bass.IndirectOffsetOnAxis(ap=slots[:, 1, t:t + 1], axis=0))\
                  .then_inc(in2[t % 8], 16)

        @block.sync
        def _(sp):
            sp.dma_start(g[:, :], gamma.partition_broadcast(P)).then_inc(c_in, 16)
            sp.dma_start(bt[:, :], beta.partition_broadcast(P)).then_inc(c_in, 16)
            sp.wait_ge(done, 1)
            sp.dma_start(out.rearrange("b s d -> (b s) d").rearrange("(t p) d -> p t d", p=P), y1[:, :, :]).then_inc(out_sem, 16)
            sp.wait_ge(out_sem, 16)

        @block.scalar
        def _(act):
            for n in range(2):
                act.wait_ge(var_ok, n + 1)
                act.activation(std[:, n, :], mv[:, :, 1], ACT.Sqrt).then_inc(std_ok, 1)

        @block.vector
        def _(dve):
            steps = [0]

            def stage(instructions):
                for ins in instructions:
                    last = ins
                steps[0] += 1
                last.then_inc(chain, 1)
                dve.wait_ge(chain, steps[0])

            def normed(n):
                stage(dve.bn_stats(stats[:, t, :], y1[:, t, :]) for t in range(TT))
                stage(dve.bn_aggr(mv[:, t, :], stats[:, t, :]) for t in range(TT))
                dve.tensor_scalar(mv[:, :, 1], mv[:, :, 1], EPS, None, ALU.add).then_inc(var_ok, 1)
                dve.wait_ge(std_ok, n + 1)
                stage([dve.reciprocal(std[:, n, :], std[:, n, :])])
                stage(dve.tensor_scalar(y1[:, t, :], y1[:, t, :], mv[:, t, 0:1], std[:, n, t:t + 1],
                                        ALU.subtract, ALU.mult) for t in range(TT))

            for t in range(TT):
                dve.wait_ge(in1[t % 8], 16 * (t // 8 + 1))
                stage([dve.tensor_scalar(y1[:, t, :], y1[:, t, :], w1[:, t:t + 1], None, ALU.mult)])
                dve.wait_ge(in2[t % 8], 16 * (t // 8 + 1))
                stage([dve.scalar_tensor_tensor(y1[:, t, :], y2[:, t % 8, :], w2[:, t:t + 1], y1[:, t, :],
                                                ALU.mult, ALU.add)])
                dve.scalar_tensor_tensor(y1[:, t, :], shared[:, t, :], 0.5, y1[:, t, :], ALU.mult, ALU.add)\
                   .then_inc(used, 1)
            dve.wait_ge(used, TT)
            normed(0)
            dve.wait_ge(c_in, 32)
            rows = [slice(t, t + 8) for t in range(0, TT, 8)]
            stage(dve.tensor_tensor(y1[:, r, :], y1[:, r, :], g[:, :].unsqueeze(1).to_broadcast([P, 8, D]), ALU.mult)
                  for r in rows)
            stage(dve.tensor_tensor(y1[:, r, :], y1[:, r, :], bt[:, :].unsqueeze(1).to_broadcast([P, 8, D]), ALU.add)
                  for r in rows)
            stage(dve.tensor_tensor(y1[:, r, :], y1[:, r, :], x2[:, r, :], ALU.add) for r in rows)
            normed(1)
            dve.nop().then_inc(done, 1)


def scores_all(banks):
    return banks.both[0]


def turned_all(banks):
    return banks.both[1]


class Banks:

    def __init__(self, ps):
        self.ps = ps
        self.both = [ps[:, 0:2 * BANK], ps[:, 2 * BANK:4 * BANK]]

    def __getitem__(self, i):
        if isinstance(i, slice):
            return [self[j] for j in range(*i.indices(8))]
        return self.ps[:, i * BANK:(i + 1) * BANK]


def layer(nc, x_t, x_rows, w_qkv, w_o, w_exp, b2, w_gs, shared_b, gamma, beta, out):
    attn_out = nc.dram_tensor("attn_out", [B * PAIRS, P, S], F32, kind="Internal").ap()
    rows_in = nc.dram_tensor("rows_in", [SLOTS, D], F32, kind="Internal").ap()
    rows_out = nc.dram_tensor("rows_out", [SLOTS, D], F32, kind="Internal").ap()
    with ExitStack() as ctx:
        banks = Banks(ctx.enter_context(nc.psum_tensor("banks", [P, 8 * BANK], F32)))
        attention(nc, banks, x_t, w_qkv, attn_out)
        keep = {name: ctx.enter_context(nc.sbuf_tensor(name, shape, dt)) for name, shape, dt in (
            ("x2", [P, TT, D], F32), ("shared", [P, TT, D], F32), ("logits", [P, TT, E], F32),
            ("w1", [P, TT], F32), ("w2", [P, TT], F32), ("slots", [P, 2, TT], U32),
            ("chunk_expert", [1, NCHUNK], I32))}
        tokens(nc, banks, keep, x_rows, attn_out, w_o, w_gs, shared_b)
        routing(nc, banks, keep)
        experts(nc, banks, keep, w_exp, b2, rows_in, rows_out)
        outputs(nc, banks, keep, gamma, beta, rows_out, out)


def kernel(L0_attn_x, L0_attn_kernel, L0_attn_WO, L0_ffn_W1, L0_ffn_b1, L0_ffn_W2, L0_ffn_b2, L0_ffn_gate_W,
           L0_ffn_shared_W, L0_ffn_shared_b, L0_ffn_gamma, L0_ffn_beta):
    import numpy as np
    import concourse.bacc as bacc
    from concourse.bass_utils import run_bass_kernel_spmd

    x = np.asarray(L0_attn_x)
    wk = np.asarray(L0_attn_kernel).reshape(3, PAIRS, 2, KD, P, DH)
    qk = wk[0:2].transpose(1, 4, 3, 2, 0, 5).reshape(PAIRS, P, KD, 2, P)
    vv = wk[2].transpose(0, 3, 2, 1, 4).reshape(PAIRS, P, KD, 1, P)
    w1 = np.asarray(L0_ffn_W1).reshape(E, KD, P, HID).transpose(0, 2, 1, 3).reshape(E, P, KD * HID)
    w2 = np.asarray(L0_ffn_W2).reshape(E, HB, P, D).transpose(0, 2, 1, 3).reshape(E, P, HB * D)
    b1 = np.asarray(L0_ffn_b1).reshape(E, HB, P).transpose(0, 2, 1)
    gs = np.concatenate([np.asarray(L0_ffn_shared_W), np.asarray(L0_ffn_gate_W)], axis=1)
    arrays = {
        "x_t": x.reshape(T, KD, P).transpose(2, 1, 0),
        "x_rows": x.reshape(T, D),
        "w_qkv": np.concatenate([qk, vv], axis=3),
        "w_o": np.asarray(L0_attn_WO).reshape(DH, PAIRS, 2, D).transpose(2, 0, 1, 3).reshape(P, PAIRS, D),
        "w_exp": np.concatenate([w1, w2, b1], axis=2),
        "b2": np.asarray(L0_ffn_b2),
        "w_gs": gs.reshape(KD, P, D + E).transpose(1, 0, 2),
        "shared_b": np.asarray(L0_ffn_shared_b),
        "gamma": np.asarray(L0_ffn_gamma),
        "beta": np.asarray(L0_ffn_beta),
    }
    arrays = {name: np.ascontiguousarray(a) for name, a in arrays.items()}
    nc = bacc.Bacc("TRN2", target_bir_lowering=False, num_devices=1)
    args = [nc.dram_tensor(name, a.shape, mybir.dt.from_np(a.dtype), kind="ExternalInput").ap()
            for name, a in arrays.items()]
    out = nc.dram_tensor("out", [B, S, D], F32, kind="ExternalOutput").ap()
    layer(nc, *args, out)
    return run_bass_kernel_spmd(nc, [arrays], core_ids=[0]).results[0]["out"]
```

```python
from contextlib import ExitStack

import concourse.bass as bass
from concourse import mybir

F32 = mybir.dt.float32
I32 = mybir.dt.int32
U32 = mybir.dt.uint32
ALU = mybir.AluOpType
ACT = mybir.ActivationFunctionType
AX = mybir.AxisListType

P = 128
B, S, D = 4, 1024, 256
H, DH = 16, 64
E, HID, TOPK = 8, 1024, 2
T = B * S
KD = D // P
PAIRS = H // 2
ST = S // P
TT = T // P
BANK = 512
NB = S // BANK
HB = HID // P
SCALE = 1.0 / (DH * DH * H)
EPS = 1e-5
CHUNK = 256
CT = CHUNK // P
NCHUNK = (TOPK * T + E * (CHUNK - 1)) // CHUNK
NCHUNK += NCHUNK % 2
SLOTS = NCHUNK * CHUNK
WX = KD * HID + HB * D + HB
NEVER = -3.0e38
LIMIT = 40.0
INVERT_AT = 4
DIVIDE_AT = 1
SUM_TURN = 2
TV_AT, QK_AT, VT_AT = 0, 2, 6
LAG = 3
POOL_EL = ()


def prime(engine, *semaphores):
    for semaphore in semaphores:
        engine.nop().then_inc(semaphore, 1)


def make_identity(gpsimd, tile, done):
    gpsimd.memset(tile[:, :], 0.0).then_inc(done, 1)
    gpsimd.wait_ge(done, 1)
    gpsimd.affine_select(out=tile[:, :], in_=tile[:, :], compare_op=ALU.not_equal, fill=1.0, base=0,
                         pattern=[[-1, P]], channel_multiplier=1).then_inc(done, 1)


def score_bound(nc, banks, keep, x_rows, w_qkv):
    bounded = keep["bounded"]
    QK = PAIRS * 4
    with ExitStack() as ctx:
        def sb(name, shape, dt=F32):
            return ctx.enter_context(nc.sbuf_tensor(name, shape, dt))

        def sem(name):
            return ctx.enter_context(nc.semaphore(name))

        xr = sb("b_xr", [P, TT, D])
        wr = sb("b_wr", [P, PAIRS, KD * 3 * P])
        xx = sb("b_xx", [P, TT])
        xm = sb("b_xm", [P, P])
        wsq = sb("b_wsq", [P, KD, QK, DH])
        ww = sb("b_ww", [P, KD, QK])
        junk = sb("b_junk", [P, 2, D])
        ones = sb("b_ones", [P, P])
        ident = sb("b_ident", [P, P])
        xtop = sb("b_xtop", [1, 1])
        wtot = sb("b_wtot", [1, 2, QK])
        wsum = sb("b_wsum", [1, QK])
        wprod = sb("b_wprod", [1, QK // 2])
        wtop = sb("b_wtop", [1, 1])
        b1 = sb("b_b1", [1, 1])
        b2 = sb("b_b2", [1, 1])
        b3 = sb("b_b3", [1, 1])
        flag = sb("b_flag", [1, 1])
        x_in, w_in, ident_ok, ones_ok = sem("b_x_in"), sem("b_w_in"), sem("b_ident_ok"), sem("b_ones_ok")
        xx_ok, ww_ok, xx_turned, ww_summed, chain = (
            sem("b_" + n) for n in ("xx_ok", "ww_ok", "xx_turned", "ww_summed", "chain"))
        block = ctx.enter_context(nc.Block())

        @block.sync
        def _(sp):
            sp.dma_start(xr[:, :, :], x_rows.rearrange("(t p) d -> p t d", p=P)).then_inc(x_in, 16)

        @block.scalar
        def _(act):
            act.dma_start(wr[:, :, :], w_qkv.rearrange("a p k b c -> p a (k b c)")).then_inc(w_in, 16)
            act.wait_ge(w_in, 16)
            w6 = wr[:, :, :].rearrange("p a (k b c) -> p k a b c", k=KD, b=3)
            for kk in range(KD):
                for a in range(PAIRS):
                    ins = act.activation(wsq[:, kk, 4 * a:4 * a + 4, :].rearrange("p (b g) c -> p b (g c)", b=2),
                                         w6[:, kk, a, 0:2, :], ACT.Square)
            ins.then_inc(ww_ok, 1)

        @block.gpsimd
        def _(gp):
            gp.memset(ones[:, :], 1.0).then_inc(ones_ok, 1)
            make_identity(gp, ident, ident_ok)

        @block.tensor
        def _(pe):
            pe.wait_ge(ident_ok, 2)
            pe.wait_ge(ones_ok, 1)
            pe.wait_ge(xx_ok, 1)
            pe.transpose(banks[0][:, 0:P], xm[:, :], ident[:, :]).then_inc(xx_turned, 1)
            pe.wait_ge(ww_ok, 2)
            pe.matmul(banks[1][:, 0:KD * QK], ones[:, :], ww[:, :, :].rearrange("p a b -> p (a b)"),
                      start=True, stop=True).then_inc(ww_summed, 1)

        @block.vector
        def _(dve):
            steps = [0]

            def link(ins):
                steps[0] += 1
                ins.then_inc(chain, 1)
                dve.wait_ge(chain, steps[0])

            dve.wait_ge(x_in, 16)
            link(dve.memset(xm[:, :], 0.0))
            for t in range(TT):
                link(dve.tensor_tensor_reduce(out=junk[:, t % 2, :], in0=xr[:, t, :], in1=xr[:, t, :], scale=1.0,
                                              scalar=0.0, op0=ALU.mult, op1=ALU.add, accum_out=xx[:, t:t + 1]))
            dve.tensor_reduce(xm[:, 0:1], xx[:, :], AX.X, ALU.max).then_inc(xx_ok, 1)
            dve.wait_ge(ww_ok, 1)
            dve.tensor_reduce(ww[:, :, :], wsq[:, :, :, :], AX.X, ALU.add).then_inc(ww_ok, 1)
            dve.wait_ge(xx_turned, 1)
            link(dve.tensor_reduce(xtop[:, :], banks[0][0:1, 0:P], AX.X, ALU.max))
            dve.wait_ge(ww_summed, 1)
            link(dve.tensor_copy(wtot[:, :, :].rearrange("p a b -> p (a b)"), banks[1][0:1, 0:KD * QK]))
            link(dve.tensor_tensor(wsum[:, :], wtot[:, 0, :], wtot[:, 1, :], ALU.add))
            pair = wsum[:, :].rearrange("p (a two) -> p a two", two=2)
            link(dve.tensor_tensor(wprod[:, :], pair[:, :, 0], pair[:, :, 1], ALU.mult))
            link(dve.tensor_reduce(wtop[:, :], wprod[:, :], AX.X, ALU.max))
            link(dve.tensor_scalar(b1[:, :], xtop[:, :], SCALE, None, ALU.mult))
            link(dve.tensor_tensor(b2[:, :], b1[:, :], b1[:, :], ALU.mult))
            link(dve.tensor_tensor(b3[:, :], b2[:, :], wtop[:, :], ALU.mult))
            link(dve.tensor_scalar(flag[:, :], b3[:, :], LIMIT * LIMIT, None, ALU.is_le))
            link(dve.tensor_copy(bounded[:, :], flag[:, :]))


def attention(nc, banks, keep, x_t, w_qkv, inv_row, attn_out):
    UNITS = 2 * ST
    SLOTS_ = B * H
    NE = 4
    R32 = mybir.dt.float32r
    with ExitStack() as ctx:
        def sb(name, shape, dt=F32):
            return ctx.enter_context(nc.sbuf_tensor(name, shape, dt))

        def sem(name):
            return ctx.enter_context(nc.semaphore(name))

        xh = sb("a_xh", [P, KD, T], R32)
        xl = sb("a_xl", [P, KD, T], R32)
        w = sb("a_w", [P, KD, 3, P])
        wh = sb("a_wh", [P, KD, 3, P], R32)
        wl = sb("a_wl", [P, KD, 3, P], R32)
        qa = [sb(f"a_qa{j}", [P, S], R32) for j in range(2)]
        ka = [sb(f"a_ka{j}", [P, S], R32) for j in range(2)]
        kb = [sb(f"a_kb{j}", [P, S], R32) for j in range(2)]
        e = [sb(f"a_e{j}", [P, S]) for j in range(NE)]
        eh = [sb(f"a_eh{j}", [P, S], R32) for j in range(NE)]
        el = [sb(f"a_el{j}", [P, S], R32) for j in range(NE)]
        vv = [sb(f"a_vv{h}", [P, ST, 2, DH], R32) for h in range(2)]
        vt = sb("a_vt", [P, S])
        vst = sb("a_vst", [P, ST, P])
        esum = [sb(f"a_esum{j}", [P, S]) for j in range(2)]
        inv = sb("a_inv", [P, S])
        srow = sb("a_srow", [1, S])
        scol = sb("a_scol", [P, S // P])
        icol = sb("a_icol", [P, S // P])
        ob = sb("a_ob", [DH, S])
        osum = sb("a_osum", [DH, S])
        ot = sb("a_ot", [P, S])
        xb = sb("a_xb", [P, KD, S])
        ones = sb("a_ones", [P, DH])
        ident = sb("a_ident", [P, P])
        small = sb("a_small", [P, 4])
        ring, proj, o_acc = banks.both[0:2], banks.both[2], banks.both[3]
        bounded = keep["bounded"]

        ident_ok, ones_ok = sem("a_ident_ok"), sem("a_ones_ok")
        x_in = [sem(f"a_x_in{j}") for j in range(NE)]
        xh_ok, xl_ok, w_in, wh_ok, wl_ok = (sem("a_" + n) for n in ("xh_ok", "xl_ok", "w_in", "wh_ok", "wl_ok"))
        qk_done, qk_hi, qk_lo = sem("a_qk_done"), sem("a_qk_hi"), sem("a_qk_lo")
        kh_dup, kl_dup = ([sem(f"a_{name}_dup{j}") for j in range(2)] for name in ("kh", "kl"))
        vt_done, vt_ok, tv_done, vst_ok = (sem("a_" + n) for n in ("vt_done", "vt_ok", "tv_done", "vst_ok"))
        v_ok = [sem(f"a_v_ok{h}") for h in range(2)]
        s_done, e_ok, eh_ok, acc_ok, pv_done = (sem("a_" + n) for n in ("s_done", "e_ok", "eh_ok", "acc_ok", "pv_done"))
        v_hi, stored = sem("a_v_hi"), sem("a_stored")
        el_ok = {"dve": sem("a_el_dve"), "pool": sem("a_el_pool")}
        r_done, srow_ok, row_spread, col_in, icol_ok, icol_out, icol_stored, inv_in, ob_ok, osum_ok, ot_ok, ot_out = (
            sem("a_" + n) for n in ("r_done", "srow_ok", "row_spread", "col_in", "icol_ok", "icol_out",
                                     "icol_stored", "inv_in", "ob_ok", "osum_ok", "ot_ok", "ot_out"))

        def turn(h, position):
            return ring[(h * (ST + 1) + position) % 2]

        def members(who):
            return [n for n in range(ST) if (n in POOL_EL) == (who == "pool")]

        def wait_el(eng, slot, n):
            who = "pool" if n in POOL_EL else "dve"
            mine = members(who)
            eng.wait_ge(el_ok[who], slot * len(mine) + mine.index(n) + 1)

        def make_el(eng, slot, n, first):
            who = "pool" if n in POOL_EL else "dve"
            eng.wait_ge(eh_ok, slot * ST + n + 1)
            if not (first and n < NE):
                eng.wait_ge(pv_done, slot * ST + n - NE + 1)
            eng.tensor_tensor(el[n % NE][:, :], e[n % NE][:, :], eh[n % NE][:, :].bitcast(F32), ALU.subtract)\
               .then_inc(el_ok[who], 1)

        def sp_bounded(sp):
            prime(sp, stored, row_spread, icol_stored)
            for j in range(T // BANK):
                if j >= NE:
                    sp.wait_ge(xl_ok, j - NE + 1)
                sp.dma_start(e[j % NE][:, :].rearrange("p (k s) -> p k s", k=KD),
                             x_t[:, :, j * BANK:(j + 1) * BANK]).then_inc(x_in[j % NE], 16)

            def dup(slot, j):
                sp.wait_ge(qk_hi, slot * 2 + 2)
                sp.dma_start(ka[j][0:DH, :].bitcast(F32), ka[j][DH:P, :].bitcast(F32)).then_inc(kh_dup[j], 16)
                sp.wait_ge(qk_lo, slot + 1)
                sp.dma_start(kb[j][0:DH, :].bitcast(F32), kb[j][DH:P, :].bitcast(F32)).then_inc(kl_dup[j], 16)

            def spread(slot):
                sp.wait_ge(srow_ok, slot + 1)
                sp.dma_start(scol[:, :], srow[:, :]).then_inc(col_in, 16)
                sp.wait_ge(col_in, 16 * slot + 16)
                sp.nop().then_inc(row_spread, 1)

            def broadcast(slot):
                sp.wait_ge(icol_ok, slot + 1)
                sp.dma_start(inv_row.rearrange("(p c) -> p c", p=P), icol[:, :]).then_inc(icol_out, 16)
                sp.wait_ge(icol_out, 16 * slot + 16)
                sp.nop().then_inc(icol_stored, 1)
                sp.wait_ge(ot_ok, slot + 1)
                sp.dma_start(inv[0:DH, :], inv_row.partition_broadcast(DH)).then_inc(inv_in, 16)
                sp.wait_ge(inv_in, 16 * slot + 16)

            def weights(n, pair):
                if n is not None:
                    sp.wait_ge(wl_ok, n)
                sp.dma_start(w[:, :, :, :], w_qkv[pair]).then_inc(w_in, 16)

            def store(pair):
                sp.wait_ge(ot_ok, pair * 2 + 3)
                sp.dma_start(attn_out[pair], ot[:, :]).then_inc(ot_out, 16)
                sp.wait_ge(ot_out, 16 * pair + 16)
                sp.nop().then_inc(stored, 1)

            weights(None, 0)
            dup(0, 0)
            weights(1, 1)
            dup(1, 1)
            with sp.Fori(0, B * PAIRS - 1) as i:
                weights(i + 2, (i + 2) % PAIRS)
                spread(2 * i)
                dup(2 * i + 2, 0)
                broadcast(2 * i)
                spread(2 * i + 1)
                dup(2 * i + 3, 1)
                broadcast(2 * i + 1)
                store(i)
            spread(SLOTS_ - 2)
            broadcast(SLOTS_ - 2)
            spread(SLOTS_ - 1)
            broadcast(SLOTS_ - 1)
            store(B * PAIRS - 1)

        def pe_bounded(pe):
            def project(blk, b, half):
                cols = bass.ds(b * S + half * BANK, BANK)
                parts = [(wt[:, kk, blk, :], xs[:, kk, cols]) for kk in range(KD)
                         for wt, xs in ((wh, xh), (wh, xl), (wl, xh))]
                for m, (lhs, rhs) in enumerate(parts):
                    mm = pe.matmul(proj[:, half * BANK:(half + 1) * BANK], lhs, rhs, start=m == 0,
                                   stop=m == len(parts) - 1)
                return mm

            def project_qk(slot, h, b, half):
                if half == 0:
                    pe.wait_ge(wl_ok, (slot + 1) // 2 + 1)
                    if h:
                        pe.wait_ge(vst_ok, slot // 2 + 1)
                    else:
                        pe.wait_ge(qk_lo, slot + 1)
                mm = project(h, b, half)
                if half:
                    mm.then_inc(qk_done, 1)

            def project_v(pair, b, half):
                if half == 0:
                    pe.wait_ge(qk_lo, pair * 2 + 1)
                mm = project(2, b, half)
                if half:
                    mm.then_inc(vt_done, 1)

            def turn_v(pair):
                pe.wait_ge(vt_ok, pair + 1)
                for t in range(ST):
                    mm = pe.transpose(proj[:, t * P:(t + 1) * P], vt[:, t * P:(t + 1) * P], ident[:, :])
                mm.then_inc(tv_done, 1)

            def sums(slot, h):
                pe.wait_ge(acc_ok, slot * (ST - 1) + ST - 1)
                pe.wait_ge(e_ok, (slot + 1) * ST + 1)
                for m in range(NB):
                    mm = pe.matmul(turn(1 - h, SUM_TURN)[0:DH, m * BANK:(m + 1) * BANK], ones[:, :],
                                   esum[h][:, m * BANK:(m + 1) * BANK], start=True, stop=True)
                mm.then_inc(r_done, 1)

            def scores(slot, h, n, first):
                if n == 0:
                    pe.wait_ge(qk_lo, slot + 1)
                    pe.wait_ge(kh_dup[h], (slot // 2) * 16 + 16)
                if n in (0, 1) or n > 3:
                    if not (first and n < 2):
                        pe.wait_ge(e_ok, slot * ST + n - 1)
                elif n == 2:
                    pe.wait_ge(e_ok, slot * ST + 2)
                elif not first:
                    pe.wait_ge(srow_ok, slot)
                tile = turn(h, n + (n >= SUM_TURN))
                for part, (start, stop) in ((ka, (True, False)), (kb, (False, True))):
                    if n == 0 and part is kb:
                        pe.wait_ge(kl_dup[h], (slot // 2) * 16 + 16)
                    for m in range(NB):
                        mm = pe.matmul(tile[:, m * BANK:(m + 1) * BANK], part[h][:, n * P:(n + 1) * P],
                                       qa[h][:, m * BANK:(m + 1) * BANK], start=start, stop=stop,
                                       skip_group_check=True)
                mm.then_inc(s_done, 1)

            def values(slot, h, n, first=False):
                if n == 0:
                    pe.wait_ge(v_ok[h], slot // 2 + 1)
                    if not first:
                        pe.wait_ge(osum_ok, slot)
                pe.wait_ge(eh_ok, slot * ST + n + 1)
                lhs = vv[h][:, n, :, :].rearrange("p a d -> p (a d)")
                for part in (eh, el):
                    if part is el:
                        wait_el(pe, slot, n)
                    for m in range(NB):
                        mm = pe.matmul(o_acc[:, m * BANK:(m + 1) * BANK], lhs, part[n % NE][:, m * BANK:(m + 1) * BANK],
                                       start=n == 0 and part is eh, stop=n == ST - 1 and part is el,
                                       skip_group_check=True)
                mm.then_inc(pv_done, 1)

            def slot_program(slot, h, b, first=False, last=False):
                for n in range(ST):
                    scores(slot, h, n, first)
                    if n == 1 and not first:
                        sums(slot - 1, 1 - h)
                    if n == QK_AT + 1 and not last:
                        project_qk(slot, 1 - h, b, 1)
                    if n >= LAG:
                        values(slot, h, n - LAG, first)
                    elif not first:
                        values(slot - 1, 1 - h, ST - LAG + n)
                    if n == TV_AT and not h:
                        turn_v(slot // 2)
                    if n == QK_AT and not last:
                        project_qk(slot, 1 - h, b, 0)
                    if n in (VT_AT, VT_AT + 1) and h and not last:
                        project_v(slot // 2 + 1, b, n - VT_AT)

            pe.wait_ge(ident_ok, 2)
            pe.wait_ge(ones_ok, 1)
            pe.wait_ge(xl_ok, T // BANK)
            pe.wait_ge(wl_ok, 1)
            for half in range(2):
                mm = project(0, 0, half)
            mm.then_inc(qk_done, 1)
            for half in range(2):
                project_v(0, 0, half)
            slot_program(0, 0, 0, first=True)
            with pe.Fori(0, B * PAIRS - 1) as i:
                b = (i + 1) // PAIRS
                slot_program(2 * i + 1, 1, b)
                slot_program(2 * i + 2, 0, b)
            slot_program(SLOTS_ - 1, 1, 0, last=True)
            for n in range(ST - LAG, ST):
                values(SLOTS_ - 1, 1, n)
            pe.wait_ge(acc_ok, SLOTS_ * (ST - 1))
            pe.wait_ge(e_ok, SLOTS_ * ST)
            for m in range(NB):
                mm = pe.matmul(turn(0, SUM_TURN)[0:DH, m * BANK:(m + 1) * BANK], ones[:, :],
                               esum[1][:, m * BANK:(m + 1) * BANK], start=True, stop=True)
            mm.then_inc(r_done, 1)

        def act_bounded(act):
            for j in range(T // BANK):
                act.wait_ge(x_in[j % NE], 16 * (j // NE + 1))
                act.copy(xh[:, :, j * BANK:(j + 1) * BANK],
                         e[j % NE][:, :].rearrange("p (k s) -> p k s", k=KD)).then_inc(xh_ok, 1)

            def weights(n):
                act.wait_ge(w_in, 16 * n)
                act.copy(wh[:, :, :, :], w[:, :, :, :]).then_inc(wh_ok, 1)

            def qk_high(slot, j):
                act.wait_ge(qk_done, slot + 1)
                act.copy(qa[j][0:DH, :], proj[0:DH, :]).then_inc(qk_hi, 1)
                act.copy(ka[j][DH:P, :], proj[DH:P, :]).then_inc(qk_hi, 1)

            def v_turned(pair):
                act.wait_ge(vt_done, pair + 1)
                act.copy(vt[:, :], proj).then_inc(vt_ok, 1)

            def v_rows(pair):
                act.wait_ge(tv_done, pair + 1)
                act.copy(vst[:, :, :].rearrange("p a b -> p (a b)"), proj).then_inc(vst_ok, 1)

            def probs(slot, h, n, first):
                act.wait_ge(s_done, slot * ST + n + 1)
                if not (first and n < NE):
                    before = slot if n >= NE else slot - 1
                    m = (n - NE) % ST
                    wait_el(act, before, m)
                    act.wait_ge(acc_ok, before * (ST - 1) + max(m, 1))
                act.activation(e[n % NE][:, :], turn(h, n + (n >= SUM_TURN)), ACT.Exp, scale=SCALE).then_inc(e_ok, 1)

            def high(slot, n, first=False):
                act.wait_ge(e_ok, slot * ST + n + 1)
                if not (first and n < NE):
                    act.wait_ge(pv_done, slot * ST + n - NE + 1)
                act.copy(eh[n % NE][:, :], e[n % NE][:, :]).then_inc(eh_ok, 1)

            def o_low(slot):
                act.wait_ge(pv_done, slot * ST + ST)
                act.copy(ob[:, :], o_acc[DH:P, :]).then_inc(ob_ok, 1)

            def sum_row(slot, h):
                act.wait_ge(r_done, slot + 1)
                act.wait_ge(row_spread, slot + 1)
                act.copy(srow[:, :], turn(1 - h, SUM_TURN)[0:1, :]).then_inc(srow_ok, 1)

            def slot_program(slot, h, first=False, last=False):
                for n in range(ST):
                    if n == SUM_TURN and not first:
                        sum_row(slot - 1, 1 - h)
                    if n == LAG and not first:
                        o_low(slot - 1)
                    if n == 0 and not h and not first:
                        v_turned(slot // 2)
                    probs(slot, h, n, first)
                    if n >= 1:
                        high(slot, n - 1, first)
                    elif not first:
                        high(slot - 1, ST - 1)
                    if n == TV_AT + 1 and not h:
                        v_rows(slot // 2)
                    if n == QK_AT + 2 and not last:
                        qk_high(slot + 1, 1 - h)
                        if not h:
                            weights(slot // 2 + 2)

            weights(1)
            qk_high(0, 0)
            v_turned(0)
            slot_program(0, 0, first=True)
            with act.Fori(0, B * PAIRS - 1) as i:
                slot_program(2 * i + 1, 1)
                slot_program(2 * i + 2, 0)
            slot_program(SLOTS_ - 1, 1, last=True)
            high(SLOTS_ - 1, ST - 1)
            o_low(SLOTS_ - 1)
            sum_row(SLOTS_ - 1, 1)

        def dve_bounded(dve):
            for j in range(T // BANK):
                dve.wait_ge(xh_ok, j + 1)
                cols = slice(j * BANK, (j + 1) * BANK)
                dve.tensor_tensor(xl[:, :, cols], e[j % NE][:, :].rearrange("p (k s) -> p k s", k=KD),
                                  xh[:, :, cols].bitcast(F32), ALU.subtract).then_inc(xl_ok, 1)

            def weights(n):
                dve.wait_ge(wh_ok, n)
                dve.tensor_tensor(wl[:, :, :, :], w[:, :, :, :], wh[:, :, :, :].bitcast(F32), ALU.subtract)\
                   .then_inc(wl_ok, 1)

            def qk_low(slot, j):
                dve.wait_ge(qk_hi, slot * 2 + 1)
                dve.tensor_tensor(qa[j][DH:P, :], proj[0:DH, :], qa[j][0:DH, :].bitcast(F32), ALU.subtract)
                dve.wait_ge(qk_hi, slot * 2 + 2)
                dve.tensor_tensor(kb[j][DH:P, :], proj[DH:P, :], ka[j][DH:P, :].bitcast(F32), ALU.subtract)\
                   .then_inc(qk_lo, 1)

            def split_v(slot, h):
                if h == 0:
                    dve.wait_ge(vst_ok, slot // 2 + 1)
                part = vst[:, :, h * DH:(h + 1) * DH]
                dve.tensor_copy(vv[h][:, :, 0, :], part).then_inc(v_hi, 1)
                dve.wait_ge(v_hi, slot + h + 1)
                dve.tensor_tensor(vv[h][:, :, 1, :], part, vv[h][:, :, 0, :].bitcast(F32), ALU.subtract)\
                   .then_inc(v_ok[h], 1)

            def add(slot, h, n):
                acc = esum[h][:, :]
                if n == 1:
                    dve.tensor_tensor(acc, e[0][:, :], e[1][:, :], ALU.add).then_inc(acc_ok, 1)
                else:
                    dve.wait_ge(acc_ok, slot * (ST - 1) + n - 1)
                    dve.tensor_tensor(acc, acc, e[n % NE][:, :], ALU.add).then_inc(acc_ok, 1)

            def o_sum(slot):
                dve.wait_ge(ob_ok, slot + 1)
                dve.wait_ge(ot_ok, slot + 1)
                dve.tensor_tensor(osum[:, :], o_acc[0:DH, :], ob[:, :], ALU.add).then_inc(osum_ok, 1)

            def invert(slot):
                dve.wait_ge(col_in, 16 * slot + 16)
                dve.wait_ge(icol_stored, slot + 1)
                dve.reciprocal(icol[:, :], scol[:, :]).then_inc(icol_ok, 1)

            def divide(slot, h):
                dve.wait_ge(osum_ok, slot + 1)
                dve.wait_ge(inv_in, 16 * slot + 16)
                if h == 0:
                    dve.wait_ge(stored, slot // 2 + 1)
                dve.tensor_tensor(ot[h * DH:(h + 1) * DH, :], osum[:, :], inv[0:DH, :], ALU.mult).then_inc(ot_ok, 1)

            def slot_program(slot, h, first=False, second=False, last=False):
                for n in range(ST):
                    if n == LAG and not first:
                        o_sum(slot - 1)
                    if n == DIVIDE_AT and not first and not second:
                        divide(slot - 2, h)
                    if n >= 1:
                        make_el(dve, slot, n - 1, first)
                        dve.wait_ge(e_ok, slot * ST + n + 1)
                        add(slot, h, n)
                    elif not first:
                        make_el(dve, slot - 1, ST - 1, False)
                    if n == TV_AT + 1 and not h:
                        split_v(slot, 0)
                    if n == TV_AT + 3 and not h:
                        split_v(slot, 1)
                    if n == QK_AT + 2 and not last:
                        qk_low(slot + 1, 1 - h)
                        if not h:
                            weights(slot // 2 + 2)
                    if n == INVERT_AT and not first:
                        invert(slot - 1)

            prime(dve, ot_ok)
            weights(1)
            qk_low(0, 0)
            slot_program(0, 0, first=True)
            slot_program(1, 1, second=True)
            with dve.Fori(1, B * PAIRS - 1) as i:
                slot_program(2 * i, 0)
                slot_program(2 * i + 1, 1)
            slot_program(SLOTS_ - 2, 0)
            slot_program(SLOTS_ - 1, 1, last=True)
            divide(SLOTS_ - 2, 0)
            make_el(dve, SLOTS_ - 1, ST - 1, False)
            o_sum(SLOTS_ - 1)
            invert(SLOTS_ - 1)
            divide(SLOTS_ - 1, 1)

        def pool_bounded(gp):
            def slot_program(slot, first=False):
                for n in POOL_EL:
                    make_el(gp, slot, n, first)

            if POOL_EL:
                slot_program(0, first=True)
                with gp.Fori(1, SLOTS_) as slot:
                    slot_program(slot)

        q = [e[h][0:DH, :] for h in range(2)]
        k = [e[2 + h][0:DH, :] for h in range(2)]
        top, shift, total, rcp = (small[:, n:n + 1] for n in range(4))
        scores, turned, misc, o_ps = banks[0:2], banks[2:4], banks[4:6], banks[6]
        g_qkv_done = sem("a_g_qkv_done")
        g_qkv_evac = sem("a_g_qkv_evac")
        g_w_in = sem("a_g_w_in")
        g_vt_turned = sem("a_g_vt_turned")
        g_v_ready = sem("a_g_v_ready")
        g_s_done = sem("a_g_s_done")
        g_top_ok = sem("a_g_top_ok")
        g_shift_ok = sem("a_g_shift_ok")
        g_e_done = sem("a_g_e_done")
        g_inv_ok = sem("a_g_inv_ok")
        g_e_norm = sem("a_g_e_norm")
        g_et_done = sem("a_g_et_done")
        g_et_evac = sem("a_g_et_evac")
        g_pv_done = sem("a_g_pv_done")
        g_o_evac = sem("a_g_o_evac")
        g_ot_out = sem("a_g_ot_out")
        g_stored = sem("a_g_stored")
        g_x_in = sem("a_g_x_in")

        def sp_general(sp):
            prime(sp, g_stored)
            with sp.Fori(0, B) as b:
                sp.wait_ge(g_qkv_done, b * PAIRS * 6 + 1)
                sp.dma_start(xb[:, :, :], x_t[:, :, bass.ds(b * S, S)]).then_inc(g_x_in, 16)
                with sp.Fori(0, PAIRS) as p:
                    i = b * PAIRS + p
                    sp.wait_ge(g_qkv_done, i * 6 + 1)
                    sp.dma_start(w[:, :, :, :], w_qkv[p]).then_inc(g_w_in, 16)
                    sp.wait_ge(g_o_evac, i * UNITS + UNITS + 1)
                    sp.dma_start(attn_out[i], ot[:, :]).then_inc(g_ot_out, 16)
                    sp.wait_ge(g_ot_out, 16 * i + 16)
                    sp.nop().then_inc(g_stored, 1)

        def pe_general(pe):
            prime(pe, g_qkv_done, g_vt_turned, g_s_done, g_et_done, g_pv_done)
            pe.wait_ge(ident_ok, 2)
            with pe.Fori(0, B) as b:
                with pe.Fori(0, PAIRS) as p:
                    i = b * PAIRS + p
                    pe.wait_ge(g_x_in, 16 * b + 16)
                    pe.wait_ge(g_w_in, 16 * i + 16)
                    for c in range(6):
                        blk, n = c // NB, c % NB
                        pe.wait_ge(g_qkv_evac, i * 6 + max(c - 1, 0) + 1)
                        for kk in range(KD):
                            mm = pe.matmul(misc[c % 2][:, :], w[:, kk, blk, :],
                                           xb[:, kk, n * BANK:(n + 1) * BANK],
                                           start=kk == 0, stop=kk == KD - 1)
                        mm.then_inc(g_qkv_done, 1)
                    pe.wait_ge(g_qkv_evac, i * 6 + 6 + 1)
                    pe.wait_ge(g_et_evac, i * UNITS + 1)
                    for t in range(ST):
                        mm = pe.transpose(turned[t // 4][:, (t % 4) * P:(t % 4 + 1) * P],
                                          vt[:, t * P:(t + 1) * P], ident[:, :])
                    mm.then_inc(g_vt_turned, 1)
                    for h in range(2):
                        for st in range(ST):
                            g = i * UNITS + h * ST + st
                            pe.wait_ge(g_e_done, g + 1)
                            for n in range(NB):
                                mm = pe.matmul(scores[n][:, :], q[h][:, st * P:(st + 1) * P],
                                               k[h][:, n * BANK:(n + 1) * BANK], start=True, stop=True)
                            mm.then_inc(g_s_done, 1)
                            pe.wait_ge(g_e_norm, g + 1)
                            pe.wait_ge(g_v_ready, i + 1)
                            pe.wait_ge(g_et_evac, g + 1)
                            for t in range(ST):
                                mm = pe.transpose(turned[t // 4][:, (t % 4) * P:(t % 4 + 1) * P],
                                                  esum[0][:, t * P:(t + 1) * P], ident[:, :])
                            mm.then_inc(g_et_done, 1)
                            pe.wait_ge(g_et_evac, g + 2)
                            pe.wait_ge(g_o_evac, g + 1)
                            for t in range(ST):
                                mm = pe.matmul(o_ps[h * DH:(h + 1) * DH, 0:P], vst[:, t, h * DH:(h + 1) * DH],
                                               inv[:, t * P:(t + 1) * P], start=t == 0, stop=t == ST - 1)
                            mm.then_inc(g_pv_done, 1)

        def act_general(act):
            prime(act, g_qkv_evac, g_e_done, g_et_evac)
            with act.Fori(0, B) as b:
                with act.Fori(0, PAIRS) as p:
                    i = b * PAIRS + p
                    act.wait_ge(g_s_done, i * UNITS + 1)
                    for c in range(6):
                        blk, n = c // NB, c % NB
                        cols = slice(n * BANK, (n + 1) * BANK)
                        act.wait_ge(g_qkv_done, i * 6 + c + 2)
                        if blk < 2:
                            act.copy(q[blk][:, cols], misc[c % 2][0:DH, :])
                            act.copy(k[blk][:, cols], misc[c % 2][DH:P, :]).then_inc(g_qkv_evac, 1)
                        else:
                            act.wait_ge(g_vt_turned, i + 1)
                            act.copy(vt[:, cols], misc[c % 2][:, :]).then_inc(g_qkv_evac, 1)
                    for u in range(UNITS):
                        g = i * UNITS + u
                        act.wait_ge(g_shift_ok, g + 1)
                        act.wait_ge(g_et_done, g + 1)
                        act.activation(esum[0][:, :], banks.both[0], ACT.Exp, bias=shift[:, :], scale=SCALE,
                                       accum_out=total[:, :]).then_inc(g_e_done, 1)
                        act.wait_ge(g_et_done, g + 2)
                        act.wait_ge(g_pv_done, g + 1)
                        act.copy(inv[:, :], banks.both[1]).then_inc(g_et_evac, 1)

        def dve_general(dve):
            prime(dve, g_o_evac)
            with dve.Fori(0, B) as b:
                with dve.Fori(0, PAIRS) as p:
                    i = b * PAIRS + p
                    dve.wait_ge(g_vt_turned, i + 2)
                    dve.wait_ge(g_pv_done, i * UNITS + 1)
                    dve.tensor_copy(vst[:, :, :].rearrange("p a b -> p (a b)"), banks.both[1]).then_inc(g_v_ready, 1)
                    for h in range(2):
                        for st in range(ST):
                            g = i * UNITS + h * ST + st
                            dve.wait_ge(g_s_done, g + 2)
                            dve.tensor_reduce(top[:, :], banks.both[0], AX.X, ALU.max, negate=True)\
                               .then_inc(g_top_ok, 1)
                            dve.wait_ge(g_top_ok, g + 1)
                            dve.tensor_scalar(shift[:, :], top[:, :], SCALE, None, ALU.mult).then_inc(g_shift_ok, 1)
                            dve.wait_ge(g_e_done, g + 2)
                            dve.reciprocal(rcp[:, :], total[:, :]).then_inc(g_inv_ok, 1)
                            dve.wait_ge(g_inv_ok, g + 1)
                            dve.tensor_scalar(esum[0][:, :], esum[0][:, :], rcp[:, :], None, ALU.mult).then_inc(g_e_norm, 1)
                            dve.wait_ge(g_pv_done, g + 2)
                            dve.wait_ge(g_stored, i + 1)
                            dve.tensor_copy(ot[h * DH:(h + 1) * DH, st * P:(st + 1) * P],
                                            o_ps[h * DH:(h + 1) * DH, 0:P]).then_inc(g_o_evac, 1)

        block = ctx.enter_context(nc.Block())

        @block.sync
        def _(sp):
            flag = sp.value_load(bounded[0:1, 0:1], min_val=0, max_val=1)
            with sp.If(flag > 0):
                sp_bounded(sp)
            with sp.Else():
                sp_general(sp)

        @block.gpsimd
        def _(gp):
            gp.memset(ones[:, :], 1.0).then_inc(ones_ok, 1)
            make_identity(gp, ident, ident_ok)
            if POOL_EL:
                flag = gp.value_load(bounded[0:1, 0:1], min_val=0, max_val=1)
                with gp.If(flag > 0):
                    pool_bounded(gp)

        @block.tensor
        def _(pe):
            flag = pe.value_load(bounded[0:1, 0:1], min_val=0, max_val=1)
            with pe.If(flag > 0):
                pe_bounded(pe)
            with pe.Else():
                pe_general(pe)

        @block.scalar
        def _(act):
            flag = act.value_load(bounded[0:1, 0:1], min_val=0, max_val=1)
            with act.If(flag > 0):
                act_bounded(act)
            with act.Else():
                act_general(act)

        @block.vector
        def _(dve):
            flag = dve.value_load(bounded[0:1, 0:1], min_val=0, max_val=1)
            with dve.If(flag > 0):
                dve_bounded(dve)
            with dve.Else():
                dve_general(dve)


def tokens(nc, banks, keep, x_rows, attn_out, w_o, w_gs, shared_b):
    x2, shared, logits = keep["x2"], keep["shared"], keep["logits"]
    GS = D + E
    with ExitStack() as ctx:
        def sb(name, shape, dt=F32):
            return ctx.enter_context(nc.sbuf_tensor(name, shape, dt))

        def sem(name):
            return ctx.enter_context(nc.semaphore(name))

        ot = sb("t_ot", [P, 2, PAIRS, P])
        xr = sb("t_xr", [P, 2, D])
        wo = sb("t_wo", [P, PAIRS, D])
        wgs = sb("t_wgs", [P, KD, GS])
        sbias = sb("t_sbias", [P, D])
        stats = sb("t_stats", [P, TT, 6])
        mv = sb("t_mv", [P, TT, 2])
        var = sb("t_var", [P, TT])
        std = sb("t_std", [P, TT])
        rstd = sb("t_rstd", [P, TT])
        mean8 = sb("t_mean8", [P, ST])
        rstd8 = sb("t_rstd8", [P, ST])
        xn = sb("t_xn", [P, 2, D])
        x2t = sb("t_x2t", [P, 2, KD, P])
        pre = sb("t_pre", [P, 2, D])
        ident = sb("t_ident", [P, P])

        c_in, ident_ok = sem("t_c_in"), sem("t_ident_ok")
        ot_in = [sem(f"t_ot_in{u}") for u in range(2)]
        y_done, r_done = sem("t_y_done"), sem("t_r_done")
        stats_ok, mv_ok, var_ok = sem("t_stats_ok"), sem("t_mv_ok"), sem("t_var_ok")
        std_ok, rstd_ok = sem("t_std_ok"), sem("t_rstd_ok")
        m8_ok = sem("t_m8_ok")
        xn_ok, x2_ok, turned, x2t_ok, gs_done, pre_ok, sh_ok = (
            sem("t_" + n) for n in ("xn_ok", "x2_ok", "turned", "x2t_ok", "gs_done", "pre_ok", "sh_ok"))
        log_ok = sem("t_log_ok")
        block = ctx.enter_context(nc.Block())

        @block.sync
        def _(sp):
            sp.dma_start(wo[:, :, :], w_o).then_inc(c_in, 16)
            sp.dma_start(wgs[:, :, :], w_gs).then_inc(c_in, 16)
            sp.dma_start(sbias[:, :], shared_b.partition_broadcast(P)).then_inc(c_in, 16)
            with sp.Fori(0, B) as b:
                for st in range(ST):
                    u = st % 2
                    g = b * ST + st
                    if st >= 2:
                        sp.wait_ge(r_done, g + 0)
                    else:
                        sp.wait_ge(r_done, b * ST + 1)
                    sp.dma_start(ot[:, u, :, :], attn_out[bass.ds(b * PAIRS, PAIRS), :, st * P:(st + 1) * P]
                                 .rearrange("a p s -> p a s")).then_inc(ot_in[u], 16)
                    sp.dma_start(xr[:, u, :], x_rows[bass.ds(b * S + st * P, P), :]).then_inc(ot_in[u], 16)

        @block.gpsimd
        def _(gp):
            make_identity(gp, ident, ident_ok)

        @block.tensor
        def _(pe):
            prime(pe, turned)
            pe.wait_ge(c_in, 48)
            with pe.Fori(0, B) as b:
                for st in range(ST):
                    u = st % 2
                    g = b * ST + st
                    pe.wait_ge(ot_in[u], (b * (ST // 2) + st // 2 + 1) * 32)
                    if st >= 2:
                        pe.wait_ge(r_done, g + 0)
                    for a in range(PAIRS):
                        mm = pe.matmul(banks[u][:, 0:D], ot[:, u, a, :], wo[:, a, :], start=a == 0, stop=a == PAIRS - 1)
                    mm.then_inc(y_done, 1)
            pe.wait_ge(ident_ok, 2)
            with pe.Fori(0, B) as b:
                for st in range(ST):
                    u = st % 2
                    g = b * ST + st
                    pe.wait_ge(xn_ok, g + 2)
                    pe.wait_ge(x2t_ok, g + 1)
                    for kk in range(KD):
                        mm = pe.transpose(banks[2][:, kk * P:(kk + 1) * P], xn[:, u, kk * P:(kk + 1) * P], ident[:, :])
                    mm.then_inc(turned, 1)
                    pe.wait_ge(x2t_ok, g + 2)
                    pe.wait_ge(log_ok, g + 1)
                    for kk in range(KD):
                        mm = pe.matmul(banks[3][:, 0:GS], x2t[:, u, kk, :], wgs[:, kk, :], start=kk == 0, stop=kk == KD - 1)
                    mm.then_inc(gs_done, 1)

        @block.scalar
        def _(act):
            prime(act, x2_ok, x2t_ok, sh_ok)
            act.wait_ge(var_ok, 1)
            act.activation(std[:, :], var[:, :], ACT.Sqrt).then_inc(std_ok, 1)
            with act.Fori(0, B) as b:
                for st in range(ST):
                    u = st % 2
                    g = b * ST + st
                    act.wait_ge(xn_ok, g + 2)
                    act.copy(x2[:, bass.ds(g, 1), :].rearrange("p a d -> p (a d)"), xn[:, u, :]).then_inc(x2_ok, 1)
                    act.wait_ge(turned, g + 2)
                    act.copy(x2t[:, u, :, :].rearrange("p a b -> p (a b)"), banks[2][:, 0:D]).then_inc(x2t_ok, 1)
                    act.wait_ge(pre_ok, g + 1)
                    act.activation(shared[:, bass.ds(g, 1), :].rearrange("p a d -> p (a d)"), pre[:, u, :],
                                   ACT.Gelu).then_inc(sh_ok, 1)

        @block.vector
        def _(dve):
            prime(dve, r_done, log_ok, xn_ok)
            with dve.Fori(0, B) as b:
                for st in range(ST):
                    u = st % 2
                    g = b * ST + st
                    dve.wait_ge(y_done, g + 1)
                    dve.wait_ge(ot_in[u], (b * (ST // 2) + st // 2 + 1) * 32)
                    row = x2[:, bass.ds(g, 1), :].rearrange("p a d -> p (a d)")
                    dve.tensor_tensor(row, banks[u][:, 0:D], xr[:, u, :], ALU.add).then_inc(r_done, 1)
            dve.wait_ge(r_done, TT + 1)
            for t in range(TT):
                ins = dve.bn_stats(stats[:, t, :], x2[:, t, :])
            ins.then_inc(stats_ok, 1)
            dve.wait_ge(stats_ok, 1)
            for t in range(TT):
                ins = dve.bn_aggr(mv[:, t, :], stats[:, t, :])
            ins.then_inc(mv_ok, 1)
            dve.wait_ge(mv_ok, 1)
            dve.tensor_scalar(var[:, :], mv[:, :, 1], EPS, None, ALU.add).then_inc(var_ok, 1)
            dve.wait_ge(std_ok, 1)
            dve.reciprocal(rstd[:, :], std[:, :]).then_inc(rstd_ok, 1)
            dve.wait_ge(rstd_ok, 1)
            with dve.Fori(0, B) as b:
                dve.wait_ge(xn_ok, b * ST + 1)
                dve.tensor_copy(mean8[:, :], mv[:, bass.ds(b * ST, ST), 0]).then_inc(m8_ok, 1)
                dve.tensor_copy(rstd8[:, :], rstd[:, bass.ds(b * ST, ST)]).then_inc(m8_ok, 1)
                dve.wait_ge(m8_ok, b * 2 + 2)
                for st in range(ST):
                    u = st % 2
                    g = b * ST + st
                    if st >= 2:
                        dve.wait_ge(x2_ok, g + 0)
                        dve.wait_ge(turned, g + 0)
                    else:
                        dve.wait_ge(x2_ok, b * ST + 1)
                        dve.wait_ge(turned, b * ST + 1)
                    dve.tensor_scalar(xn[:, u, :], x2[:, bass.ds(g, 1), :].rearrange("p a d -> p (a d)"),
                                      mean8[:, st:st + 1], rstd8[:, st:st + 1], ALU.subtract, ALU.mult).then_inc(xn_ok, 1)
                    dve.wait_ge(gs_done, g + 1)
                    if st >= 2:
                        dve.wait_ge(sh_ok, g + 0)
                    else:
                        dve.wait_ge(sh_ok, b * ST + 1)
                    dve.tensor_tensor(pre[:, u, :], banks[3][:, 0:D], sbias[:, :], ALU.add).then_inc(pre_ok, 1)
                    dve.tensor_copy(logits[:, bass.ds(g, 1), :].rearrange("p a d -> p (a d)"),
                                    banks[3][:, D:GS]).then_inc(log_ok, 1)


def routing(nc, banks, keep):
    logits, w1, w2, slots, chunk_expert = (keep[n] for n in ("logits", "w1", "w2", "slots", "chunk_expert"))
    with ExitStack() as ctx:
        def sb(name, shape, dt=F32):
            return ctx.enter_context(nc.sbuf_tensor(name, shape, dt))

        def sem(name):
            return ctx.enter_context(nc.semaphore(name))

        first = sb("r_first", [P, E])
        best = [sb(f"r_best{j}", [P, TT]) for j in range(2)]
        eq = sb("r_eq", [P, TT, E])
        pref = sb("r_pref", [P, TT, E])
        ptop = sb("r_ptop", [P, TT])
        hot = [sb(f"r_hot{j}", [P, TT, E]) for j in range(2)]
        rest = sb("r_rest", [P, TT, E])
        gap = sb("r_gap", [P, TT])
        e2 = sb("r_e2", [P, TT])
        den = sb("r_den", [P, TT])
        chosen = sb("r_chosen", [P, TT, E])
        before = sb("r_before", [P, P])
        ones = sb("r_ones", [P, P])
        cnt = sb("r_cnt", [P, TT, E])
        run = [sb(f"r_run{j}", [P, TT, E]) for j in range(2)]
        nch = sb("r_nch", [P, E])
        ends = [sb(f"r_ends{j}", [P, E]) for j in range(2)]
        base = sb("r_base", [P, E])
        slot = sb("r_slot", [P, TT, E])
        pick = sb("r_pick", [P, TT, E])
        slotf = sb("r_slotf", [P, TT])
        cidx = sb("r_cidx", [1, NCHUNK, E])
        past = sb("r_past", [1, NCHUNK, E])
        cexp = sb("r_cexp", [1, NCHUNK])
        consts_ok, chain, m_ok, counted, gap_ok, e2_ok = (
            sem("r_" + n) for n in ("consts_ok", "chain", "m_ok", "counted", "gap_ok", "e2_ok"))
        block = ctx.enter_context(nc.Block())

        def over_experts(a):
            return a[:, :].unsqueeze(2).to_broadcast([P, TT, E])

        def over_tiles(a):
            return a[:, :].unsqueeze(1).to_broadcast([P, TT, E])

        @block.gpsimd
        def _(gp):
            gp.memset(ones[:, :], 1.0).then_inc(consts_ok, 1)
            gp.wait_ge(consts_ok, 1)
            gp.affine_select(out=before[:, :], in_=ones[:, :], compare_op=ALU.is_ge, fill=0.0, base=-1,
                             pattern=[[1, P]], channel_multiplier=-1).then_inc(consts_ok, 1)
            for e in range(E):
                gp.memset(first[:, e:e + 1], float(E - e)).then_inc(consts_ok, 1)
            for c in range(NCHUNK):
                gp.memset(cidx[:, c, :], float(c)).then_inc(consts_ok, 1)

        @block.tensor
        def _(pe):
            pe.wait_ge(m_ok, 1)
            flat = chosen[:, :, :].rearrange("p a b -> p (a b)")
            pe.matmul(banks[0][:, 0:TT * E], before[:, :], flat, start=True, stop=True)
            pe.matmul(banks[1][:, 0:TT * E], ones[:, :], flat, start=True, stop=True).then_inc(counted, 1)

        @block.scalar
        def _(act):
            act.wait_ge(gap_ok, 1)
            act.activation(e2[:, :], gap[:, :], ACT.Exp).then_inc(e2_ok, 1)

        @block.vector
        def _(dve):
            steps = [0]

            def link(ins):
                steps[0] += 1
                ins.then_inc(chain, 1)
                dve.wait_ge(chain, steps[0])

            dve.wait_ge(consts_ok, 2 + E + NCHUNK)
            left = logits
            for j in range(2):
                link(dve.tensor_reduce(best[j][:, :], left[:, :, :], AX.X, ALU.max))
                link(dve.tensor_tensor(eq[:, :, :], left[:, :, :], over_experts(best[j]), ALU.is_equal))
                link(dve.tensor_tensor(pref[:, :, :], eq[:, :, :], over_tiles(first), ALU.mult))
                link(dve.tensor_reduce(ptop[:, :], pref[:, :, :], AX.X, ALU.max))
                link(dve.tensor_tensor(hot[j][:, :, :], pref[:, :, :], over_experts(ptop), ALU.is_equal))
                if j == 0:
                    link(dve.scalar_tensor_tensor(rest[:, :, :], hot[0][:, :, :], NEVER, logits[:, :, :],
                                                  ALU.mult, ALU.add))
                    left = rest
            dve.tensor_tensor(gap[:, :], best[1][:, :], best[0][:, :], ALU.subtract).then_inc(gap_ok, 1)
            dve.tensor_tensor(chosen[:, :, :], hot[0][:, :, :], hot[1][:, :, :], ALU.add).then_inc(m_ok, 1)
            dve.wait_ge(e2_ok, 1)
            link(dve.tensor_scalar(den[:, :], e2[:, :], 1.0, None, ALU.add))
            link(dve.reciprocal(w1[:, :], den[:, :]))
            link(dve.tensor_tensor(w2[:, :], e2[:, :], w1[:, :], ALU.mult))
            dve.wait_ge(counted, 1)
            link(dve.tensor_copy(cnt[:, :, :].rearrange("p a b -> p (a b)"), banks[1][:, 0:TT * E]))
            src, n, step = cnt, 0, 1
            while step < TT:
                dst = run[n % 2]
                link(dve.tensor_tensor(dst[:, step:TT, :], src[:, step:TT, :], src[:, 0:TT - step, :], ALU.add))
                link(dve.tensor_copy(dst[:, 0:step, :], src[:, 0:step, :]))
                src, n, step = dst, n + 1, 2 * step
            total = src[:, TT - 1, :]
            link(dve.tensor_scalar(nch[:, :], total, 1.0 / CHUNK, 0.5 - 0.5 / CHUNK, ALU.mult, ALU.add))
            link(dve.tensor_scalar(nch[:, :], nch[:, :], 1.5 * 2.0 ** 23, None, ALU.add))
            link(dve.tensor_scalar(nch[:, :], nch[:, :], -1.5 * 2.0 ** 23, None, ALU.add))
            esrc, n, step = nch, 0, 1
            while step < E:
                dst = ends[n % 2]
                link(dve.tensor_tensor(dst[:, step:E], esrc[:, step:E], esrc[:, 0:E - step], ALU.add))
                link(dve.tensor_copy(dst[:, 0:step], esrc[:, 0:step]))
                esrc, n, step = dst, n + 1, 2 * step
            link(dve.tensor_tensor(base[:, :], esrc[:, :], nch[:, :], ALU.subtract))
            link(dve.tensor_scalar(base[:, :], base[:, :], float(CHUNK), None, ALU.mult))
            link(dve.tensor_tensor(slot[:, :, :], src[:, :, :], cnt[:, :, :], ALU.subtract))
            link(dve.tensor_tensor(slot[:, :, :], slot[:, :, :], over_tiles(base), ALU.add))
            link(dve.tensor_tensor(slot[:, :, :], slot[:, :, :],
                                   banks[0][:, 0:TT * E].rearrange("p (a b) -> p a b", b=E), ALU.add))
            for j in range(2):
                link(dve.tensor_tensor(pick[:, :, :], slot[:, :, :], hot[j][:, :, :], ALU.mult))
                link(dve.tensor_reduce(slotf[:, :], pick[:, :, :], AX.X, ALU.add))
                link(dve.tensor_copy(slots[:, j, :], slotf[:, :]))
            link(dve.tensor_tensor(past[:, :, :], cidx[:, :, :],
                                   esrc[0:1, :].unsqueeze(1).to_broadcast([1, NCHUNK, E]), ALU.is_ge))
            link(dve.tensor_reduce(cexp[:, :], past[:, :, :], AX.X, ALU.add))
            link(dve.tensor_scalar(cexp[:, :], cexp[:, :], float(E - 1), None, ALU.min))
            link(dve.tensor_copy(chunk_expert[:, :], cexp[:, :]))


def experts(nc, banks, keep, w_exp, b2, rows_in, rows_out):
    x2, slots, chunk_expert = keep["x2"], keep["slots"], keep["chunk_expert"]
    with ExitStack() as ctx:
        def sb(name, shape, dt=F32):
            return ctx.enter_context(nc.sbuf_tensor(name, shape, dt))

        def sem(name):
            return ctx.enter_context(nc.semaphore(name))

        w = sb("e_w", [P, 2, WX])
        b2r = sb("e_b2r", [P, 2, D])
        xg = sb("e_xg", [P, 2, CT, D])
        xgt = sb("e_xgt", [P, 2, KD, CHUNK])
        ht = sb("e_ht", [P, 2, HB, CHUNK])
        y = sb("e_y", [P, 2, CT, D])
        ident = sb("e_ident", [P, P])
        zero = sb("e_zero", [P, 2048])
        ident_ok, zero_ok, cleared, placed = (sem("e_" + n) for n in ("ident_ok", "zero_ok", "cleared", "placed"))
        scattered = sem("e_scattered")
        chunk_in = [sem(f"e_chunk_in{u}") for u in range(2)]
        turned, xgt_ok, h_done, h_ok, y_done, y_ok = (
            sem("e_" + n) for n in ("turned", "xgt_ok", "h_done", "h_ok", "y_done", "y_ok"))
        y_out, y_stored = sem("e_y_out"), sem("e_y_stored")
        block = ctx.enter_context(nc.Block())
        W1 = [[w[:, u, kk * HID:(kk + 1) * HID] for kk in range(KD)] for u in range(2)]
        W2 = [[w[:, u, KD * HID + hb * D:KD * HID + (hb + 1) * D] for hb in range(HB)] for u in range(2)]
        B1 = [w[:, u, KD * HID + HB * D:WX] for u in range(2)]

        @block.gpsimd
        def _(gp):
            prime(gp, y_stored)
            make_identity(gp, ident, ident_ok)
            gp.memset(zero[:, :], 0.0).then_inc(zero_ok, 1)
            gp.wait_ge(cleared, 16)
            for t in range(TT):
                for j in range(2):
                    gp.indirect_dma_start(
                        out=rows_in, out_offset=bass.IndirectOffsetOnAxis(ap=slots[:, j, t:t + 1], axis=0),
                        in_=x2[:, t, :], in_offset=None).then_inc(placed, 16)
            gp.wait_ge(placed, 16 * 2 * TT)
            gp.nop().then_inc(scattered, 1)

        @block.sync
        def _(sp):
            sp.wait_ge(zero_ok, 1)
            per = SLOTS * D // P
            z = rows_in.rearrange("(p a) d -> p (a d)", p=P)
            n = 0
            sp.dma_start(z.rearrange("p (a c) -> p a c", c=2048),
                         zero[:, :].unsqueeze(1).to_broadcast([P, per // 2048, 2048])).then_inc(cleared, 16)
            sp.wait_ge(scattered, 1)
            with sp.Fori(0, NCHUNK // 2) as c2:
                for u in range(2):
                    c = c2 * 2 + u
                    sp.wait_ge(y_ok, c2 * 2 * CT + 1)
                    ex = sp.value_load(chunk_expert[0:1, bass.ds(c, 1)], min_val=0, max_val=E - 1)
                    sp.dma_start(xg[:, u, :, :], rows_in[bass.ds(c * CHUNK, CHUNK), :]
                                 .rearrange("(a p) d -> p a d", p=P)).then_inc(chunk_in[u], 16)
                    sp.dma_start(w[:, u, :], w_exp[bass.ds(ex, 1)].rearrange("a p n -> p (a n)")).then_inc(chunk_in[u], 16)
                    sp.dma_start(b2r[:, u, :], b2[bass.ds(ex, 1), :].rearrange("a n -> (a n)").partition_broadcast(P))\
                      .then_inc(chunk_in[u], 16)

        @block.tensor
        def _(pe):
            pe.wait_ge(ident_ok, 2)
            with pe.Fori(0, NCHUNK // 2) as c2:
                for u in range(2):
                    c = c2 * 2 + u
                    pe.wait_ge(chunk_in[u], (c2 + 1) * 48)
                    pe.wait_ge(xgt_ok, c + 1)
                    for kk in range(KD):
                        for a in range(CT):
                            mm = pe.transpose(banks[0][:, kk * CHUNK + a * P:kk * CHUNK + (a + 1) * P],
                                              xg[:, u, a, kk * P:(kk + 1) * P], ident[:, :])
                    mm.then_inc(turned, 1)
                    pe.wait_ge(xgt_ok, c + 2)
                    for hb in range(HB):
                        pe.wait_ge(h_ok, c * HB + max(hb - 1, 0) + 1)
                        for kk in range(KD):
                            mm = pe.matmul(banks[1 + hb % 2][:, 0:CHUNK], W1[u][kk][:, hb * P:(hb + 1) * P],
                                           xgt[:, u, kk, :], start=kk == 0, stop=kk == KD - 1)
                        mm.then_inc(h_done, 1)
                    pe.wait_ge(h_ok, c * HB + HB + 1)
                    for a in range(CT):
                        pe.wait_ge(y_ok, c * CT + max(a - 1, 0) + 1)
                        for hb in range(HB):
                            mm = pe.matmul(banks[3 + a % 2][:, 0:D], ht[:, u, hb, a * P:(a + 1) * P], W2[u][hb],
                                           start=hb == 0, stop=hb == HB - 1)
                        mm.then_inc(y_done, 1)

        @block.scalar
        def _(act):
            prime(act, xgt_ok, h_ok)
            with act.Fori(0, NCHUNK // 2) as c2:
                for u in range(2):
                    c = c2 * 2 + u
                    act.wait_ge(turned, c + 1)
                    act.copy(xgt[:, u, :, :].rearrange("p a b -> p (a b)"), banks[0][:, 0:KD * CHUNK]).then_inc(xgt_ok, 1)
                    act.wait_ge(chunk_in[u], (c2 + 1) * 48)
                    for hb in range(HB):
                        act.wait_ge(h_done, c * HB + hb + 1)
                        act.activation(ht[:, u, hb, :], banks[1 + hb % 2][:, 0:CHUNK], ACT.Gelu,
                                       bias=B1[u][:, hb:hb + 1]).then_inc(h_ok, 1)

        @block.vector
        def _(dve):
            prime(dve, y_ok)
            with dve.Fori(0, NCHUNK // 2) as c2:
                for u in range(2):
                    c = c2 * 2 + u
                    dve.wait_ge(chunk_in[u], (c2 + 1) * 48)
                    dve.wait_ge(y_stored, c + 1)
                    for a in range(CT):
                        dve.wait_ge(y_done, c * CT + a + 1)
                        dve.tensor_tensor(y[:, u, a, :], banks[3 + a % 2][:, 0:D], b2r[:, u, :], ALU.add).then_inc(y_ok, 1)

        @block.gpsimd
        def _(gp):
            with gp.Fori(0, NCHUNK // 2) as c2:
                for u in range(2):
                    c = c2 * 2 + u
                    gp.wait_ge(y_ok, c * CT + CT + 1)
                    gp.dma_start(rows_out[bass.ds(c * CHUNK, CHUNK), :].rearrange("(a p) d -> p a d", p=P),
                                 y[:, u, :, :]).then_inc(y_out, 16)
                    gp.wait_ge(y_out, 16 * c + 16)
                    gp.nop().then_inc(y_stored, 1)


def outputs(nc, banks, keep, gamma, beta, rows_out, out):
    x2, shared, w1, w2, slots = (keep[n] for n in ("x2", "shared", "w1", "w2", "slots"))
    with ExitStack() as ctx:
        def sb(name, shape, dt=F32):
            return ctx.enter_context(nc.sbuf_tensor(name, shape, dt))

        def sem(name):
            return ctx.enter_context(nc.semaphore(name))

        g = sb("o_g", [P, D])
        bt = sb("o_b", [P, D])
        y1 = sb("o_y1", [P, TT, D])
        y2 = sb("o_y2", [P, 8, D])
        stats = sb("o_stats", [P, TT, 6])
        mv = sb("o_mv", [P, TT, 2])
        std = sb("o_std", [P, 2, TT])
        c_in = sem("o_c_in")
        in1 = [sem(f"o_in1_{i}") for i in range(8)]
        in2 = [sem(f"o_in2_{i}") for i in range(8)]
        used, chain, var_ok, std_ok, done = (sem("o_" + n) for n in ("used", "chain", "var_ok", "std_ok", "done"))
        out_sem = sem("o_out")
        block = ctx.enter_context(nc.Block())

        @block.gpsimd
        def _(gp):
            for t in range(TT):
                if t >= 8:
                    gp.wait_ge(used, t - 7)
                gp.indirect_dma_start(out=y1[:, t, :], out_offset=None, in_=rows_out,
                                      in_offset=bass.IndirectOffsetOnAxis(ap=slots[:, 0, t:t + 1], axis=0))\
                  .then_inc(in1[t % 8], 16)
                gp.indirect_dma_start(out=y2[:, t % 8, :], out_offset=None, in_=rows_out,
                                      in_offset=bass.IndirectOffsetOnAxis(ap=slots[:, 1, t:t + 1], axis=0))\
                  .then_inc(in2[t % 8], 16)

        @block.sync
        def _(sp):
            sp.dma_start(g[:, :], gamma.partition_broadcast(P)).then_inc(c_in, 16)
            sp.dma_start(bt[:, :], beta.partition_broadcast(P)).then_inc(c_in, 16)
            sp.wait_ge(done, 1)
            sp.dma_start(out.rearrange("b s d -> (b s) d").rearrange("(t p) d -> p t d", p=P), y1[:, :, :]).then_inc(out_sem, 16)
            sp.wait_ge(out_sem, 16)

        @block.scalar
        def _(act):
            for n in range(2):
                act.wait_ge(var_ok, n + 1)
                act.activation(std[:, n, :], mv[:, :, 1], ACT.Sqrt).then_inc(std_ok, 1)

        @block.vector
        def _(dve):
            steps = [0]

            def stage(instructions):
                for ins in instructions:
                    last = ins
                steps[0] += 1
                last.then_inc(chain, 1)
                dve.wait_ge(chain, steps[0])

            def normed(n):
                stage(dve.bn_stats(stats[:, t, :], y1[:, t, :]) for t in range(TT))
                stage(dve.bn_aggr(mv[:, t, :], stats[:, t, :]) for t in range(TT))
                dve.tensor_scalar(mv[:, :, 1], mv[:, :, 1], EPS, None, ALU.add).then_inc(var_ok, 1)
                dve.wait_ge(std_ok, n + 1)
                stage([dve.reciprocal(std[:, n, :], std[:, n, :])])
                stage(dve.tensor_scalar(y1[:, t, :], y1[:, t, :], mv[:, t, 0:1], std[:, n, t:t + 1],
                                        ALU.subtract, ALU.mult) for t in range(TT))

            for t in range(TT):
                dve.wait_ge(in1[t % 8], 16 * (t // 8 + 1))
                stage([dve.tensor_scalar(y1[:, t, :], y1[:, t, :], w1[:, t:t + 1], None, ALU.mult)])
                dve.wait_ge(in2[t % 8], 16 * (t // 8 + 1))
                stage([dve.scalar_tensor_tensor(y1[:, t, :], y2[:, t % 8, :], w2[:, t:t + 1], y1[:, t, :],
                                                ALU.mult, ALU.add)])
                dve.scalar_tensor_tensor(y1[:, t, :], shared[:, t, :], 0.5, y1[:, t, :], ALU.mult, ALU.add)\
                   .then_inc(used, 1)
            dve.wait_ge(used, TT)
            normed(0)
            dve.wait_ge(c_in, 32)
            rows = [slice(t, t + 8) for t in range(0, TT, 8)]
            stage(dve.tensor_tensor(y1[:, r, :], y1[:, r, :], g[:, :].unsqueeze(1).to_broadcast([P, 8, D]), ALU.mult)
                  for r in rows)
            stage(dve.tensor_tensor(y1[:, r, :], y1[:, r, :], bt[:, :].unsqueeze(1).to_broadcast([P, 8, D]), ALU.add)
                  for r in rows)
            stage(dve.tensor_tensor(y1[:, r, :], y1[:, r, :], x2[:, r, :], ALU.add) for r in rows)
            normed(1)
            dve.nop().then_inc(done, 1)


class Banks:

    def __init__(self, ps):
        self.ps = ps
        self.both = [ps[:, 2 * i * BANK:2 * (i + 1) * BANK] for i in range(4)]

    def __getitem__(self, i):
        if isinstance(i, slice):
            return [self[j] for j in range(*i.indices(8))]
        return self.ps[:, i * BANK:(i + 1) * BANK]


def layer(nc, x_t, x_rows, w_qkv, w_o, w_exp, b2, w_gs, shared_b, gamma, beta, out):
    attn_out = nc.dram_tensor("attn_out", [B * PAIRS, P, S], F32, kind="Internal").ap()
    inv_row = nc.dram_tensor("inv_row", [S], F32, kind="Internal").ap()
    rows_in = nc.dram_tensor("rows_in", [SLOTS, D], F32, kind="Internal").ap()
    rows_out = nc.dram_tensor("rows_out", [SLOTS, D], F32, kind="Internal").ap()
    with ExitStack() as ctx:
        banks = Banks(ctx.enter_context(nc.psum_tensor("banks", [P, 8 * BANK], F32)))
        keep = {"bounded": ctx.enter_context(nc.sbuf_tensor("bounded", [1, 1], I32))}
        score_bound(nc, banks, keep, x_rows, w_qkv)
        attention(nc, banks, keep, x_t, w_qkv, inv_row, attn_out)
        keep |= {name: ctx.enter_context(nc.sbuf_tensor(name, shape, dt)) for name, shape, dt in (
            ("x2", [P, TT, D], F32), ("shared", [P, TT, D], F32), ("logits", [P, TT, E], F32),
            ("w1", [P, TT], F32), ("w2", [P, TT], F32), ("slots", [P, 2, TT], U32),
            ("chunk_expert", [1, NCHUNK], I32))}
        tokens(nc, banks, keep, x_rows, attn_out, w_o, w_gs, shared_b)
        routing(nc, banks, keep)
        experts(nc, banks, keep, w_exp, b2, rows_in, rows_out)
        outputs(nc, banks, keep, gamma, beta, rows_out, out)


def kernel(L0_attn_x, L0_attn_kernel, L0_attn_WO, L0_ffn_W1, L0_ffn_b1, L0_ffn_W2, L0_ffn_b2, L0_ffn_gate_W,
           L0_ffn_shared_W, L0_ffn_shared_b, L0_ffn_gamma, L0_ffn_beta):
    import numpy as np
    import concourse.bacc as bacc
    from concourse.bass_utils import run_bass_kernel_spmd

    x = np.asarray(L0_attn_x)
    wk = np.asarray(L0_attn_kernel).reshape(3, PAIRS, 2, KD, P, DH)
    qk = wk[0:2].transpose(1, 4, 3, 2, 0, 5).reshape(PAIRS, P, KD, 2, P)
    vv = wk[2].transpose(0, 3, 2, 1, 4).reshape(PAIRS, P, KD, 1, P)
    w1 = np.asarray(L0_ffn_W1).reshape(E, KD, P, HID).transpose(0, 2, 1, 3).reshape(E, P, KD * HID)
    w2 = np.asarray(L0_ffn_W2).reshape(E, HB, P, D).transpose(0, 2, 1, 3).reshape(E, P, HB * D)
    b1 = np.asarray(L0_ffn_b1).reshape(E, HB, P).transpose(0, 2, 1)
    gs = np.concatenate([np.asarray(L0_ffn_shared_W), np.asarray(L0_ffn_gate_W)], axis=1)
    arrays = {
        "x_t": x.reshape(T, KD, P).transpose(2, 1, 0),
        "x_rows": x.reshape(T, D),
        "w_qkv": np.concatenate([qk, vv], axis=3),
        "w_o": np.asarray(L0_attn_WO).reshape(DH, PAIRS, 2, D).transpose(2, 0, 1, 3).reshape(P, PAIRS, D),
        "w_exp": np.concatenate([w1, w2, b1], axis=2),
        "b2": np.asarray(L0_ffn_b2),
        "w_gs": gs.reshape(KD, P, D + E).transpose(1, 0, 2),
        "shared_b": np.asarray(L0_ffn_shared_b),
        "gamma": np.asarray(L0_ffn_gamma),
        "beta": np.asarray(L0_ffn_beta),
    }
    arrays = {name: np.ascontiguousarray(a) for name, a in arrays.items()}
    nc = bacc.Bacc("TRN2", target_bir_lowering=False, num_devices=1)
    args = [nc.dram_tensor(name, a.shape, mybir.dt.from_np(a.dtype), kind="ExternalInput").ap()
            for name, a in arrays.items()]
    out = nc.dram_tensor("out", [B, S, D], F32, kind="ExternalOutput").ap()
    layer(nc, *args, out)
    return run_bass_kernel_spmd(nc, [arrays], core_ids=[0]).results[0]["out"]
```

```python
from contextlib import ExitStack

import concourse.bass as bass
from concourse import mybir

F32 = mybir.dt.float32
I32 = mybir.dt.int32
U32 = mybir.dt.uint32
ALU = mybir.AluOpType
ACT = mybir.ActivationFunctionType
AX = mybir.AxisListType

P = 128
B, S, D = 4, 1024, 256
H, DH = 16, 64
E, HID, TOPK = 8, 1024, 2
T = B * S
KD = D // P
PAIRS = H // 2
ST = S // P
TT = T // P
BANK = 512
NB = S // BANK
HB = HID // P
SCALE = 1.0 / (DH * DH * H)
EPS = 1e-5
CHUNK = 256
CT = CHUNK // P
NCHUNK = (TOPK * T + E * (CHUNK - 1)) // CHUNK
NCHUNK += NCHUNK % 2
AHEAD = 2
PLANNED = NCHUNK + AHEAD
EXPERT, NEW, USED = range(3)
NEVER = -3.0e38
LIMIT = 40.0
INVERT_AT = 4
DIVIDE_AT = 1
SUM_TURN = 2
TV_AT, QK_AT, SPLIT_QK_AT, VT_AT = 0, 2, 3, 6
DIRECT = 1
LAG = 3
POOL_EL = ()


def prime(engine, *semaphores):
    for semaphore in semaphores:
        engine.nop().then_inc(semaphore, 1)


def make_identity(gpsimd, tile, done):
    gpsimd.memset(tile[:, :], 0.0).then_inc(done, 1)
    gpsimd.wait_ge(done, 1)
    gpsimd.affine_select(out=tile[:, :], in_=tile[:, :], compare_op=ALU.not_equal, fill=1.0, base=0,
                         pattern=[[-1, P]], channel_multiplier=1).then_inc(done, 1)


def score_bound(nc, banks, keep, x_rows, w_qkv):
    bounded = keep["bounded"]
    QK = PAIRS * 4
    with ExitStack() as ctx:
        def sb(name, shape, dt=F32):
            return ctx.enter_context(nc.sbuf_tensor(name, shape, dt))

        def sem(name):
            return ctx.enter_context(nc.semaphore(name))

        xr = sb("b_xr", [P, TT, D])
        wr = sb("b_wr", [P, PAIRS, KD * 3 * P])
        xx = sb("b_xx", [P, TT])
        xm = sb("b_xm", [P, P])
        wsq = sb("b_wsq", [P, KD, QK, DH])
        ww = sb("b_ww", [P, KD, QK])
        junk = sb("b_junk", [P, 2, D])
        ones = sb("b_ones", [P, P])
        ident = sb("b_ident", [P, P])
        xtop = sb("b_xtop", [1, 1])
        wtot = sb("b_wtot", [1, 2, QK])
        wsum = sb("b_wsum", [1, QK])
        wprod = sb("b_wprod", [1, QK // 2])
        wtop = sb("b_wtop", [1, 1])
        b1 = sb("b_b1", [1, 1])
        b2 = sb("b_b2", [1, 1])
        b3 = sb("b_b3", [1, 1])
        flag = sb("b_flag", [1, 1])
        x_in, w_in, ident_ok, ones_ok = sem("b_x_in"), sem("b_w_in"), sem("b_ident_ok"), sem("b_ones_ok")
        xx_ok, ww_ok, xx_turned, ww_summed, chain = (
            sem("b_" + n) for n in ("xx_ok", "ww_ok", "xx_turned", "ww_summed", "chain"))
        block = ctx.enter_context(nc.Block())

        @block.sync
        def _(sp):
            sp.dma_start(xr[:, :, :], x_rows.rearrange("(t p) d -> p t d", p=P)).then_inc(x_in, 16)

        @block.scalar
        def _(act):
            act.dma_start(wr[:, :, :], w_qkv.rearrange("a p k b c -> p a (k b c)")).then_inc(w_in, 16)
            act.wait_ge(w_in, 16)
            w6 = wr[:, :, :].rearrange("p a (k b c) -> p k a b c", k=KD, b=3)
            for kk in range(KD):
                for a in range(PAIRS):
                    ins = act.activation(wsq[:, kk, 4 * a:4 * a + 4, :].rearrange("p (b g) c -> p b (g c)", b=2),
                                         w6[:, kk, a, 0:2, :], ACT.Square)
            ins.then_inc(ww_ok, 1)

        @block.gpsimd
        def _(gp):
            gp.memset(ones[:, :], 1.0).then_inc(ones_ok, 1)
            make_identity(gp, ident, ident_ok)

        @block.tensor
        def _(pe):
            pe.wait_ge(ident_ok, 2)
            pe.wait_ge(ones_ok, 1)
            pe.wait_ge(xx_ok, 1)
            pe.transpose(banks[0][:, 0:P], xm[:, :], ident[:, :]).then_inc(xx_turned, 1)
            pe.wait_ge(ww_ok, 2)
            pe.matmul(banks[1][:, 0:KD * QK], ones[:, :], ww[:, :, :].rearrange("p a b -> p (a b)"),
                      start=True, stop=True).then_inc(ww_summed, 1)

        @block.vector
        def _(dve):
            steps = [0]

            def link(ins):
                steps[0] += 1
                ins.then_inc(chain, 1)
                dve.wait_ge(chain, steps[0])

            dve.wait_ge(x_in, 16)
            link(dve.memset(xm[:, :], 0.0))
            for t in range(TT):
                link(dve.tensor_tensor_reduce(out=junk[:, t % 2, :], in0=xr[:, t, :], in1=xr[:, t, :], scale=1.0,
                                              scalar=0.0, op0=ALU.mult, op1=ALU.add, accum_out=xx[:, t:t + 1]))
            dve.tensor_reduce(xm[:, 0:1], xx[:, :], AX.X, ALU.max).then_inc(xx_ok, 1)
            dve.wait_ge(ww_ok, 1)
            dve.tensor_reduce(ww[:, :, :], wsq[:, :, :, :], AX.X, ALU.add).then_inc(ww_ok, 1)
            dve.wait_ge(xx_turned, 1)
            link(dve.tensor_reduce(xtop[:, :], banks[0][0:1, 0:P], AX.X, ALU.max))
            dve.wait_ge(ww_summed, 1)
            link(dve.tensor_copy(wtot[:, :, :].rearrange("p a b -> p (a b)"), banks[1][0:1, 0:KD * QK]))
            link(dve.tensor_tensor(wsum[:, :], wtot[:, 0, :], wtot[:, 1, :], ALU.add))
            pair = wsum[:, :].rearrange("p (a two) -> p a two", two=2)
            link(dve.tensor_tensor(wprod[:, :], pair[:, :, 0], pair[:, :, 1], ALU.mult))
            link(dve.tensor_reduce(wtop[:, :], wprod[:, :], AX.X, ALU.max))
            link(dve.tensor_scalar(b1[:, :], xtop[:, :], SCALE, None, ALU.mult))
            link(dve.tensor_tensor(b2[:, :], b1[:, :], b1[:, :], ALU.mult))
            link(dve.tensor_tensor(b3[:, :], b2[:, :], wtop[:, :], ALU.mult))
            link(dve.tensor_scalar(flag[:, :], b3[:, :], LIMIT * LIMIT, None, ALU.is_le))
            link(dve.tensor_copy(bounded[:, :], flag[:, :]))


def attention(nc, banks, keep, x_t, w_qkv, inv_row, attn_out):
    UNITS = 2 * ST
    SLOTS_ = B * H
    NE = 4
    ADDS = ST - 1 - DIRECT
    R32 = mybir.dt.float32r
    with ExitStack() as ctx:
        def sb(name, shape, dt=F32):
            return ctx.enter_context(nc.sbuf_tensor(name, shape, dt))

        def sem(name):
            return ctx.enter_context(nc.semaphore(name))

        xh = sb("a_xh", [P, KD, T], R32)
        xl = sb("a_xl", [P, KD, T], R32)
        w = sb("a_w", [P, KD, 3, P])
        wh = sb("a_wh", [P, KD, 3, P], R32)
        wl = sb("a_wl", [P, KD, 3, P], R32)
        qa = [sb(f"a_qa{j}", [P, S], R32) for j in range(2)]
        ka = [sb(f"a_ka{j}", [P, S], R32) for j in range(2)]
        kb = [sb(f"a_kb{j}", [P, S], R32) for j in range(2)]
        e = [sb(f"a_e{j}", [P, S]) for j in range(NE)]
        eh = [sb(f"a_eh{j}", [P, S], R32) for j in range(NE)]
        el = [sb(f"a_el{j}", [P, S], R32) for j in range(NE)]
        vv = [sb(f"a_vv{h}", [P, ST, 2, DH], R32) for h in range(2)]
        vt = sb("a_vt", [P, S])
        vst = sb("a_vst", [P, ST, P])
        esum = [sb(f"a_esum{j}", [P, S]) for j in range(2)]
        inv = sb("a_inv", [P, S])
        srow = sb("a_srow", [1, S])
        scol = sb("a_scol", [P, S // P])
        icol = sb("a_icol", [P, S // P])
        ob = sb("a_ob", [DH, S])
        osum = sb("a_osum", [DH, S])
        ot = sb("a_ot", [P, S])
        xb = sb("a_xb", [P, KD, S])
        ones = sb("a_ones", [P, DH])
        ones_r = sb("a_ones_r", [P, DH], R32)
        ident = sb("a_ident", [P, P])
        small = sb("a_small", [P, 4])
        ring, proj, o_acc = banks.both[0:2], banks.both[2], banks.both[3]
        bounded = keep["bounded"]

        ident_ok, ones_ok = sem("a_ident_ok"), sem("a_ones_ok")
        x_in = [sem(f"a_x_in{j}") for j in range(NE)]
        xh_ok, xl_ok, w_in, wh_ok, wl_ok = (sem("a_" + n) for n in ("xh_ok", "xl_ok", "w_in", "wh_ok", "wl_ok"))
        qk_done, qk_hi, qk_lo = sem("a_qk_done"), sem("a_qk_hi"), sem("a_qk_lo")
        kh_dup, kl_dup = ([sem(f"a_{name}_dup{j}") for j in range(2)] for name in ("kh", "kl"))
        vt_done, vt_ok, tv_done, vst_ok = (sem("a_" + n) for n in ("vt_done", "vt_ok", "tv_done", "vst_ok"))
        v_ok = [sem(f"a_v_ok{h}") for h in range(2)]
        s_done, e_ok, eh_ok, acc_ok, pv_done = (sem("a_" + n) for n in ("s_done", "e_ok", "eh_ok", "acc_ok", "pv_done"))
        v_hi, stored = sem("a_v_hi"), sem("a_stored")
        el_ok = {"dve": sem("a_el_dve"), "pool": sem("a_el_pool")}
        r_done, srow_ok, row_spread, col_in, icol_ok, icol_out, icol_stored, inv_in, ob_ok, osum_ok, ot_ok, ot_out = (
            sem("a_" + n) for n in ("r_done", "srow_ok", "row_spread", "col_in", "icol_ok", "icol_out",
                                     "icol_stored", "inv_in", "ob_ok", "osum_ok", "ot_ok", "ot_out"))

        def turn(h, position):
            return ring[(h * (ST + 1) + position) % 2]

        def members(who):
            return [n for n in range(ST) if (n in POOL_EL) == (who == "pool")]

        def wait_el(eng, slot, n):
            who = "pool" if n in POOL_EL else "dve"
            mine = members(who)
            eng.wait_ge(el_ok[who], slot * len(mine) + mine.index(n) + 1)

        def make_el(eng, slot, n, first):
            who = "pool" if n in POOL_EL else "dve"
            eng.wait_ge(eh_ok, slot * ST + n + 1)
            if not (first and n < NE):
                eng.wait_ge(pv_done, slot * ST + n - NE + 1)
            eng.tensor_tensor(el[n % NE][:, :], e[n % NE][:, :], eh[n % NE][:, :].bitcast(F32), ALU.subtract)\
               .then_inc(el_ok[who], 1)

        def sp_bounded(sp):
            prime(sp, stored, row_spread, icol_stored)
            for j in range(T // BANK):
                if j >= NE:
                    sp.wait_ge(xl_ok, j - NE + 1)
                sp.dma_start(e[j % NE][:, :].rearrange("p (k s) -> p k s", k=KD),
                             x_t[:, :, j * BANK:(j + 1) * BANK]).then_inc(x_in[j % NE], 16)

            def dup(slot, j):
                sp.wait_ge(qk_hi, slot * 2 + 2)
                sp.dma_start(ka[j][0:DH, :].bitcast(F32), ka[j][DH:P, :].bitcast(F32)).then_inc(kh_dup[j], 16)
                sp.wait_ge(qk_lo, slot + 1)
                sp.dma_start(kb[j][0:DH, :].bitcast(F32), kb[j][DH:P, :].bitcast(F32)).then_inc(kl_dup[j], 16)

            def spread(slot):
                sp.wait_ge(srow_ok, slot + 1)
                sp.dma_start(scol[:, :], srow[:, :]).then_inc(col_in, 16)
                sp.wait_ge(col_in, 16 * slot + 16)
                sp.nop().then_inc(row_spread, 1)

            def broadcast(slot):
                sp.wait_ge(icol_ok, slot + 1)
                sp.dma_start(inv_row.rearrange("(p c) -> p c", p=P), icol[:, :]).then_inc(icol_out, 16)
                sp.wait_ge(icol_out, 16 * slot + 16)
                sp.nop().then_inc(icol_stored, 1)
                sp.wait_ge(ot_ok, slot + 1)
                sp.dma_start(inv[0:DH, :], inv_row.partition_broadcast(DH)).then_inc(inv_in, 16)
                sp.wait_ge(inv_in, 16 * slot + 16)

            def weights(n, pair):
                if n is not None:
                    sp.wait_ge(wl_ok, n)
                sp.dma_start(w[:, :, :, :], w_qkv[pair]).then_inc(w_in, 16)

            def store(pair):
                sp.wait_ge(ot_ok, pair * 2 + 3)
                sp.dma_start(attn_out[pair], ot[:, :]).then_inc(ot_out, 16)
                sp.wait_ge(ot_out, 16 * pair + 16)
                sp.nop().then_inc(stored, 1)

            weights(None, 0)
            dup(0, 0)
            weights(1, 1)
            dup(1, 1)
            with sp.Fori(0, B * PAIRS - 1) as i:
                weights(i + 2, (i + 2) % PAIRS)
                spread(2 * i)
                dup(2 * i + 2, 0)
                broadcast(2 * i)
                spread(2 * i + 1)
                dup(2 * i + 3, 1)
                broadcast(2 * i + 1)
                store(i)
            spread(SLOTS_ - 2)
            broadcast(SLOTS_ - 2)
            spread(SLOTS_ - 1)
            broadcast(SLOTS_ - 1)
            store(B * PAIRS - 1)

        def pe_bounded(pe):
            def project(blk, b, half):
                cols = bass.ds(b * S + half * BANK, BANK)
                parts = [(wt[:, kk, blk, :], xs[:, kk, cols]) for kk in range(KD)
                         for wt, xs in ((wh, xh), (wh, xl), (wl, xh))]
                for m, (lhs, rhs) in enumerate(parts):
                    mm = pe.matmul(proj[:, half * BANK:(half + 1) * BANK], lhs, rhs, start=m == 0,
                                   stop=m == len(parts) - 1)
                return mm

            def project_qk(slot, h, b, half):
                if half == 0:
                    pe.wait_ge(wl_ok, (slot + 1) // 2 + 1)
                    if h:
                        pe.wait_ge(vst_ok, slot // 2 + 1)
                    else:
                        pe.wait_ge(qk_lo, slot + 1)
                mm = project(h, b, half)
                if half:
                    mm.then_inc(qk_done, 1)

            def project_v(pair, b, half):
                if half == 0:
                    pe.wait_ge(qk_lo, pair * 2 + 1)
                mm = project(2, b, half)
                if half:
                    mm.then_inc(vt_done, 1)

            def turn_v(pair):
                pe.wait_ge(vt_ok, pair + 1)
                for t in range(ST):
                    mm = pe.transpose(proj[:, t * P:(t + 1) * P], vt[:, t * P:(t + 1) * P], ident[:, :])
                mm.then_inc(tv_done, 1)

            def sums(slot, h, last=False):
                pe.wait_ge(acc_ok, slot * ADDS + ADDS)
                if not last:
                    pe.wait_ge(e_ok, (slot + 1) * ST + 1)
                out = turn(1 - h, SUM_TURN)[0:DH, :]
                for m in range(NB):
                    pe.matmul(out[:, m * BANK:(m + 1) * BANK], ones[:, :], esum[h][:, m * BANK:(m + 1) * BANK],
                              start=True, stop=False, skip_group_check=True)
                for n in range(ST - DIRECT, ST):
                    for part in (eh, el):
                        if part is eh:
                            pe.wait_ge(eh_ok, slot * ST + n + 1)
                        else:
                            wait_el(pe, slot, n)
                        for m in range(NB):
                            mm = pe.matmul(out[:, m * BANK:(m + 1) * BANK], ones_r[:, :],
                                           part[n % NE][:, m * BANK:(m + 1) * BANK], start=False,
                                           stop=n == ST - 1 and part is el, skip_group_check=True)
                mm.then_inc(r_done, 1)

            def scores(slot, h, n, first):
                if n == 0:
                    pe.wait_ge(qk_lo, slot + 1)
                    pe.wait_ge(kh_dup[h], (slot // 2) * 16 + 16)
                if n in (0, 1) or n > 3:
                    if not (first and n < 2):
                        pe.wait_ge(e_ok, slot * ST + n - 1)
                elif n == 2:
                    pe.wait_ge(e_ok, slot * ST + 2)
                elif not first:
                    pe.wait_ge(srow_ok, slot)
                tile = turn(h, n + (n >= SUM_TURN))
                for part, (start, stop) in ((ka, (True, False)), (kb, (False, True))):
                    if n == 0 and part is kb:
                        pe.wait_ge(kl_dup[h], (slot // 2) * 16 + 16)
                    for m in range(NB):
                        mm = pe.matmul(tile[:, m * BANK:(m + 1) * BANK], part[h][:, n * P:(n + 1) * P],
                                       qa[h][:, m * BANK:(m + 1) * BANK], start=start, stop=stop,
                                       skip_group_check=True)
                mm.then_inc(s_done, 1)

            def values(slot, h, n, first=False):
                if n == 0:
                    pe.wait_ge(v_ok[h], slot // 2 + 1)
                    if not first:
                        pe.wait_ge(osum_ok, slot)
                pe.wait_ge(eh_ok, slot * ST + n + 1)
                lhs = vv[h][:, n, :, :].rearrange("p a d -> p (a d)")
                for part in (eh, el):
                    if part is el:
                        wait_el(pe, slot, n)
                    for m in range(NB):
                        mm = pe.matmul(o_acc[:, m * BANK:(m + 1) * BANK], lhs, part[n % NE][:, m * BANK:(m + 1) * BANK],
                                       start=n == 0 and part is eh, stop=n == ST - 1 and part is el,
                                       skip_group_check=True)
                mm.then_inc(pv_done, 1)

            def slot_program(slot, h, b, first=False, last=False):
                for n in range(ST):
                    scores(slot, h, n, first)
                    if n == 1 and not first:
                        sums(slot - 1, 1 - h)
                    if n == QK_AT + 1 and not last:
                        project_qk(slot, 1 - h, b, 1)
                    if n >= LAG:
                        values(slot, h, n - LAG, first)
                    elif not first:
                        values(slot - 1, 1 - h, ST - LAG + n)
                    if n == TV_AT and not h:
                        turn_v(slot // 2)
                    if n == QK_AT and not last:
                        project_qk(slot, 1 - h, b, 0)
                    if n in (VT_AT, VT_AT + 1) and h and not last:
                        project_v(slot // 2 + 1, b, n - VT_AT)

            pe.wait_ge(ident_ok, 2)
            pe.wait_ge(ones_ok, 2)
            pe.wait_ge(xl_ok, T // BANK)
            pe.wait_ge(wl_ok, 1)
            for half in range(2):
                mm = project(0, 0, half)
            mm.then_inc(qk_done, 1)
            for half in range(2):
                project_v(0, 0, half)
            slot_program(0, 0, 0, first=True)
            with pe.Fori(0, B * PAIRS - 1) as i:
                b = (i + 1) // PAIRS
                slot_program(2 * i + 1, 1, b)
                slot_program(2 * i + 2, 0, b)
            slot_program(SLOTS_ - 1, 1, 0, last=True)
            for n in range(ST - LAG, ST):
                values(SLOTS_ - 1, 1, n)
            pe.wait_ge(e_ok, SLOTS_ * ST)
            sums(SLOTS_ - 1, 1, last=True)

        def act_bounded(act):
            for j in range(T // BANK):
                act.wait_ge(x_in[j % NE], 16 * (j // NE + 1))
                act.copy(xh[:, :, j * BANK:(j + 1) * BANK],
                         e[j % NE][:, :].rearrange("p (k s) -> p k s", k=KD)).then_inc(xh_ok, 1)

            def weights(n):
                act.wait_ge(w_in, 16 * n)
                act.copy(wh[:, :, :, :], w[:, :, :, :]).then_inc(wh_ok, 1)

            def qk_high(slot, j):
                act.wait_ge(qk_done, slot + 1)
                act.copy(qa[j][0:DH, :], proj[0:DH, :]).then_inc(qk_hi, 1)
                act.copy(ka[j][DH:P, :], proj[DH:P, :]).then_inc(qk_hi, 1)

            def v_turned(pair):
                act.wait_ge(vt_done, pair + 1)
                act.copy(vt[:, :], proj).then_inc(vt_ok, 1)

            def v_rows(pair):
                act.wait_ge(tv_done, pair + 1)
                act.copy(vst[:, :, :].rearrange("p a b -> p (a b)"), proj).then_inc(vst_ok, 1)

            def probs(slot, h, n, first):
                act.wait_ge(s_done, slot * ST + n + 1)
                if not (first and n < NE):
                    before = slot if n >= NE else slot - 1
                    m = (n - NE) % ST
                    wait_el(act, before, m)
                    act.wait_ge(acc_ok, before * ADDS + min(max(m, 1), ADDS))
                act.activation(e[n % NE][:, :], turn(h, n + (n >= SUM_TURN)), ACT.Exp, scale=SCALE).then_inc(e_ok, 1)

            def high(slot, n, first=False):
                act.wait_ge(e_ok, slot * ST + n + 1)
                if not (first and n < NE):
                    act.wait_ge(pv_done, slot * ST + n - NE + 1)
                act.copy(eh[n % NE][:, :], e[n % NE][:, :]).then_inc(eh_ok, 1)

            def o_low(slot):
                act.wait_ge(pv_done, slot * ST + ST)
                act.copy(ob[:, :], o_acc[DH:P, :]).then_inc(ob_ok, 1)

            def sum_row(slot, h):
                act.wait_ge(r_done, slot + 1)
                act.wait_ge(row_spread, slot + 1)
                act.copy(srow[:, :], turn(1 - h, SUM_TURN)[0:1, :]).then_inc(srow_ok, 1)

            def slot_program(slot, h, first=False, last=False):
                for n in range(ST):
                    if n == SUM_TURN and not first:
                        sum_row(slot - 1, 1 - h)
                    if n == 0 and not h and not first:
                        v_turned(slot // 2)
                    probs(slot, h, n, first)
                    if n == LAG - 1 and not first:
                        o_low(slot - 1)
                    if n >= 1:
                        high(slot, n - 1, first)
                    elif not first:
                        high(slot - 1, ST - 1)
                    if n == TV_AT + 1 and not h:
                        v_rows(slot // 2)
                    if n == SPLIT_QK_AT and not last:
                        qk_high(slot + 1, 1 - h)
                        if not h:
                            weights(slot // 2 + 2)

            weights(1)
            qk_high(0, 0)
            v_turned(0)
            slot_program(0, 0, first=True)
            with act.Fori(0, B * PAIRS - 1) as i:
                slot_program(2 * i + 1, 1)
                slot_program(2 * i + 2, 0)
            slot_program(SLOTS_ - 1, 1, last=True)
            high(SLOTS_ - 1, ST - 1)
            o_low(SLOTS_ - 1)
            sum_row(SLOTS_ - 1, 1)

        def dve_bounded(dve):
            for j in range(T // BANK):
                dve.wait_ge(xh_ok, j + 1)
                cols = slice(j * BANK, (j + 1) * BANK)
                dve.tensor_tensor(xl[:, :, cols], e[j % NE][:, :].rearrange("p (k s) -> p k s", k=KD),
                                  xh[:, :, cols].bitcast(F32), ALU.subtract).then_inc(xl_ok, 1)

            def weights(n):
                dve.wait_ge(wh_ok, n)
                dve.tensor_tensor(wl[:, :, :, :], w[:, :, :, :], wh[:, :, :, :].bitcast(F32), ALU.subtract)\
                   .then_inc(wl_ok, 1)

            def qk_low(slot, j):
                dve.wait_ge(qk_hi, slot * 2 + 1)
                dve.tensor_tensor(qa[j][DH:P, :], proj[0:DH, :], qa[j][0:DH, :].bitcast(F32), ALU.subtract)
                dve.wait_ge(qk_hi, slot * 2 + 2)
                dve.tensor_tensor(kb[j][DH:P, :], proj[DH:P, :], ka[j][DH:P, :].bitcast(F32), ALU.subtract)\
                   .then_inc(qk_lo, 1)

            def split_v(slot, h):
                if h == 0:
                    dve.wait_ge(vst_ok, slot // 2 + 1)
                part = vst[:, :, h * DH:(h + 1) * DH]
                dve.tensor_copy(vv[h][:, :, 0, :], part).then_inc(v_hi, 1)
                dve.wait_ge(v_hi, slot + h + 1)
                dve.tensor_tensor(vv[h][:, :, 1, :], part, vv[h][:, :, 0, :].bitcast(F32), ALU.subtract)\
                   .then_inc(v_ok[h], 1)

            def add(slot, h, n):
                acc = esum[h][:, :]
                if n == 1:
                    dve.tensor_tensor(acc, e[0][:, :], e[1][:, :], ALU.add).then_inc(acc_ok, 1)
                else:
                    dve.wait_ge(acc_ok, slot * ADDS + n - 1)
                    dve.tensor_tensor(acc, acc, e[n % NE][:, :], ALU.add).then_inc(acc_ok, 1)

            def o_sum(slot):
                dve.wait_ge(ob_ok, slot + 1)
                dve.wait_ge(ot_ok, slot + 1)
                dve.tensor_tensor(osum[:, :], o_acc[0:DH, :], ob[:, :], ALU.add).then_inc(osum_ok, 1)

            def invert(slot):
                dve.wait_ge(col_in, 16 * slot + 16)
                dve.wait_ge(icol_stored, slot + 1)
                dve.reciprocal(icol[:, :], scol[:, :]).then_inc(icol_ok, 1)

            def divide(slot, h):
                dve.wait_ge(osum_ok, slot + 1)
                dve.wait_ge(inv_in, 16 * slot + 16)
                if h == 0:
                    dve.wait_ge(stored, slot // 2 + 1)
                dve.tensor_tensor(ot[h * DH:(h + 1) * DH, :], osum[:, :], inv[0:DH, :], ALU.mult).then_inc(ot_ok, 1)

            def slot_program(slot, h, first=False, second=False, last=False):
                for n in range(ST):
                    if n == LAG - 1 and not first:
                        o_sum(slot - 1)
                    if n == DIVIDE_AT and not first and not second:
                        divide(slot - 2, h)
                    if n >= 1:
                        make_el(dve, slot, n - 1, first)
                        if n <= ADDS:
                            dve.wait_ge(e_ok, slot * ST + n + 1)
                            add(slot, h, n)
                    elif not first:
                        make_el(dve, slot - 1, ST - 1, False)
                    if n == TV_AT + 1 and not h:
                        split_v(slot, 0)
                    if n == TV_AT + 3 and not h:
                        split_v(slot, 1)
                    if n == SPLIT_QK_AT and not last:
                        qk_low(slot + 1, 1 - h)
                        if not h:
                            weights(slot // 2 + 2)
                    if n == INVERT_AT and not first:
                        invert(slot - 1)

            prime(dve, ot_ok)
            dve.wait_ge(ones_ok, 1)
            dve.tensor_copy(ones_r[:, :], ones[:, :]).then_inc(ones_ok, 1)
            weights(1)
            qk_low(0, 0)
            slot_program(0, 0, first=True)
            slot_program(1, 1, second=True)
            with dve.Fori(1, B * PAIRS - 1) as i:
                slot_program(2 * i, 0)
                slot_program(2 * i + 1, 1)
            slot_program(SLOTS_ - 2, 0)
            slot_program(SLOTS_ - 1, 1, last=True)
            divide(SLOTS_ - 2, 0)
            make_el(dve, SLOTS_ - 1, ST - 1, False)
            o_sum(SLOTS_ - 1)
            invert(SLOTS_ - 1)
            divide(SLOTS_ - 1, 1)

        def pool_bounded(gp):
            def slot_program(slot, first=False):
                for n in POOL_EL:
                    make_el(gp, slot, n, first)

            if POOL_EL:
                slot_program(0, first=True)
                with gp.Fori(1, SLOTS_) as slot:
                    slot_program(slot)

        q = [e[h][0:DH, :] for h in range(2)]
        k = [e[2 + h][0:DH, :] for h in range(2)]
        top, shift, total, rcp = (small[:, n:n + 1] for n in range(4))
        scores, turned, misc, o_ps = banks[0:2], banks[2:4], banks[4:6], banks[6]
        g_qkv_done = sem("a_g_qkv_done")
        g_qkv_evac = sem("a_g_qkv_evac")
        g_w_in = sem("a_g_w_in")
        g_vt_turned = sem("a_g_vt_turned")
        g_v_ready = sem("a_g_v_ready")
        g_s_done = sem("a_g_s_done")
        g_top_ok = sem("a_g_top_ok")
        g_shift_ok = sem("a_g_shift_ok")
        g_e_done = sem("a_g_e_done")
        g_inv_ok = sem("a_g_inv_ok")
        g_e_norm = sem("a_g_e_norm")
        g_et_done = sem("a_g_et_done")
        g_et_evac = sem("a_g_et_evac")
        g_pv_done = sem("a_g_pv_done")
        g_o_evac = sem("a_g_o_evac")
        g_ot_out = sem("a_g_ot_out")
        g_stored = sem("a_g_stored")
        g_x_in = sem("a_g_x_in")

        def sp_general(sp):
            prime(sp, g_stored)
            with sp.Fori(0, B) as b:
                sp.wait_ge(g_qkv_done, b * PAIRS * 6 + 1)
                sp.dma_start(xb[:, :, :], x_t[:, :, bass.ds(b * S, S)]).then_inc(g_x_in, 16)
                with sp.Fori(0, PAIRS) as p:
                    i = b * PAIRS + p
                    sp.wait_ge(g_qkv_done, i * 6 + 1)
                    sp.dma_start(w[:, :, :, :], w_qkv[p]).then_inc(g_w_in, 16)
                    sp.wait_ge(g_o_evac, i * UNITS + UNITS + 1)
                    sp.dma_start(attn_out[i], ot[:, :]).then_inc(g_ot_out, 16)
                    sp.wait_ge(g_ot_out, 16 * i + 16)
                    sp.nop().then_inc(g_stored, 1)

        def pe_general(pe):
            prime(pe, g_qkv_done, g_vt_turned, g_s_done, g_et_done, g_pv_done)
            pe.wait_ge(ident_ok, 2)
            with pe.Fori(0, B) as b:
                with pe.Fori(0, PAIRS) as p:
                    i = b * PAIRS + p
                    pe.wait_ge(g_x_in, 16 * b + 16)
                    pe.wait_ge(g_w_in, 16 * i + 16)
                    for c in range(6):
                        blk, n = c // NB, c % NB
                        pe.wait_ge(g_qkv_evac, i * 6 + max(c - 1, 0) + 1)
                        for kk in range(KD):
                            mm = pe.matmul(misc[c % 2][:, :], w[:, kk, blk, :],
                                           xb[:, kk, n * BANK:(n + 1) * BANK],
                                           start=kk == 0, stop=kk == KD - 1)
                        mm.then_inc(g_qkv_done, 1)
                    pe.wait_ge(g_qkv_evac, i * 6 + 6 + 1)
                    pe.wait_ge(g_et_evac, i * UNITS + 1)
                    for t in range(ST):
                        mm = pe.transpose(turned[t // 4][:, (t % 4) * P:(t % 4 + 1) * P],
                                          vt[:, t * P:(t + 1) * P], ident[:, :])
                    mm.then_inc(g_vt_turned, 1)
                    for h in range(2):
                        for st in range(ST):
                            g = i * UNITS + h * ST + st
                            pe.wait_ge(g_e_done, g + 1)
                            for n in range(NB):
                                mm = pe.matmul(scores[n][:, :], q[h][:, st * P:(st + 1) * P],
                                               k[h][:, n * BANK:(n + 1) * BANK], start=True, stop=True)
                            mm.then_inc(g_s_done, 1)
                            pe.wait_ge(g_e_norm, g + 1)
                            pe.wait_ge(g_v_ready, i + 1)
                            pe.wait_ge(g_et_evac, g + 1)
                            for t in range(ST):
                                mm = pe.transpose(turned[t // 4][:, (t % 4) * P:(t % 4 + 1) * P],
                                                  esum[0][:, t * P:(t + 1) * P], ident[:, :])
                            mm.then_inc(g_et_done, 1)
                            pe.wait_ge(g_et_evac, g + 2)
                            pe.wait_ge(g_o_evac, g + 1)
                            for t in range(ST):
                                mm = pe.matmul(o_ps[h * DH:(h + 1) * DH, 0:P], vst[:, t, h * DH:(h + 1) * DH],
                                               inv[:, t * P:(t + 1) * P], start=t == 0, stop=t == ST - 1)
                            mm.then_inc(g_pv_done, 1)

        def act_general(act):
            prime(act, g_qkv_evac, g_e_done, g_et_evac)
            with act.Fori(0, B) as b:
                with act.Fori(0, PAIRS) as p:
                    i = b * PAIRS + p
                    act.wait_ge(g_s_done, i * UNITS + 1)
                    for c in range(6):
                        blk, n = c // NB, c % NB
                        cols = slice(n * BANK, (n + 1) * BANK)
                        act.wait_ge(g_qkv_done, i * 6 + c + 2)
                        if blk < 2:
                            act.copy(q[blk][:, cols], misc[c % 2][0:DH, :])
                            act.copy(k[blk][:, cols], misc[c % 2][DH:P, :]).then_inc(g_qkv_evac, 1)
                        else:
                            act.wait_ge(g_vt_turned, i + 1)
                            act.copy(vt[:, cols], misc[c % 2][:, :]).then_inc(g_qkv_evac, 1)
                    for u in range(UNITS):
                        g = i * UNITS + u
                        act.wait_ge(g_shift_ok, g + 1)
                        act.wait_ge(g_et_done, g + 1)
                        act.activation(esum[0][:, :], banks.both[0], ACT.Exp, bias=shift[:, :], scale=SCALE,
                                       accum_out=total[:, :]).then_inc(g_e_done, 1)
                        act.wait_ge(g_et_done, g + 2)
                        act.wait_ge(g_pv_done, g + 1)
                        act.copy(inv[:, :], banks.both[1]).then_inc(g_et_evac, 1)

        def dve_general(dve):
            prime(dve, g_o_evac)
            with dve.Fori(0, B) as b:
                with dve.Fori(0, PAIRS) as p:
                    i = b * PAIRS + p
                    dve.wait_ge(g_vt_turned, i + 2)
                    dve.wait_ge(g_pv_done, i * UNITS + 1)
                    dve.tensor_copy(vst[:, :, :].rearrange("p a b -> p (a b)"), banks.both[1]).then_inc(g_v_ready, 1)
                    for h in range(2):
                        for st in range(ST):
                            g = i * UNITS + h * ST + st
                            dve.wait_ge(g_s_done, g + 2)
                            dve.tensor_reduce(top[:, :], banks.both[0], AX.X, ALU.max, negate=True)\
                               .then_inc(g_top_ok, 1)
                            dve.wait_ge(g_top_ok, g + 1)
                            dve.tensor_scalar(shift[:, :], top[:, :], SCALE, None, ALU.mult).then_inc(g_shift_ok, 1)
                            dve.wait_ge(g_e_done, g + 2)
                            dve.reciprocal(rcp[:, :], total[:, :]).then_inc(g_inv_ok, 1)
                            dve.wait_ge(g_inv_ok, g + 1)
                            dve.tensor_scalar(esum[0][:, :], esum[0][:, :], rcp[:, :], None, ALU.mult).then_inc(g_e_norm, 1)
                            dve.wait_ge(g_pv_done, g + 2)
                            dve.wait_ge(g_stored, i + 1)
                            dve.tensor_copy(ot[h * DH:(h + 1) * DH, st * P:(st + 1) * P],
                                            o_ps[h * DH:(h + 1) * DH, 0:P]).then_inc(g_o_evac, 1)

        block = ctx.enter_context(nc.Block())

        @block.sync
        def _(sp):
            flag = sp.value_load(bounded[0:1, 0:1], min_val=0, max_val=1)
            with sp.If(flag > 0):
                sp_bounded(sp)
            with sp.Else():
                sp_general(sp)

        @block.gpsimd
        def _(gp):
            gp.memset(ones[:, :], 1.0).then_inc(ones_ok, 1)
            make_identity(gp, ident, ident_ok)
            if POOL_EL:
                flag = gp.value_load(bounded[0:1, 0:1], min_val=0, max_val=1)
                with gp.If(flag > 0):
                    pool_bounded(gp)

        @block.tensor
        def _(pe):
            flag = pe.value_load(bounded[0:1, 0:1], min_val=0, max_val=1)
            with pe.If(flag > 0):
                pe_bounded(pe)
            with pe.Else():
                pe_general(pe)

        @block.scalar
        def _(act):
            flag = act.value_load(bounded[0:1, 0:1], min_val=0, max_val=1)
            with act.If(flag > 0):
                act_bounded(act)
            with act.Else():
                act_general(act)

        @block.vector
        def _(dve):
            flag = dve.value_load(bounded[0:1, 0:1], min_val=0, max_val=1)
            with dve.If(flag > 0):
                dve_bounded(dve)
            with dve.Else():
                dve_general(dve)


def tokens(nc, banks, keep, x_rows, attn_out, w_o, w_gs, shared_b, x2_rows):
    x2, shared, logits = keep["x2"], keep["shared"], keep["logits"]
    GS = D + E
    HALF = ST // 2
    with ExitStack() as ctx:
        def sb(name, shape, dt=F32):
            return ctx.enter_context(nc.sbuf_tensor(name, shape, dt))

        def sem(name):
            return ctx.enter_context(nc.semaphore(name))

        ot = [sb(f"t_ot{u}", [P, PAIRS, HALF * P]) for u in range(2)]
        xr = [sb(f"t_xr{u}", [P, HALF, D]) for u in range(2)]
        wo = sb("t_wo", [P, PAIRS, D])
        wgs = sb("t_wgs", [P, KD, GS])
        sbias = sb("t_sbias", [P, D])
        rt = sb("t_rt", [P, ST, D])
        xn = sb("t_xn", [P, ST, D])
        stats = sb("t_stats", [P, ST, 6])
        mv = sb("t_mv", [P, ST, 2])
        var = sb("t_var", [P, ST])
        std = sb("t_std", [P, ST])
        rstd = sb("t_rstd", [P, ST])
        x2t = [sb(f"t_x2t{u}", [P, KD, P]) for u in range(2)]
        pre = [sb(f"t_pre{u}", [P, D]) for u in range(2)]
        ident = sb("t_ident", [P, P])
        c_in, ident_ok, rows_out = sem("t_c_in"), sem("t_ident_ok"), sem("t_rows_out")
        ot_in = [sem(f"t_ot_in{u}") for u in range(2)]
        y_done, r_done, stats_ok, mv_ok, var_ok, std_ok, rstd_ok = (
            sem("t_" + n) for n in ("y_done", "r_done", "stats_ok", "mv_ok", "var_ok", "std_ok", "rstd_ok"))
        xn_ok, x2_ok, turned, x2t_ok, gs_done, pre_ok, log_ok, sh_ok = (
            sem("t_" + n) for n in ("xn_ok", "x2_ok", "turned", "x2t_ok", "gs_done", "pre_ok", "log_ok", "sh_ok"))
        block = ctx.enter_context(nc.Block())

        def two_before(engine, done, b, st):
            engine.wait_ge(done, b * ST + (st if st >= 2 else 1))

        @block.sync
        def _(sp):
            def load(b, u):
                sp.dma_start(ot[u][:, :, :], attn_out[bass.ds(b * PAIRS, PAIRS), :, u * HALF * P:(u + 1) * HALF * P]
                             .rearrange("a p s -> p a s")).then_inc(ot_in[u], 16)
                sp.dma_start(xr[u][:, :, :], x_rows[bass.ds(b * S + u * HALF * P, HALF * P), :]
                             .rearrange("(t p) d -> p t d", p=P)).then_inc(ot_in[u], 16)

            sp.dma_start(wo[:, :, :], w_o).then_inc(c_in, 16)
            load(0, 0)
            sp.dma_start(wgs[:, :, :], w_gs).then_inc(c_in, 16)
            sp.dma_start(sbias[:, :], shared_b.partition_broadcast(P)).then_inc(c_in, 16)
            load(0, 1)
            with sp.Fori(1, B) as b:
                for u in range(2):
                    sp.wait_ge(r_done, b * ST - ST + (u + 1) * HALF)
                    load(b, u)

        @block.gpsimd
        def _(gp):
            make_identity(gp, ident, ident_ok)
            with gp.Fori(0, B) as b:
                gp.wait_ge(xn_ok, b * ST + ST)
                gp.dma_start(x2_rows[bass.ds(b * S, S), :].rearrange("(t p) d -> p t d", p=P), xn[:, :, :])\
                  .then_inc(rows_out, 16)
            gp.wait_ge(rows_out, 16 * B)

        @block.tensor
        def _(pe):
            def project(b, st, first=False):
                pe.wait_ge(ot_in[st // HALF], b * 32 + 32)
                if not (first and st < 2):
                    pe.wait_ge(r_done, b * ST + st - 1)
                cols = slice(st % HALF * P, (st % HALF + 1) * P)
                for a in range(PAIRS):
                    mm = pe.matmul(banks[st % 2][:, 0:D], ot[st // HALF][:, a, cols], wo[:, a, :], start=a == 0,
                                   stop=a == PAIRS - 1)
                mm.then_inc(y_done, 1)

            def turn(b, st):
                pe.wait_ge(xn_ok, b * ST + st + 1)
                two_before(pe, x2t_ok, b, st)
                for kk in range(KD):
                    mm = pe.transpose(banks[2 + st % 2][:, kk * P:(kk + 1) * P], xn[:, st, kk * P:(kk + 1) * P],
                                      ident[:, :])
                mm.then_inc(turned, 1)

            def branch(b, st):
                pe.wait_ge(x2t_ok, b * ST + st + 2)
                two_before(pe, log_ok, b, st)
                for kk in range(KD):
                    mm = pe.matmul(banks[4 + st % 2][:, 0:GS], x2t[st % 2][:, kk, :], wgs[:, kk, :], start=kk == 0,
                                   stop=kk == KD - 1)
                mm.then_inc(gs_done, 1)

            pe.wait_ge(c_in, 48)
            pe.wait_ge(ident_ok, 2)
            for st in range(ST):
                project(0, st, first=True)
            with pe.Fori(1, B) as b:
                for st in range(ST):
                    turn(b - 1, st)
                    project(b, st)
                    branch(b - 1, st)
            for st in range(ST):
                turn(B - 1, st)
                if st:
                    branch(B - 1, st - 1)
            branch(B - 1, ST - 1)

        @block.scalar
        def _(act):
            def deviation(b):
                act.wait_ge(var_ok, b + 1)
                act.activation(std[:, :], var[:, :], ACT.Sqrt).then_inc(std_ok, 1)

            def batch(b):
                for st in range(ST + 1):
                    if st < ST:
                        g = b * ST + st
                        act.wait_ge(turned, g + 1)
                        act.copy(x2t[st % 2][:, :, :].rearrange("p a b -> p (a b)"), banks[2 + st % 2][:, 0:D])\
                           .then_inc(x2t_ok, 1)
                        act.copy(x2[:, bass.ds(g, 1), :].rearrange("p a d -> p (a d)"), xn[:, st, :]).then_inc(x2_ok, 1)
                    if st:
                        g = b * ST + st - 1
                        act.wait_ge(pre_ok, g + 1)
                        act.activation(shared[:, bass.ds(g, 1), :].rearrange("p a d -> p (a d)"), pre[(st - 1) % 2][:, :],
                                       ACT.Gelu).then_inc(sh_ok, 1)

            prime(act, x2t_ok, sh_ok)
            deviation(0)
            with act.Fori(1, B) as b:
                batch(b - 1)
                deviation(b)
            batch(B - 1)

        @block.vector
        def _(dve):
            def add(b, st):
                dve.wait_ge(y_done, b * ST + st + 1)
                dve.wait_ge(ot_in[st // HALF], b * 32 + 32)
                dve.tensor_tensor(rt[:, st, :], banks[st % 2][:, 0:D], xr[st // HALF][:, st % HALF, :], ALU.add)\
                   .then_inc(r_done, 1)

            def statistics(b, st):
                dve.wait_ge(r_done, b * ST + st + 1)
                dve.bn_stats(stats[:, st, :], rt[:, st, :]).then_inc(stats_ok, 1)

            def biased(b, st):
                g = b * ST + st
                dve.wait_ge(gs_done, g + 1)
                two_before(dve, sh_ok, b, st)
                dve.tensor_tensor(pre[st % 2][:, :], banks[4 + st % 2][:, 0:D], sbias[:, :], ALU.add).then_inc(pre_ok, 1)
                dve.tensor_copy(logits[:, bass.ds(g, 1), :].rearrange("p a d -> p (a d)"),
                                banks[4 + st % 2][:, D:GS]).then_inc(log_ok, 1)

            def normalize(b, first=False):
                for st in range(ST):
                    ins = dve.bn_aggr(mv[:, st, :], stats[:, st, :])
                ins.then_inc(mv_ok, 1)
                dve.wait_ge(mv_ok, b + 1)
                dve.tensor_scalar(var[:, :], mv[:, :, 1], EPS, None, ALU.add).then_inc(var_ok, 1)
                dve.wait_ge(std_ok, b + 1)
                dve.reciprocal(rstd[:, :], std[:, :]).then_inc(rstd_ok, 1)
                dve.wait_ge(rstd_ok, b + 1)
                for st in range(ST):
                    if st == 0 and not first:
                        dve.wait_ge(turned, b * ST)
                        dve.wait_ge(x2_ok, b * ST)
                        dve.wait_ge(rows_out, b * 16)
                    dve.tensor_scalar(xn[:, st, :], rt[:, st, :], mv[:, st, 0:1], rstd[:, st:st + 1], ALU.subtract,
                                      ALU.mult).then_inc(xn_ok, 1)

            prime(dve, log_ok)
            dve.wait_ge(c_in, 48)
            for st in range(ST):
                add(0, st)
                statistics(0, st)
            dve.wait_ge(stats_ok, ST)
            normalize(0, first=True)
            with dve.Fori(1, B) as b:
                for st in range(ST):
                    add(b, st)
                    statistics(b, st)
                    if st == ST - 1:
                        dve.wait_ge(stats_ok, b * ST + ST)
                    biased(b - 1, st)
                normalize(b)
            for st in range(ST):
                biased(B - 1, st)


def routing(nc, banks, keep):
    logits, w1, w2, source, target, plan = (keep[n] for n in ("logits", "w1", "w2", "source", "target", "plan"))
    BF16 = mybir.dt.bfloat16
    PT = PLANNED * CT
    CH = TOPK * TT
    ROUND = 1.5 * 2.0 ** 23
    PARTS = 4
    with ExitStack() as ctx:
        def sb(name, shape, dt=F32):
            return ctx.enter_context(nc.sbuf_tensor(name, shape, dt))

        def sem(name):
            return ctx.enter_context(nc.semaphore(name))

        first = sb("r_first", [P, E])
        best = [sb(f"r_best{j}", [P, TT]) for j in range(2)]
        eq = sb("r_eq", [P, TT, E])
        pref = sb("r_pref", [P, TT, E])
        ptop = sb("r_ptop", [P, TT])
        hot = [sb(f"r_hot{j}", [P, TT, E]) for j in range(2)]
        rest = sb("r_rest", [P, TT, E])
        gap = sb("r_gap", [P, TT])
        e2 = sb("r_e2", [P, TT])
        den = sb("r_den", [P, TT])
        chosen = sb("r_chosen", [P, TT, E])
        before = sb("r_before", [P, P])
        ones = sb("r_ones", [P, P])
        cnt = sb("r_cnt", [P, TT, E])
        run = [sb(f"r_run{j}", [P, TT, E]) for j in range(2)]
        nch = sb("r_nch", [P, E])
        ends = [sb(f"r_ends{j}", [P, E]) for j in range(2)]
        base = sb("r_base", [P, E])
        slot = sb("r_slot", [P, TT, E])
        pick = sb("r_pick", [P, TT, E])
        place, high, low = (sb("r_" + n, [P, TOPK, TT]) for n in ("place", "high", "low"))
        low_hot = sb("r_low_hot", [P, CH, P], BF16)
        high_hot = sb("r_high_hot", [P, CH, 3, PT], BF16)
        counting_i, counting = sb("r_counting_i", [P, P], I32), sb("r_counting", [P, P])
        own_i, own = sb("r_own_i", [P, 1], I32), sb("r_own", [P, 1])
        label_i, label = sb("r_label_i", [P, TOPK, TT], I32), sb("r_label", [P, TOPK, TT])
        spare_i, spare = sb("r_spare_i", [P, PLANNED, CT], I32), sb("r_spare", [P, PLANNED, CT])
        found = sb("r_found", [P, 3, PT])
        tile_of, source_f, target_f, pad = (sb("r_" + n, [P, PT]) for n in ("tile_of", "source_f", "target_f", "pad"))
        cidx = sb("r_cidx", [1, PLANNED, E])
        past = sb("r_past", [1, PLANNED, E])
        cexp = sb("r_cexp", [1, PLANNED])
        cnew = sb("r_cnew", [1, PLANNED])
        cused = sb("r_cused", [1, PLANNED])
        hot_ok, high_ok, split_ok, sorted_ok, iota_ok = (
            sem("r_" + n) for n in ("hot_ok", "high_ok", "split_ok", "sorted_ok", "iota_ok"))
        consts_ok, chain, m_ok, counted, gap_ok, e2_ok = (
            sem("r_" + n) for n in ("consts_ok", "chain", "m_ok", "counted", "gap_ok", "e2_ok"))
        block = ctx.enter_context(nc.Block())

        def over_experts(a):
            return a[:, :].unsqueeze(2).to_broadcast([P, TT, E])

        def over_tiles(a):
            return a[:, :].unsqueeze(1).to_broadcast([P, TT, E])

        @block.gpsimd
        def _(gp):
            gp.memset(ones[:, :], 1.0).then_inc(consts_ok, 1)
            gp.wait_ge(consts_ok, 1)
            gp.affine_select(out=before[:, :], in_=ones[:, :], compare_op=ALU.is_ge, fill=0.0, base=-1,
                             pattern=[[1, P]], channel_multiplier=-1).then_inc(consts_ok, 1)
            for e in range(E):
                gp.memset(first[:, e:e + 1], float(E - e)).then_inc(consts_ok, 1)
            for c in range(PLANNED):
                gp.memset(cidx[:, c, :], float(c)).then_inc(consts_ok, 1)
            gp.iota(counting_i[:, :], pattern=[[1, P]], base=0, channel_multiplier=0).then_inc(iota_ok, 1)
            gp.iota(own_i[:, :], pattern=[[0, 1]], base=0, channel_multiplier=1).then_inc(iota_ok, 1)
            gp.iota(label_i[:, :, :], pattern=[[1, TOPK], [TOPK, TT]], base=0, channel_multiplier=0).then_inc(iota_ok, 1)
            gp.iota(spare_i[:, :, :], pattern=[[0, PLANNED], [P, CT]], base=TOPK * T, channel_multiplier=1)\
              .then_inc(iota_ok, 1)

        @block.tensor
        def _(pe):
            pe.wait_ge(m_ok, 1)
            flat = chosen[:, :, :].rearrange("p a b -> p (a b)")
            pe.matmul(banks[0][:, 0:TT * E], before[:, :], flat, start=True, stop=True)
            pe.matmul(banks[1][:, 0:TT * E], ones[:, :], flat, start=True, stop=True).then_inc(counted, 1)
            for part in range(PARTS):
                pe.wait_ge(split_ok, part + 1)
                pe.wait_ge(high_ok, part + 1)
                for n in range(part * CH // PARTS, (part + 1) * CH // PARTS):
                    mm = pe.matmul(banks[2][:, 0:3 * PT], low_hot[:, n, :],
                                   high_hot[:, n, :, :].rearrange("p a b -> p (a b)"), start=n == 0, stop=n == CH - 1)
            mm.then_inc(sorted_ok, 1)

        @block.scalar
        def _(act):
            act.wait_ge(gap_ok, 1)
            act.activation(e2[:, :], gap[:, :], ACT.Exp).then_inc(e2_ok, 1)
            for part in range(PARTS):
                these = slice(part * CH // PARTS, (part + 1) * CH // PARTS)
                act.wait_ge(hot_ok, part + 1)
                act.activation(high_hot[:, these, 0, :], high_hot[:, these, 2, :], ACT.Identity, scale=own[:, :])\
                   .then_inc(high_ok, 1)

        @block.vector
        def _(dve):
            steps = [0]

            def link(ins):
                steps[0] += 1
                ins.then_inc(chain, 1)
                dve.wait_ge(chain, steps[0])

            dve.wait_ge(consts_ok, 2 + E + PLANNED)
            dve.wait_ge(iota_ok, 4)
            for to, whole in ((counting, counting_i), (own, own_i)):
                dve.tensor_copy(to[:, :], whole[:, :])
            for to, whole in ((label, label_i), (spare, spare_i)):
                ins = dve.tensor_copy(to[:, :, :], whole[:, :, :])
            link(ins)
            left = logits
            for j in range(2):
                link(dve.tensor_reduce(best[j][:, :], left[:, :, :], AX.X, ALU.max))
                link(dve.tensor_tensor(eq[:, :, :], left[:, :, :], over_experts(best[j]), ALU.is_equal))
                link(dve.tensor_tensor(pref[:, :, :], eq[:, :, :], over_tiles(first), ALU.mult))
                link(dve.tensor_reduce(ptop[:, :], pref[:, :, :], AX.X, ALU.max))
                link(dve.tensor_tensor(hot[j][:, :, :], pref[:, :, :], over_experts(ptop), ALU.is_equal))
                if j == 0:
                    link(dve.scalar_tensor_tensor(rest[:, :, :], hot[0][:, :, :], NEVER, logits[:, :, :],
                                                  ALU.mult, ALU.add))
                    left = rest
            dve.tensor_tensor(gap[:, :], best[1][:, :], best[0][:, :], ALU.subtract).then_inc(gap_ok, 1)
            dve.tensor_tensor(chosen[:, :, :], hot[0][:, :, :], hot[1][:, :, :], ALU.add).then_inc(m_ok, 1)
            dve.wait_ge(e2_ok, 1)
            link(dve.tensor_scalar(den[:, :], e2[:, :], 1.0, None, ALU.add))
            link(dve.reciprocal(w1[:, :], den[:, :]))
            link(dve.tensor_tensor(w2[:, :], e2[:, :], w1[:, :], ALU.mult))
            dve.wait_ge(counted, 1)
            link(dve.tensor_copy(cnt[:, :, :].rearrange("p a b -> p (a b)"), banks[1][:, 0:TT * E]))
            src, n, step = cnt, 0, 1
            while step < TT:
                dst = run[n % 2]
                link(dve.tensor_tensor(dst[:, step:TT, :], src[:, step:TT, :], src[:, 0:TT - step, :], ALU.add))
                link(dve.tensor_copy(dst[:, 0:step, :], src[:, 0:step, :]))
                src, n, step = dst, n + 1, 2 * step
            total = src[:, TT - 1, :]
            link(dve.tensor_scalar(nch[:, :], total, 1.0 / CHUNK, 0.5 - 0.5 / CHUNK, ALU.mult, ALU.add))
            link(dve.tensor_scalar(nch[:, :], nch[:, :], 1.5 * 2.0 ** 23, None, ALU.add))
            link(dve.tensor_scalar(nch[:, :], nch[:, :], -1.5 * 2.0 ** 23, None, ALU.add))
            esrc, n, step = nch, 0, 1
            while step < E:
                dst = ends[n % 2]
                link(dve.tensor_tensor(dst[:, step:E], esrc[:, step:E], esrc[:, 0:E - step], ALU.add))
                link(dve.tensor_copy(dst[:, 0:step], esrc[:, 0:step]))
                esrc, n, step = dst, n + 1, 2 * step
            link(dve.tensor_tensor(base[:, :], esrc[:, :], nch[:, :], ALU.subtract))
            link(dve.tensor_scalar(base[:, :], base[:, :], float(CHUNK), None, ALU.mult))
            link(dve.tensor_tensor(slot[:, :, :], src[:, :, :], cnt[:, :, :], ALU.subtract))
            link(dve.tensor_tensor(slot[:, :, :], slot[:, :, :], over_tiles(base), ALU.add))
            link(dve.tensor_tensor(slot[:, :, :], slot[:, :, :],
                                   banks[0][:, 0:TT * E].rearrange("p (a b) -> p a b", b=E), ALU.add))
            for j in range(2):
                link(dve.tensor_tensor(pick[:, :, :], slot[:, :, :], hot[j][:, :, :], ALU.mult))
                link(dve.tensor_reduce(place[:, j, :], pick[:, :, :], AX.X, ALU.add))
            link(dve.tensor_scalar(high[:, :, :], place[:, :, :], 1.0 / P, 0.5 / P - 0.5, ALU.mult, ALU.add))
            link(dve.tensor_scalar(high[:, :, :], high[:, :, :], ROUND, None, ALU.add))
            link(dve.tensor_scalar(high[:, :, :], high[:, :, :], -ROUND, None, ALU.add))
            link(dve.scalar_tensor_tensor(low[:, :, :], high[:, :, :], -float(P), place[:, :, :], ALU.mult, ALU.add))
            flat_high, flat_low, flat_label = (a[:, :, :].rearrange("p a b -> p (a b)") for a in (high, low, label))
            for part in range(PARTS):
                these = slice(part * CH // PARTS, (part + 1) * CH // PARTS)
                n = CH // PARTS
                ones_at = high_hot[:, these, 2, :]
                dve.tensor_tensor(ones_at, counting[:, 0:PT].unsqueeze(1).to_broadcast([P, n, PT]),
                                  flat_high[:, these].unsqueeze(2).to_broadcast([P, n, PT]), ALU.is_equal)\
                   .then_inc(hot_ok, 1)
                dve.tensor_tensor(low_hot[:, these, :], counting[:, :].unsqueeze(1).to_broadcast([P, n, P]),
                                  flat_low[:, these].unsqueeze(2).to_broadcast([P, n, P]), ALU.is_equal)
                dve.wait_ge(hot_ok, part + 1)
                dve.tensor_tensor(high_hot[:, these, 1, :], ones_at,
                                  flat_label[:, these].unsqueeze(2).to_broadcast([P, n, PT]), ALU.mult)\
                   .then_inc(split_ok, 1)
            link(dve.tensor_tensor(past[:, :, :], cidx[:, :, :],
                                   esrc[0:1, :].unsqueeze(1).to_broadcast([1, PLANNED, E]), ALU.is_ge))
            link(dve.tensor_reduce(cexp[:, :], past[:, :, :], AX.X, ALU.add))
            link(dve.tensor_scalar(cused[:, :], cexp[:, :], float(E), None, ALU.is_lt))
            link(dve.tensor_scalar(cexp[:, :], cexp[:, :], float(E - 1), None, ALU.min))
            link(dve.memset(cnew[:, :], 1.0))
            link(dve.tensor_tensor(cnew[:, 1:PLANNED], cexp[:, 1:PLANNED], cexp[:, 0:PLANNED - 1], ALU.not_equal))
            link(dve.tensor_copy(plan[:, EXPERT, :], cexp[:, :]))
            link(dve.tensor_copy(plan[:, NEW, :], cnew[:, :]))
            link(dve.tensor_copy(plan[:, USED, :], cused[:, :]))
            dve.wait_ge(sorted_ok, 1)
            link(dve.tensor_copy(found[:, :, :].rearrange("p a b -> p (a b)"), banks[2][:, 0:3 * PT]))
            link(dve.tensor_scalar(tile_of[:, :], found[:, 1, :], 0.5, -0.25, ALU.mult, ALU.add))
            link(dve.tensor_scalar(tile_of[:, :], tile_of[:, :], ROUND, None, ALU.add))
            link(dve.tensor_scalar(tile_of[:, :], tile_of[:, :], -ROUND, None, ALU.add))
            link(dve.scalar_tensor_tensor(source_f[:, :], tile_of[:, :], float(P), found[:, 0, :], ALU.mult, ALU.add))
            link(dve.tensor_copy(source[:, :], source_f[:, :]))
            link(dve.tensor_scalar(pad[:, :], found[:, 2, :], -1.0, 1.0, ALU.mult, ALU.add))
            link(dve.tensor_tensor(pad[:, :], pad[:, :], spare[:, :, :].rearrange("p a b -> p (a b)"), ALU.mult))
            link(dve.scalar_tensor_tensor(target_f[:, :], found[:, 1, :], float(P), found[:, 0, :], ALU.mult, ALU.add))
            link(dve.tensor_tensor(target_f[:, :], target_f[:, :], pad[:, :], ALU.add))
            link(dve.tensor_copy(target[:, :], target_f[:, :]))


def experts(nc, banks, keep, w_up, w_down, b_up, b2, beta, x2_rows, expert_rows):
    x2, source, target, plan = (keep[n] for n in ("x2", "source", "target", "plan"))
    R32 = mybir.dt.float32r
    GROUPS = HB * CHUNK // BANK
    PER = HB // GROUPS
    with ExitStack() as ctx:
        def sb(name, shape, dt=F32):
            return ctx.enter_context(nc.sbuf_tensor(name, shape, dt))

        def sem(name):
            return ctx.enter_context(nc.semaphore(name))

        w1 = sb("e_w1", [P, KD * HID])
        w1h = sb("e_w1h", [P, KD * HID], R32)
        w1l = sb("e_w1l", [P, KD * HID], R32)
        w2 = sb("e_w2", [P, HB * D])
        w2h = sb("e_w2h", [P, HB * D], R32)
        w2l = sb("e_w2l", [P, HB * D], R32)
        b1all = sb("e_b1all", [P, E, HB])
        b2all = sb("e_b2all", [P, E, D])
        b1c = [sb(f"e_b1c{u}", [P, HB]) for u in range(2)]
        xg = [sb(f"e_xg{u}", [P, CT, D]) for u in range(2)]
        xh = [sb(f"e_xh{u}", [P, KD, CHUNK], R32) for u in range(2)]
        xl = [sb(f"e_xl{u}", [P, KD, CHUNK], R32) for u in range(2)]
        g = sb("e_g", [P, HB, CHUNK])
        hh = [sb(f"e_hh{u}", [P, HB, CHUNK], R32) for u in range(2)]
        hl = [sb(f"e_hl{u}", [P, HB, CHUNK], R32) for u in range(2)]
        y = [sb(f"e_y{u}", [P, CT, D]) for u in range(2)]
        ident = sb("e_ident", [P, P])
        warm = sb("e_warm", [1, 1])
        source_c = [sb(f"e_source{u}", [P, CT], U32) for u in range(2)]
        target_c = sb("e_target", [P, CT], U32)
        source_ok, target_ok = sem("e_source_ok"), sem("e_target_ok")
        beta_rows = sb("e_beta", [P, D])
        beta_in, numbers_ok = sem("e_beta_in"), sem("e_numbers_ok")
        ident_ok, bias_in = sem("e_ident_ok"), sem("e_bias_in")
        w1_in, w1h_ok, w1l_ok, w2_in, w2h_ok, w2l_ok = (
            sem("e_" + n) for n in ("w1_in", "w1h_ok", "w1l_ok", "w2_in", "w2h_ok", "w2l_ok"))
        xg_in = [sem(f"e_xg_in{u}") for u in range(2)]
        turned, xh_ok, xl_ok, b1_ok, h_done, g_ok, hh_ok, hl_ok, y_done, y_ok = (
            sem("e_" + n) for n in ("turned", "xh_ok", "xl_ok", "b1_ok", "h_done", "g_ok", "hh_ok", "hl_ok",
                                     "y_done", "y_ok"))
        y_out, y_stored = sem("e_y_out"), sem("e_y_stored")
        block = ctx.enter_context(nc.Block())
        h_ps, t_ps, y_ps = banks[0:GROUPS], banks[GROUPS:GROUPS + 2], banks[GROUPS + 2:GROUPS + 4]

        def look(engine, what, c):
            return engine.value_load(plan[0:1, what, bass.ds(c, 1)], min_val=0, max_val=E - 1)

        @block.gpsimd
        def _(gp):
            prime(gp, y_stored)
            make_identity(gp, ident, ident_ok)

            def numbers(to, table, c, done, count):
                gp.tensor_copy(to[:, :], table[:, bass.ds(c * CT, CT)]).then_inc(done, 1)
                gp.wait_ge(done, count)
                gp.nop().then_inc(numbers_ok, 1)

            def gather(u):
                for a in range(CT):
                    gp.indirect_dma_start(out=xg[u][:, a, :], out_offset=None, in_=x2_rows,
                                          in_offset=bass.IndirectOffsetOnAxis(ap=source_c[u][:, a:a + 1], axis=0))\
                      .then_inc(xg_in[u], 16)

            for u in range(2):
                gp.tensor_copy(source_c[u][:, :], source[:, u * CT:(u + 1) * CT]).then_inc(source_ok, 1)
                gp.wait_ge(source_ok, u + 1)
                gather(u)
            gp.wait_ge(beta_in, 16)
            for t in range(0, TT, ST):
                gp.tensor_tensor(x2[:, t:t + ST, :], x2[:, t:t + ST, :],
                                 beta_rows[:, :].unsqueeze(1).to_broadcast([P, ST, D]), ALU.add)
            with gp.Fori(0, NCHUNK // 2) as c2:
                for u in range(2):
                    c = c2 * 2 + u
                    with gp.If(look(gp, USED, c) > 0):
                        gp.wait_ge(turned, c + 1)
                        numbers(source_c[u], source, c + AHEAD, source_ok, c + AHEAD + 1)
                        gather(u)
                        gp.wait_ge(y_ok, c * CT + CT + 1)
                        numbers(target_c, target, c, target_ok, c + 1)
                        for a in range(CT):
                            gp.indirect_dma_start(
                                out=expert_rows, in_=y[u][:, a, :], in_offset=None,
                                out_offset=bass.IndirectOffsetOnAxis(ap=target_c[:, a:a + 1], axis=0)).then_inc(y_out, 16)
                        gp.wait_ge(y_out, c * (16 * CT) + 16 * CT)
                        gp.wait_ge(xg_in[u], c2 * (16 * CT) + 2 * 16 * CT)
                        gp.nop().then_inc(y_stored, 1)

        @block.sync
        def _(sp):
            def load(to, source, expert, done):
                sp.dma_start(to[:, :], source[bass.ds(expert, 1)].rearrange("a p n -> p (a n)")).then_inc(done, 16)

            def load_new(to, source, c, done):
                expert = look(sp, EXPERT, c)
                with sp.If(look(sp, NEW, c) > 0):
                    load(to, source, expert, done)
                with sp.Else():
                    sp.nop().then_inc(done, 16)

            first = sp.value_load(plan[0:1, EXPERT, 0:1], min_val=0, max_val=E - 1)
            sp.dma_start(beta_rows[:, :], beta.partition_broadcast(P)).then_inc(beta_in, 16)
            load(w1, w_up, first, w1_in)
            load(w2, w_down, first, w2_in)
            sp.dma_start(b1all[:, :, :], b_up).then_inc(bias_in, 16)
            sp.dma_start(b2all[:, :, :].rearrange("p e d -> p (e d)"),
                         b2.rearrange("e d -> (e d)").partition_broadcast(P)).then_inc(bias_in, 16)
            sp.wait_ge(w1h_ok, 1)
            sp.wait_ge(w1l_ok, 1)
            load_new(w1, w_up, 1, w1_in)
            with sp.Fori(0, NCHUNK // 2) as c2:
                for u in range(2):
                    c = c2 * 2 + u
                    with sp.If(look(sp, USED, c) > 0):
                        sp.wait_ge(w2h_ok, c + 1)
                        sp.wait_ge(w2l_ok, c + 1)
                        load_new(w2, w_down, c + 1, w2_in)
                        sp.wait_ge(w1h_ok, c + 2)
                        sp.wait_ge(w1l_ok, c + 2)
                        load_new(w1, w_up, c + 2, w1_in)
                    with sp.Else():
                        for done in (w2_in, w1_in):
                            sp.nop().then_inc(done, 16)
            sp.wait_ge(w1_in, 16 * (NCHUNK + 2))
            sp.wait_ge(w2_in, 16 * (NCHUNK + 1))

        @block.tensor
        def _(pe):
            def turn_rows(u):
                for kk in range(KD):
                    for a in range(CT):
                        mm = pe.transpose(t_ps[u][:, kk * CHUNK + a * P:kk * CHUNK + (a + 1) * P],
                                          xg[u][:, a, kk * P:(kk + 1) * P], ident[:, :])
                mm.then_inc(turned, 1)

            def up(c, u):
                pe.wait_ge(xl_ok, c + 1)
                pe.wait_ge(w1l_ok, c + 1)
                for hb in range(HB):
                    out = h_ps[hb // PER][:, (hb % PER) * CHUNK:(hb % PER + 1) * CHUNK]
                    parts = [(wt[:, kk * HID + hb * P:kk * HID + (hb + 1) * P], xt[u][:, kk, :])
                             for kk in range(KD) for wt, xt in ((w1h, xh), (w1h, xl), (w1l, xh))]
                    for m, (lhs, rhs) in enumerate(parts):
                        mm = pe.matmul(out, lhs, rhs, start=m == 0, stop=m == len(parts) - 1)
                    mm.then_inc(h_done, 1)

            def down(c, u):
                pe.wait_ge(w2l_ok, c + 1)
                pe.wait_ge(y_ok, c * CT + 1)
                for a in range(CT):
                    for hb in range(HB):
                        if a == 0 and hb % PER == 0:
                            pe.wait_ge(hl_ok, c * GROUPS + hb // PER + 2)
                        wb = slice(hb * D, (hb + 1) * D)
                        for m, (lhs, rhs) in enumerate(((hh, w2h), (hl, w2h), (hh, w2l))):
                            mm = pe.matmul(y_ps[u][:, a * D:(a + 1) * D], lhs[u][:, hb, a * P:(a + 1) * P], rhs[:, wb],
                                           start=hb == 0 and m == 0, stop=hb == HB - 1 and m == 2)
                    mm.then_inc(y_done, 1)

            pe.wait_ge(ident_ok, 2)
            pe.wait_ge(xg_in[0], 16 * CT)
            turn_rows(0)
            with pe.Fori(0, NCHUNK // 2) as c2:
                for u in range(2):
                    c = c2 * 2 + u
                    with pe.If(look(pe, USED, c) > 0):
                        up(c, u)
                        pe.wait_ge(xg_in[1 - u], (c2 + u) * (16 * CT) + 16 * CT)
                        turn_rows(1 - u)
                        down(c, u)

        @block.scalar
        def _(act):
            def rows_high(c, u):
                act.wait_ge(turned, c + 1)
                act.copy(xh[u][:, :, :].rearrange("p a b -> p (a b)"), t_ps[u][:, 0:KD * CHUNK]).then_inc(xh_ok, 1)

            prime(act, y_done)
            act.wait_ge(ident_ok, 2)
            act.wait_ge(w1_in, 16)
            act.copy(w1h[:, :], w1[:, :]).then_inc(w1h_ok, 1)
            rows_high(0, 0)
            with act.Fori(0, NCHUNK // 2) as c2:
                for u in range(2):
                    c = c2 * 2 + u
                    with act.If(look(act, USED, c) > 0):
                        act.wait_ge(hl_ok, c * GROUPS + 1)
                        with act.If(look(act, NEW, c) > 0):
                            act.wait_ge(w2_in, c * 16 + 16)
                            act.wait_ge(y_done, c * CT + 1)
                            act.copy(w2h[:, :], w2[:, :]).then_inc(w2h_ok, 1)
                        with act.Else():
                            act.nop().then_inc(w2h_ok, 1)
                        act.activation(warm[:, :], ident[0:1, 0:1], ACT.Gelu)
                        act.wait_ge(b1_ok, c + 1)
                        for hb in range(HB):
                            if hb % PER == 0:
                                act.wait_ge(h_done, c * HB + hb + PER)
                            act.activation(g[:, hb, :], h_ps[hb // PER][:, (hb % PER) * CHUNK:(hb % PER + 1) * CHUNK],
                                           ACT.Gelu, bias=b1c[u][:, hb:hb + 1]).then_inc(g_ok, 1)
                        rows_high(c + 1, 1 - u)
                        with act.If(look(act, NEW, c + 1) > 0):
                            act.wait_ge(w1_in, c * 16 + 32)
                            act.wait_ge(h_done, c * HB + HB)
                            act.copy(w1h[:, :], w1[:, :]).then_inc(w1h_ok, 1)
                        with act.Else():
                            act.nop().then_inc(w1h_ok, 1)

        @block.vector
        def _(dve):
            def low(to, full, high, done):
                dve.tensor_tensor(to, full, high.bitcast(F32), ALU.subtract).then_inc(done, 1)

            def rows_low(c, u):
                dve.wait_ge(xh_ok, c + 1)
                low(xl[u][:, :, :].rearrange("p a b -> p (a b)"), t_ps[u][:, 0:KD * CHUNK],
                    xh[u][:, :, :].rearrange("p a b -> p (a b)"), xl_ok)

            def bias(c, u):
                expert = look(dve, EXPERT, c)
                dve.tensor_scalar(b1c[u][:, :], b1all[:, bass.ds(expert, 1), :].rearrange("p a b -> p (a b)"),
                                  1.0, None, ALU.mult).then_inc(b1_ok, 1)

            prime(dve, y_ok, hl_ok)
            dve.wait_ge(w1h_ok, 1)
            low(w1l[:, :], w1[:, :], w1h[:, :], w1l_ok)
            dve.wait_ge(bias_in, 32)
            rows_low(0, 0)
            bias(0, 0)
            with dve.Fori(0, NCHUNK // 2) as c2:
                for u in range(2):
                    c = c2 * 2 + u
                    with dve.If(look(dve, USED, c) > 0):
                        with dve.If(look(dve, NEW, c) > 0):
                            dve.wait_ge(w2h_ok, c + 1)
                            low(w2l[:, :], w2[:, :], w2h[:, :], w2l_ok)
                        with dve.Else():
                            dve.nop().then_inc(w2l_ok, 1)
                        for group in range(GROUPS):
                            these = slice(group * PER, (group + 1) * PER)
                            dve.wait_ge(g_ok, c * HB + (group + 1) * PER)
                            dve.tensor_copy(hh[u][:, these, :], g[:, these, :]).then_inc(hh_ok, 1)
                            dve.wait_ge(hh_ok, c * GROUPS + group + 1)
                            low(hl[u][:, these, :], g[:, these, :], hh[u][:, these, :], hl_ok)
                        rows_low(c + 1, 1 - u)
                        bias(c + 1, 1 - u)
                        with dve.If(look(dve, NEW, c + 1) > 0):
                            dve.wait_ge(w1h_ok, c + 2)
                            low(w1l[:, :], w1[:, :], w1h[:, :], w1l_ok)
                        with dve.Else():
                            dve.nop().then_inc(w1l_ok, 1)
                        dve.wait_ge(y_stored, c + 1)
                        expert = look(dve, EXPERT, c)
                        dve.wait_ge(y_done, c * CT + CT + 1)
                        for a in range(CT):
                            dve.tensor_tensor(y[u][:, a, :], y_ps[u][:, a * D:(a + 1) * D],
                                              b2all[:, bass.ds(expert, 1), :].rearrange("p a b -> p (a b)"), ALU.add)\
                               .then_inc(y_ok, 1)


def outputs(nc, banks, keep, gamma, expert_rows, out):
    x2b, shared, w1, w2 = (keep[n] for n in ("x2", "shared", "w1", "w2"))
    GROUP = 4
    GROUPS = TT // GROUP
    with ExitStack() as ctx:
        def sb(name, shape, dt=F32):
            return ctx.enter_context(nc.sbuf_tensor(name, shape, dt))

        def sem(name):
            return ctx.enter_context(nc.semaphore(name))

        g = sb("o_g", [P, D])
        y1 = sb("o_y1", [P, TT, D])
        y2 = sb("o_y2", [P, 2 * GROUP, D])
        stats = [sb(f"o_stats{n}", [P, GROUP, 6]) for n in range(2)]
        mv = [sb(f"o_mv{n}", [P, GROUP, 2]) for n in range(2)]
        var = [sb(f"o_var{n}", [P, GROUP]) for n in range(2)]
        std = [sb(f"o_std{n}", [P, GROUP]) for n in range(2)]
        rstd = [sb(f"o_rstd{n}", [P, GROUP]) for n in range(2)]
        c_in = sem("o_c_in")
        rows_in = [sem(f"o_rows_in{i}") for i in range(2)]
        scaled, used, chain, done, out_sem = (sem("o_" + n) for n in ("scaled", "used", "chain", "done", "out"))
        var_ok = [sem(f"o_var_ok{n}") for n in range(2)]
        std_ok = [sem(f"o_std_ok{n}") for n in range(2)]
        block = ctx.enter_context(nc.Block())

        def tiles(k):
            return range(k * GROUP, (k + 1) * GROUP)

        @block.sync
        def _(sp):
            chosen = expert_rows[0:TOPK * T, :].rearrange("(t j p) d -> p t j d", j=TOPK, p=P)
            for k in range(GROUPS):
                if k == 1:
                    sp.dma_start(g[:, :], gamma.partition_broadcast(P)).then_inc(c_in, 16)
                these = slice(k * GROUP, (k + 1) * GROUP)
                if k >= 2:
                    sp.wait_ge(used, k - 1)
                sp.dma_start(y1[:, these, :], chosen[:, these, 0, :]).then_inc(rows_in[k % 2], 16)
                sp.dma_start(y2[:, k % 2 * GROUP:(k % 2 + 1) * GROUP, :], chosen[:, these, 1, :])\
                  .then_inc(rows_in[k % 2], 16)
            rows = out.rearrange("b s d -> (b s) d").rearrange("(t p) d -> p t d", p=P)
            for k in range(GROUPS):
                sp.wait_ge(done, k + 1)
                sp.dma_start(rows[:, k * GROUP:(k + 1) * GROUP, :], y1[:, k * GROUP:(k + 1) * GROUP, :])\
                  .then_inc(out_sem, 16)
            sp.wait_ge(out_sem, 16 * GROUPS)

        @block.scalar
        def _(act):
            def deviation(n, k):
                act.wait_ge(var_ok[n], k + 1)
                act.activation(std[n][:, :], var[n][:, :], ACT.Sqrt).then_inc(std_ok[n], 1)

            for k in range(GROUPS + 2):
                if k < GROUPS:
                    act.wait_ge(rows_in[k % 2], 32 * (k // 2 + 1))
                    for t in tiles(k):
                        act.activation(y1[:, t, :], y1[:, t, :], ACT.Identity, scale=w1[:, t:t + 1]).then_inc(scaled, 1)
                if 1 <= k <= GROUPS:
                    deviation(0, k - 1)
                if k >= 2:
                    deviation(1, k - 2)

        @block.vector
        def _(dve):
            steps = [0]

            def stage(instructions):
                for ins in instructions:
                    last = ins
                steps[0] += 1
                last.then_inc(chain, 1)
                dve.wait_ge(chain, steps[0])

            def statistics(n, k):
                stage(dve.bn_stats(stats[n][:, i, :], y1[:, t, :]) for i, t in enumerate(tiles(k)))
                stage(dve.bn_aggr(mv[n][:, i, :], stats[n][:, i, :]) for i in range(GROUP))
                dve.tensor_scalar(var[n][:, :], mv[n][:, :, 1], EPS, None, ALU.add).then_inc(var_ok[n], 1)

            def normalize(n, k):
                dve.wait_ge(std_ok[n], k + 1)
                stage([dve.reciprocal(rstd[n][:, :], std[n][:, :])])
                for i, t in enumerate(tiles(k)):
                    ins = dve.tensor_scalar(y1[:, t, :], y1[:, t, :], mv[n][:, i, 0:1], rstd[n][:, i:i + 1],
                                            ALU.subtract, ALU.mult)
                return ins

            for k in range(GROUPS + 2):
                if k == 1:
                    dve.wait_ge(c_in, 16)
                if k >= 2:
                    normalize(1, k - 2).then_inc(done, 1)
                if 1 <= k <= GROUPS:
                    rows = y1[:, (k - 1) * GROUP:k * GROUP, :]
                    stage([normalize(0, k - 1)])
                    stage([dve.tensor_tensor(rows, rows, g[:, :].unsqueeze(1).to_broadcast([P, GROUP, D]), ALU.mult)])
                    stage([dve.tensor_tensor(rows, rows, x2b[:, (k - 1) * GROUP:k * GROUP, :], ALU.add)])
                    statistics(1, k - 1)
                if k < GROUPS:
                    dve.wait_ge(rows_in[k % 2], 32 * (k // 2 + 1))
                    dve.wait_ge(scaled, (k + 1) * GROUP)
                    for t in tiles(k):
                        ins = dve.scalar_tensor_tensor(y1[:, t, :], y2[:, t % (2 * GROUP), :], w2[:, t:t + 1],
                                                       y1[:, t, :], ALU.mult, ALU.add)
                    ins.then_inc(used, 1)
                    dve.wait_ge(used, k + 1)
                    rows = slice(k * GROUP, (k + 1) * GROUP)
                    stage([dve.scalar_tensor_tensor(y1[:, rows, :], shared[:, rows, :], 0.5, y1[:, rows, :],
                                                    ALU.mult, ALU.add)])
                    statistics(0, k)


class Banks:

    def __init__(self, ps):
        self.ps = ps
        self.both = [ps[:, 2 * i * BANK:2 * (i + 1) * BANK] for i in range(4)]

    def __getitem__(self, i):
        if isinstance(i, slice):
            return [self[j] for j in range(*i.indices(8))]
        return self.ps[:, i * BANK:(i + 1) * BANK]


def layer(nc, x_t, x_rows, w_qkv, w_o, w_up, w_down, b_up, b2, w_gs, shared_b, gamma, beta, out):
    attn_out = nc.dram_tensor("attn_out", [B * PAIRS, P, S], F32, kind="Internal").ap()
    inv_row = nc.dram_tensor("inv_row", [S], F32, kind="Internal").ap()
    x2_rows = nc.dram_tensor("x2_rows", [T, D], F32, kind="Internal").ap()
    expert_rows = nc.dram_tensor("expert_rows", [TOPK * T + CHUNK, D], F32, kind="Internal").ap()
    with ExitStack() as ctx:
        banks = Banks(ctx.enter_context(nc.psum_tensor("banks", [P, 8 * BANK], F32)))
        keep = {"bounded": ctx.enter_context(nc.sbuf_tensor("bounded", [1, 1], I32))}
        score_bound(nc, banks, keep, x_rows, w_qkv)
        attention(nc, banks, keep, x_t, w_qkv, inv_row, attn_out)
        keep |= {name: ctx.enter_context(nc.sbuf_tensor(name, shape, dt)) for name, shape, dt in (
            ("x2", [P, TT, D], F32), ("shared", [P, TT, D], F32), ("logits", [P, TT, E], F32),
            ("w1", [P, TT], F32), ("w2", [P, TT], F32), ("source", [P, PLANNED * CT], U32), ("target", [P, PLANNED * CT], U32),
            ("plan", [1, 3, PLANNED], I32))}
        tokens(nc, banks, keep, x_rows, attn_out, w_o, w_gs, shared_b, x2_rows)
        routing(nc, banks, keep)
        experts(nc, banks, keep, w_up, w_down, b_up, b2, beta, x2_rows, expert_rows)
        outputs(nc, banks, keep, gamma, expert_rows, out)


def kernel(L0_attn_x, L0_attn_kernel, L0_attn_WO, L0_ffn_W1, L0_ffn_b1, L0_ffn_W2, L0_ffn_b2, L0_ffn_gate_W,
           L0_ffn_shared_W, L0_ffn_shared_b, L0_ffn_gamma, L0_ffn_beta):
    import numpy as np
    import concourse.bacc as bacc
    from concourse.bass_utils import run_bass_kernel_spmd

    x = np.asarray(L0_attn_x)
    wk = np.asarray(L0_attn_kernel).reshape(3, PAIRS, 2, KD, P, DH)
    qk = wk[0:2].transpose(1, 4, 3, 2, 0, 5).reshape(PAIRS, P, KD, 2, P)
    vv = wk[2].transpose(0, 3, 2, 1, 4).reshape(PAIRS, P, KD, 1, P)
    w1 = np.asarray(L0_ffn_W1).reshape(E, KD, P, HID).transpose(0, 2, 1, 3).reshape(E, P, KD * HID)
    w2 = np.asarray(L0_ffn_W2).reshape(E, HB, P, D).transpose(0, 2, 1, 3).reshape(E, P, HB * D)
    b1 = np.asarray(L0_ffn_b1).reshape(E, HB, P).transpose(2, 0, 1)
    gs = np.concatenate([np.asarray(L0_ffn_shared_W), np.asarray(L0_ffn_gate_W)], axis=1)
    arrays = {
        "x_t": x.reshape(T, KD, P).transpose(2, 1, 0),
        "x_rows": x.reshape(T, D),
        "w_qkv": np.concatenate([qk, vv], axis=3),
        "w_o": np.asarray(L0_attn_WO).reshape(DH, PAIRS, 2, D).transpose(2, 0, 1, 3).reshape(P, PAIRS, D),
        "w_up": w1,
        "w_down": w2,
        "b_up": b1,
        "b2": np.asarray(L0_ffn_b2),
        "w_gs": gs.reshape(KD, P, D + E).transpose(1, 0, 2),
        "shared_b": np.asarray(L0_ffn_shared_b),
        "gamma": np.asarray(L0_ffn_gamma),
        "beta": np.asarray(L0_ffn_beta),
    }
    arrays = {name: np.ascontiguousarray(a) for name, a in arrays.items()}
    nc = bacc.Bacc("TRN2", target_bir_lowering=False, num_devices=1)
    args = [nc.dram_tensor(name, a.shape, mybir.dt.from_np(a.dtype), kind="ExternalInput").ap()
            for name, a in arrays.items()]
    out = nc.dram_tensor("out", [B, S, D], F32, kind="ExternalOutput").ap()
    layer(nc, *args, out)
    return run_bass_kernel_spmd(nc, [arrays], core_ids=[0]).results[0]["out"]
```
